# Optimizing a Trainium2 kernel written in Bass

```python
import numpy as np
import jax
import jax.numpy as jnp

def _softmax(x, axis=-1):
    return jax.nn.softmax(x, axis=axis)

def _gelu(x):
    return jax.nn.gelu(x, approximate=True)

def _silu(x):
    return jax.nn.silu(x)

def _sigmoid(x):
    return jax.nn.sigmoid(x)

def _layernorm(x, axis=-1, eps=1e-05):
    m = jnp.mean(x, axis=axis, keepdims=True)
    v = jnp.var(x, axis=axis, keepdims=True)
    return (x - m) / jnp.sqrt(v + eps)

def _scatter_add(tgt, idx, src, axis=0):
    return tgt.at[idx].add(src)

def _segment_sum(src, seg, n):
    return jax.ops.segment_sum(src, seg, n)
kernel_name = 'mk_adaln_d1_jaxref_r8_eff9f4'

def setup_inputs(seed: int=0):
    np.random.seed(seed)
    _w = jnp.asarray

    def _L0_attn_setup():
        import jax, jax.numpy as jnp
        import numpy as np
        DIMS = 256
        HEAD_DIM = 64
        NUM_HEADS = DIMS // HEAD_DIM
        GQA_HEADS = 2
        EPS = 1e-08
        key = jax.random.key(seed)
        ks = jax.random.split(key, 6)
        b, s = (2, 256)
        kv_dims = HEAD_DIM * GQA_HEADS
        x = jax.random.normal(ks[0], (b, s, DIMS), dtype=jnp.float32)
        Wq = jax.random.normal(ks[1], (DIMS, DIMS), dtype=jnp.float32) * 0.02
        Wk = jax.random.normal(ks[2], (kv_dims, DIMS), dtype=jnp.float32) * 0.02
        Wv = jax.random.normal(ks[3], (kv_dims, DIMS), dtype=jnp.float32) * 0.02
        Wo = jax.random.normal(ks[4], (DIMS, DIMS), dtype=jnp.float32) * 0.02
        norm_scale = jnp.ones((DIMS,), dtype=jnp.float32)
        split_scale = jnp.full((DIMS,), 0.1, dtype=jnp.float32)
        return {'x': x, 'norm_scale': norm_scale, 'split_scale': split_scale, 'Wq': Wq, 'Wk': Wk, 'Wv': Wv, 'Wo': Wo}
    _L0_attn_in = _L0_attn_setup()

    def _L0_ffn_setup():
        import jax, jax.numpy as jnp
        import numpy as np
        SEQ, BS, H, I, E = (256, 4, 256, 512, 8)
        key = jax.random.key(seed)
        ks = jax.random.split(key, 5)
        s = 0.02
        return {'hidden_states': jax.random.normal(ks[0], (SEQ, BS, H), dtype=jnp.float32), 'router_w': jax.random.normal(ks[1], (H, E), dtype=jnp.float32) * s, 'gate_w': jax.random.normal(ks[2], (E, H, I), dtype=jnp.float32) * s, 'up_w': jax.random.normal(ks[3], (E, H, I), dtype=jnp.float32) * s, 'down_w': jax.random.normal(ks[4], (E, I, H), dtype=jnp.float32) * s}
    _L0_ffn_in = _L0_ffn_setup()
    _L0_c = _w((lambda *s: np.random.randn(*s).astype(np.float32) * 0.05)(4, 256))
    _L0_wmod = _w((lambda *s: np.random.randn(*s).astype(np.float32) * 0.05)(256, 6 * 256) * 256 ** (-0.5))
    _d = {'L0_attn_x': _L0_attn_in['x'], 'L0_attn_norm_scale': _L0_attn_in['norm_scale'], 'L0_attn_split_scale': _L0_attn_in['split_scale'], 'L0_attn_Wq': _L0_attn_in['Wq'], 'L0_attn_Wk': _L0_attn_in['Wk'], 'L0_attn_Wv': _L0_attn_in['Wv'], 'L0_attn_Wo': _L0_attn_in['Wo'], 'L0_ffn_router_w': _L0_ffn_in['router_w'], 'L0_ffn_gate_w': _L0_ffn_in['gate_w'], 'L0_ffn_up_w': _L0_ffn_in['up_w'], 'L0_ffn_down_w': _L0_ffn_in['down_w'], 'L0_c': _L0_c, 'L0_wmod': _L0_wmod}
    _x0 = _d['L0_attn_x']
    _d['L0_attn_x'] = jax.random.normal(jax.random.fold_in(jax.random.key(seed), 1), (4, 512, 256), dtype=_x0.dtype)
    del _x0
    return _d

def reference(L0_attn_x, L0_attn_norm_scale, L0_attn_split_scale, L0_attn_Wq, L0_attn_Wk, L0_attn_Wv, L0_attn_Wo, L0_ffn_router_w, L0_ffn_gate_w, L0_ffn_up_w, L0_ffn_down_w, L0_c, L0_wmod):

    def _L0_attn_ref(x, norm_scale, split_scale, Wq, Wk, Wv, Wo):
        import jax, jax.numpy as jnp
        import numpy as np
        DIMS = 256
        HEAD_DIM = 64
        NUM_HEADS = DIMS // HEAD_DIM
        GQA_HEADS = 2
        EPS = 1e-08
        b, s, d = x.shape
        H, G, dh = (NUM_HEADS, GQA_HEADS, HEAD_DIM)
        hpg = H // G
        nrm = jnp.linalg.norm(x, axis=-1, keepdims=True) * d ** (-0.5)
        h = norm_scale * x / (nrm + EPS) * split_scale
        q = (h @ Wq.T).reshape(b, s, H, dh)
        k = (h @ Wk.T).reshape(b, s, G, dh)
        v = (h @ Wv.T).reshape(b, s, G, dh)
        q = q.transpose(0, 2, 1, 3).reshape(b, G, hpg, s, dh)
        k = k.transpose(0, 2, 1, 3)
        v = v.transpose(0, 2, 1, 3)
        scores = jnp.einsum('bghsd,bgtd->bghst', q, k) / np.float32(np.sqrt(dh))
        attn = jax.nn.softmax(scores, axis=-1)
        out = jnp.einsum('bghst,bgtd->bghsd', attn, v)
        out = out.reshape(b, H, s, dh).transpose(0, 2, 1, 3).reshape(b, s, H * dh)
        return x + out @ Wo.T

    def _L0_ffn_ref(hidden_states, router_w, gate_w, up_w, down_w):
        import jax, jax.numpy as jnp
        import numpy as np
        SEQ, BS, H, I, E = (256, 4, 256, 512, 8)
        router_logits = jnp.einsum('sbh,he->sbe', hidden_states, router_w)
        routing_indices = jnp.argmax(router_logits, axis=-1)
        routing_weights = jax.nn.sigmoid(jnp.max(router_logits, axis=-1))
        out = jnp.zeros_like(hidden_states)
        for e in range(E):
            mask = (routing_indices == e)[..., None]
            g = jnp.einsum('sbh,hi->sbi', hidden_states, gate_w[e])
            u = jnp.einsum('sbh,hi->sbi', hidden_states, up_w[e])
            y = jnp.einsum('sbi,ih->sbh', jax.nn.silu(g) * u, down_w[e])
            out = out + jnp.where(mask, y, jnp.zeros((), out.dtype))
        return out
    x = L0_attn_x
    mod = (_silu(L0_c) @ L0_wmod).reshape(L0_c.shape[0], 6, 1, -1)
    sa, ca, ga, sb, cb, gb = (mod[:, 0], mod[:, 1], mod[:, 2], mod[:, 3], mod[:, 4], mod[:, 5])
    ga = (2 * (ga >= 0) - 1) * jnp.maximum(jnp.abs(ga), 0.25)
    gb = (2 * (gb >= 0) - 1) * jnp.maximum(jnp.abs(gb), 0.25)
    h = _layernorm(x, axis=-1) * (1 + ca) + sa
    x = x + ga * _L0_attn_ref(h, L0_attn_norm_scale, L0_attn_split_scale, L0_attn_Wq, L0_attn_Wk, L0_attn_Wv, L0_attn_Wo)
    h = _layernorm(x, axis=-1) * (1 + cb) + sb
    x = x + gb * _L0_ffn_ref(h, L0_ffn_router_w, L0_ffn_gate_w, L0_ffn_up_w, L0_ffn_down_w)
    return x

_drawn_inputs = setup_inputs


def setup_inputs(seed=0):
    import zlib

    import numpy as np

    out = dict(_drawn_inputs(seed))
    spreads = {'L0_attn_norm_scale': (1.0, 0.6), 'L0_attn_split_scale': (0.10000000149011612, 0.6)}
    factors = {'L0_attn_Wq': 8.0,
     'L0_attn_Wk': 8.0,
     'L0_attn_Wv': 8.0,
     'L0_attn_Wo': 8.0,
     'L0_ffn_router_w': 8.0,
     'L0_ffn_gate_w': 8.0,
     'L0_ffn_up_w': 8.0,
     'L0_ffn_down_w': 8.0}
    for name, (base, spread) in spreads.items():
        noise = np.random.default_rng([zlib.crc32(name.encode()), seed]).standard_normal(out[name].shape)
        drawn = base * np.exp(spread * noise) if base else spread * noise
        out[name] = jnp.asarray(drawn.astype(out[name].dtype))
    for name, factor in factors.items():
        out[name] = (out[name] * factor).astype(out[name].dtype)
    return out
```

```python
def build(nc, io):
    import concourse.bass as bass
    import concourse.mybir as mybir
    from contextlib import ExitStack

    f32, f32r, bf16, i32 = (mybir.dt.float32, mybir.dt.float32r, mybir.dt.bfloat16,
                            mybir.dt.int32)
    ALU = mybir.AluOpType
    ACT = mybir.ActivationFunctionType
    AX = mybir.AxisListType
    ds = bass.ds

    x_in, out = io["L0_attn_x"], io["out"]
    P = 128
    B, S, D = x_in.shape
    HEADS, GROUPS, DH = 4, 2, 64
    HPG = HEADS // GROUPS
    E, _, I = io["L0_ffn_gate_w"].shape
    KD = D // P
    KI = I // P
    TPB = S // P
    N = B * S
    NT = N // P
    TILES = NT + E - 1
    REGION = N + P
    LN_EPS, RMS_EPS = 1e-5, 1e-8
    SCALE = 1.0 / float(DH) ** 0.5
    STEPS = HEADS * TPB
    MK = DH + TPB

    def dram(name, shape, dt):
        return nc.dram_tensor(name, shape, dt, kind="Internal").ap()

    mod_d = dram("mod_d", (B, 6 * D), f32)
    xh_d = dram("xh_d", (N, D), f32)
    x1_d = dram("x1_d", (N, D), f32)
    h2_d = dram("h2_d", (N + P, D), f32)
    slots_d = dram("slots_d", (E * REGION, 1), i32)
    y_d = dram("y_d", (N + P, D), f32)

    top = ExitStack()
    sem = lambda name: top.enter_context(nc.semaphore(name))

    class Stage:
        def __init__(self, name, steps):
            self.sem, self.steps = sem(name), steps
        def after(self, step, n):
            return n * len(self.steps) + self.steps.index(step) + 1

    def names(base, n):
        return [f"{base}{i}" for i in range(n)]

    with top:
        sb = lambda name, shape, dt, c=top: c.enter_context(nc.sbuf_tensor(name, shape, dt))
        w_gate = sb("w_gate", [P, E, KD, I], f32)
        w_up = sb("w_up", [P, E, KD, I], f32)
        w_down = sb("w_down", [P, E, KI, D], f32)
        ident = sb("ident", [P, P], f32)
        tile_expert = sb("tile_expert", [1, TILES + 1], i32)
        tile_slot = sb("tile_slot", [1, TILES + 1], i32)

        w_loaded = [sem(f"w_loaded{j}") for j in range(3)]

        with ExitStack() as att:
            sa_ = lambda name, shape, dt: sb(name, shape, dt, att)
            ps = [att.enter_context(nc.psum_tensor(f"bank{i}", [P, 512], f32)) for i in range(8)]
            ST, O, X = ps[0:2], ps[2:4], ps[4:8]

            x = sa_("x", [P, TPB, D], f32)
            h = sa_("h", [P, TPB, D], f32)
            rows = sa_("rows", [P, TPB, D], f32)
            x1 = sa_("x1", [P, TPB, D], f32)
            mod_a = sa_("mod_a", [P, 3, D], f32)
            mod_c = sa_("mod_c", [P, 3, D], f32)
            t_hi = sa_("t_hi", [P, KD, S], f32r)
            t_lo = sa_("t_lo", [P, KD, S], f32r)
            q_hi = sa_("q_hi", [P, GROUPS, S], f32r)
            q_lo = sa_("q_lo", [P, GROUPS, S], f32r)
            k_hi = sa_("k_hi", [P, GROUPS, S], f32r)
            k_lo = sa_("k_lo", [P, GROUPS, S], f32r)
            max_rows = k_lo[0:HEADS * TPB, 0, :]
            v_new = sa_("v_new", [P, TPB, P], f32)
            qa = sa_("qa", [P, HEADS, S], f32r)
            qb = sa_("qb", [P, HEADS, S], f32r)
            ka = sa_("ka", [P, GROUPS, S], f32r)
            kb = sa_("kb", [P, GROUPS, S], f32r)
            va = sa_("va", [P, TPB, GROUPS, 2 * DH], f32)
            prob = sa_("prob", [P, 2, S], f32)
            inv = sa_("inv", [DH, S], f32)
            o_t = sa_("o_t", [P, HEADS // 2, S], f32)
            spare = w_down[:, :, :, :].rearrange("p e k d -> p (e k d)")
            wmod = spare[:, 0:KD * 6 * D].rearrange("p (k n) -> p k n", k=KD)
            at = KD * 6 * D
            mod_row = spare[0:B, at:at + 6 * D]
            wq_raw = spare[:, at + 1536:at + 2048].rearrange("p (o d) -> p o d", d=D)
            wk_raw = spare[:, at + 2048:at + 2304]
            wv_raw = spare[:, at + 2304:at + 2560]
            wo_raw = spare[:, at + 2560:at + 3072].rearrange("p (o d) -> p o d", d=D)
            c4 = spare[0:B, at + 3072:at + 3328]
            sc4 = spare[0:B, at + 3328:at + 3584]
            gate_abs = spare[0:B, at + 3584:at + 3840]
            gate_raw = spare[0:B, at + 3840:at + 4096]
            gate_sign = spare[0:B, at + 4096:at + 4352]
            wq_hi = sa_("wq_hi", [P, KD, D], f32r)
            wq_lo = sa_("wq_lo", [P, KD, D], f32r)
            wk_hi = sa_("wk_hi", [P, KD, GROUPS, 2, DH], f32r)
            wk_lo = sa_("wk_lo", [P, KD, GROUPS, 2, DH], f32r)
            wv_hi = sa_("wv_hi", [P, KD, P], f32r)
            wv_lo = sa_("wv_lo", [P, KD, P], f32r)
            wo_t = sa_("wo_t", [P, KD, D], f32)
            wo_g = sa_("wo_g", [P, KD, D], f32)
            wr = sa_("wr", [P, KD, E], f32)
            wr_hi = sa_("wr_hi", [P, KD, E], f32r)
            wr_lo = sa_("wr_lo", [P, KD, E], f32r)
            mask = sa_("mask", [HEADS * TPB, TPB, P], f32)
            upper = sa_("upper", [P, P], bf16)
            ones = sa_("ones", [P, P], bf16)
            rev8 = sa_("rev8", [P, TPB, E], f32)
            rev8i = sa_("rev8i", [P, TPB, E], i32)
            mhalf = sa_("mhalf", [P, TPB], f32)
            half = sa_("half", [P, TPB], f32)
            mone = sa_("mone", [P, TPB], f32)
            nsc = sa_("nsc", [P, KD], f32)
            ssc = sa_("ssc", [P, KD], f32)
            nss = sa_("nss", [P, KD], f32)
            stats = sa_("stats", [P, TPB, 6], f32)
            mv = sa_("mv", [P, TPB, 2], f32)
            var = sa_("var", [P, TPB], f32)
            rstd = sa_("rstd", [P, TPB], f32)
            nmean = sa_("nmean", [P, TPB], f32)
            nmr = sa_("nmr", [P, TPB], f32)
            ssq = sa_("ssq", [P, TPB], f32)
            nrm = sa_("nrm", [P, TPB], f32)
            nrme = sa_("nrme", [P, TPB], f32)
            rinv = sa_("rinv", [P, TPB], f32)
            stats2 = sa_("stats2", [P, TPB, 6], f32)
            mv2 = sa_("mv2", [P, TPB, 2], f32)
            var2 = sa_("var2", [P, TPB], f32)
            rstd2 = sa_("rstd2", [P, TPB], f32)
            nmean2 = sa_("nmean2", [P, TPB], f32)
            nmr2 = sa_("nmr2", [P, TPB], f32)
            neg_max = sa_("neg_max", [P, HEADS * TPB], f32)
            lmax = sa_("lmax", [P, TPB], f32)
            leq = sa_("leq", [P, TPB, E], f32)
            lw = sa_("lw", [P, TPB, E], f32)
            erev = sa_("erev", [P, TPB], f32)
            onehot = sa_("onehot", [P, TPB, E], bf16)
            before = sa_("before", [P, TPB + 1, E], bf16)
            prank = sa_("prank", [P, TPB, E], f32)
            rank = sa_("rank", [P, TPB], f32)
            slot_f = sa_("slot_f", [P, TPB], f32)
            slot = sa_("slot", [P, TPB], i32)
            token = sa_("token", [P, TPB], i32)
            fill_a = sa_("fill_a", [P, E * REGION // P], i32)
            fill = sa_("fill", [P, E * REGION // P], i32)
            counts = sa_("counts", [1, E], i32)
            ntile_i = sa_("ntile_i", [1, E], i32)
            ntile = sa_("ntile", [1, E], f32)
            pre = [sa_(f"pre{j}", [1, E], f32) for j in range(3)]
            tidx = sa_("tidx", [1, TILES + 1, E - 1], i32)
            passed = sa_("passed", [1, TILES + 1, E - 1], f32)
            passed_n = sa_("passed_n", [1, TILES + 1, E - 1], f32)
            te_f = sa_("te_f", [1, TILES + 1], f32)
            base_f = sa_("base_f", [1, TILES + 1], f32)
            j_f = sa_("j_f", [1, TILES + 1], f32)
            ts_f = sa_("ts_f", [1, TILES + 1], f32)
            sc_t = sa_("sc_t", [P, KD, B], f32)

            c_loaded = sem("c_loaded")
            wmod_loaded = sem("wmod_loaded")
            raw_loaded = sem("raw_loaded")
            small_loaded = sem("small_loaded")
            const_ready = sem("const_ready")
            mod_stored, zeros_stored = sem("mod_stored"), sem("zeros_stored")
            x_loaded, moda_loaded, modc_loaded, x1_loaded = (sem("x_loaded"), sem("moda_loaded"),
                                                             sem("modc_loaded"), sem("x1_loaded"))
            xh_stored, x1_stored, h2_stored = sem("xh_stored"), sem("x1_stored"), sem("h2_stored")
            q_live = [sem(f"q_live{hh}") for hh in range(HEADS)]
            k_live = [sem(f"k_live{g}") for g in range(GROUPS)]
            slots_filled = sem("slots_filled")
            slots_written = sem("slots_written")
            scored, exped, pved = sem("scored"), sem("exped"), sem("pved")
            inverted, normed = sem("inverted"), sem("normed")
            table_ready = sem("table_ready")
            counted = sem("counted")

            prep_pe = Stage("prep_pe", names("t", 2) + names("q", 2) + names("k", 2) + ["v"]
                            + names("max", STEPS) + ["maxt"])
            prep_act = Stage("prep_act", names("xn", TPB) + names("sq", TPB) + names("hn", TPB)
                             + names("t", 2) + names("q", 2) + names("k", 2) + ["v"])
            prep_dve = Stage("prep_dve", names("st", TPB) + names("ag", TPB) + names("t", 2)
                             + names("q", 2) + names("k", 2) + names("max", STEPS) + ["maxrow"])
            prep_pool = Stage("prep_pool", ["var", "rstd", "nmean", "nmr", "scaled", "h", "nrm",
                                            "nrme", "rinv", "gated", "xh"])
            close_pe = Stage("close_pe", ["wo0", "wo1", "t0", "t1", "logits", "prefix"])
            close_act = Stage("close_act", names("xn", TPB) + names("t", 2))
            close_dve = Stage("close_dve", ["x1_0", "x1_1"] + names("st", TPB) + names("ag", TPB)
                              + names("t", 2) + ["lmax", "leq", "lw", "erev", "onehot", "carry"]
                              + names("add", TPB) + ["prank", "rank", "slot_f", "slot"])
            close_pool = Stage("close_pool", ["wo_g", "var", "rstd", "nmean", "nmr", "scaled", "h2",
                                              "token"])

            setup_pe = Stage("setup_pe", ["sc", "mod", "w"])
            setup_act = Stage("setup_act", ["silu"] + names("w", 4 * KD) + ["wo", "wr"])
            setup_dve = Stage("setup_dve", ["kb", "fill", "rev8", "nss", "sc", "sa", "ca", "sb", "cb"]
                              + [g + s_ for g in ("ga", "gb") for s_ in ("_raw", "_abs", "_sign", "_pm", "_max", "")]
                              + names("w", 4 * KD) + ["wr"])
            setup_pool = Stage("setup_pool", names("memset", 10) + ["ident", "upper"] + names("mask", HEADS)
                               + ["rev8", "token", "tidx", "fill_iota", "fill"])

            def over_tiles(row):
                return row.unsqueeze(1).to_broadcast([P, TPB, D])

            def w(eng, s, value):
                if not isinstance(value, int) or value > 0:
                    eng.wait_ge(s, value)

            def wait(eng, stage, step, n):
                if not isinstance(n, int) or n >= 0:
                    w(eng, stage.sem, stage.after(step, n))

            def samples(eng, body):
                for b in range(B):
                    body(b, first=(b == 0), last=(b == B - 1))

            block = att.enter_context(nc.Block())

            def xrows(ap, n):
                return ap[ds(n * S, S), :].rearrange("(t p) d -> p t d", p=P)

            x_rows = x_in.rearrange("b s d -> (b s) d")

            @block.sync
            def _(sp):
                sp.dma_start(c4, io["L0_c"]).then_inc(c_loaded, 16)
                sp.dma_start(x[:, :, :], xrows(x_rows, 0)).then_inc(x_loaded, 16)
                sp.dma_start(wmod, io["L0_wmod"].rearrange("(k p) n -> p k n", p=P)).then_inc(wmod_loaded, 16)
                sp.dma_start(nsc[:, :], io["L0_attn_norm_scale"].rearrange("(k p) -> p k", p=P), allow_slow_non_contiguous=True).then_inc(small_loaded, 16)
                sp.dma_start(ssc[:, :], io["L0_attn_split_scale"].rearrange("(k p) -> p k", p=P), allow_slow_non_contiguous=True).then_inc(small_loaded, 16)
                sp.dma_start(wr[:, :, :], io["L0_ffn_router_w"].rearrange("(k p) e -> p k e", p=P)).then_inc(small_loaded, 16)
                sp.dma_start(wq_raw, io["L0_attn_Wq"].rearrange("(o p) d -> p o d", p=P)).then_inc(raw_loaded, 16)
                sp.dma_start(wk_raw, io["L0_attn_Wk"]).then_inc(raw_loaded, 16)
                sp.dma_start(wv_raw, io["L0_attn_Wv"]).then_inc(raw_loaded, 16)
                sp.dma_start(wo_raw, io["L0_attn_Wo"].rearrange("(o p) d -> p o d", p=P)).then_inc(raw_loaded, 16)
                sp.wait_ge(setup_dve.sem, setup_dve.after("gb", 0))
                sp.dma_start(mod_d, mod_row).then_inc(mod_stored, 16)
                sp.wait_ge(setup_pool.sem, setup_pool.after("fill", 0))
                sp.dma_start(slots_d.rearrange("(p j) o -> p (j o)", p=P), fill[:, :]).then_inc(slots_filled, 16)
                sp.dma_start(h2_d[N:N + P, :], h[:, 0, :]).then_inc(zeros_stored, 16)

                def load_prep(p):
                    wait(sp, prep_pool, "xh", p - 1)
                    if isinstance(p, int) and p == 0:
                        sp.wait_ge(mod_stored, 16)
                    sp.dma_start(mod_a[:, :, :].rearrange("p r d -> p (r d)"),
                                 mod_d[ds(p, 1), 0:3 * D].partition_broadcast(P)).then_inc(moda_loaded, 16)
                    if not (isinstance(p, int) and p == 0):
                        sp.wait_ge(xh_stored, 16 * p)
                        sp.dma_start(x[:, :, :], xrows(x_rows, p)).then_inc(x_loaded, 16)

                def store_xh(p):
                    wait(sp, prep_pool, "xh", p)
                    sp.dma_start(xrows(xh_d, p), x[:, :, :]).then_inc(xh_stored, 16)

                def move_k(p, g):
                    wait(sp, prep_act, "v", p)
                    wait(sp, prep_dve, f"k{g}", p)
                    w(sp, scored, STEPS * p - STEPS + (g + 1) * HPG * TPB if not isinstance(p, int) or p > 0 else 0)
                    w(sp, pved, STEPS * p - STEPS + (g + 1) * HPG * TPB if not isinstance(p, int) or p > 0 else 0)
                    sp.dma_start(ka[0:DH, g, :].bitcast(f32), k_hi[0:DH, g, :].bitcast(f32)).then_inc(k_live[g], 16)
                    sp.dma_start(ka[DH:P, g, :].bitcast(f32), k_lo[DH:P, g, :].bitcast(f32)).then_inc(k_live[g], 16)
                    sp.dma_start(kb[0:DH, g, :].bitcast(f32), k_hi[0:DH, g, :].bitcast(f32)).then_inc(k_live[g], 16)
                    sp.dma_start(va[:, :, g, 0:DH], v_new[:, :, g * DH:(g + 1) * DH]).then_inc(k_live[g], 16)

                def move_q(p, hh):
                    r, g = (hh % HPG) * DH, hh // HPG
                    wait(sp, prep_dve, "maxrow", p)
                    wait(sp, prep_act, f"q{g}", p)
                    w(sp, scored, STEPS * p - STEPS + (hh + 1) * TPB if not isinstance(p, int) or p > 0 else 0)
                    sp.dma_start(qa[0:DH, hh, :].bitcast(f32), q_hi[r:r + DH, g, :].bitcast(f32)).then_inc(q_live[hh], 16)
                    sp.dma_start(qa[DH:P, hh, :].bitcast(f32), q_hi[r:r + DH, g, :].bitcast(f32)).then_inc(q_live[hh], 16)
                    sp.dma_start(qb[0:DH, hh, :].bitcast(f32), q_lo[r:r + DH, g, :].bitcast(f32)).then_inc(q_live[hh], 16)
                    sp.dma_start(qb[DH:MK, hh, :].bitcast(f32), max_rows[hh * TPB:(hh + 1) * TPB, :].bitcast(f32)).then_inc(q_live[hh], 16)

                def moves(p):
                    for g in range(GROUPS):
                        move_k(p, g)
                        for hh in range(g * HPG, (g + 1) * HPG):
                            move_q(p, hh)

                def load_x1(c):
                    sp.wait_ge(xh_stored, 16 * c + 16)
                    w(sp, x1_stored, 16 * c)
                    sp.dma_start(x1[:, :, :], xrows(xh_d, c)).then_inc(x1_loaded, 16)

                def store_x1(c):
                    wait(sp, close_dve, "x1_1", c)
                    sp.dma_start(xrows(x1_d, c), x1[:, :, :]).then_inc(x1_stored, 16)

                def store_h2(c):
                    wait(sp, close_pool, "h2", c)
                    sp.dma_start(xrows(h2_d, c), rows[:, :, :]).then_inc(h2_stored, 16)

                def load_modc(b):
                    wait(sp, close_pool, "h2", b - 1)
                    sp.dma_start(mod_c[:, :, :].rearrange("p r d -> p (r d)"),
                                 mod_d[ds(b, 1), 2 * D:5 * D].partition_broadcast(P)).then_inc(modc_loaded, 16)

                load_prep(0)
                store_xh(0)
                moves(0)

                def body(b, first, last):
                    if not last:
                        load_prep(b + 1)
                    if not first:
                        load_x1(b - 1)
                        store_x1(b - 1)
                    if not last:
                        store_xh(b + 1)
                    if not first:
                        store_h2(b - 1)
                    load_modc(b)
                    if not last:
                        moves(b + 1)

                samples(sp, body)
                load_x1(B - 1)
                store_x1(B - 1)
                store_h2(B - 1)
                sp.wait_ge(x1_stored, 16 * B)
                sp.wait_ge(h2_stored, 16 * B)
                sp.wait_ge(zeros_stored, 16)

            @block.gpsimd
            def _(pool):
                nc_ = nc.gpsimd
                def done(ins, stage):
                    return ins.then_inc(stage.sem, 1)

                nc_.memset(ident[:, :], 0.0).then_inc(setup_pool.sem, 1)
                nc_.memset(mask[:, :, :], 0.0).then_inc(setup_pool.sem, 1)
                nc_.memset(upper[:, :], 1.0).then_inc(setup_pool.sem, 1)
                nc_.memset(ones[:, :], 1.0).then_inc(setup_pool.sem, 1)
                nc_.memset(mhalf[:, :], -0.5).then_inc(setup_pool.sem, 1)
                nc_.memset(half[:, :], 0.5).then_inc(setup_pool.sem, 1)
                nc_.memset(mone[:, :], -1.0).then_inc(setup_pool.sem, 1)
                nc_.memset(h[:, 0, :], 0.0).then_inc(setup_pool.sem, 1)
                nc_.memset(va[:, :, :, DH:2 * DH], 1.0).then_inc(setup_pool.sem, 1)
                nc_.memset(before[:, TPB, :], 0.0).then_inc(setup_pool.sem, 1)
                pool.wait_ge(setup_pool.sem, 3)
                nc_.affine_select(out=ident[:, :], in_=ident[:, :], compare_op=ALU.not_equal, fill=1.0, base=0,
                                  pattern=[[-1, P]], channel_multiplier=1).then_inc(setup_pool.sem, 1)
                nc_.affine_select(out=upper[:, :], in_=upper[:, :], compare_op=ALU.is_gt, fill=0.0, base=0,
                                  pattern=[[1, P]], channel_multiplier=-1).then_inc(setup_pool.sem, 1)
                for hh in range(HEADS):
                    pool.wait_ge(setup_pool.sem, setup_pool.after("upper", 0) + hh)
                    nc_.affine_select(out=mask[:, :, :], in_=mask[:, :, :], compare_op=ALU.not_equal, fill=1.0,
                                      base=TPB * hh, pattern=[[1, TPB], [0, P]],
                                      channel_multiplier=-1).then_inc(setup_pool.sem, 1)
                nc_.iota(rev8i[:, :, :], pattern=[[0, TPB], [-1, E]], base=E, channel_multiplier=0).then_inc(setup_pool.sem, 1)
                nc_.iota(token[:, :], pattern=[[P, TPB]], base=0, channel_multiplier=1).then_inc(setup_pool.sem, 1)
                nc_.iota(tidx[:, :, :], pattern=[[1, TILES + 1], [0, E - 1]], base=0, channel_multiplier=0).then_inc(setup_pool.sem, 1)
                nc_.iota(fill_a[:, :], pattern=[[1, E * REGION // P]], base=0,
                         channel_multiplier=E * REGION // P).then_inc(setup_pool.sem, 1)
                pool.wait_ge(setup_dve.sem, setup_dve.after("fill", 0))
                nc_.tensor_copy(fill[:, :], fill_a[:, :]).then_inc(setup_pool.sem, 1)

                def prep_stats(p):
                    wait(pool, prep_dve, "ag3", p)
                    nc_.tensor_scalar(var[:, :], mv[:, :, 1], LN_EPS, None, ALU.add).then_inc(prep_pool.sem, 1)
                    wait(pool, prep_pool, "var", p)
                    nc_.tensor_tensor(rstd[:, :], var[:, :], mhalf[:, :], ALU.pow).then_inc(prep_pool.sem, 1)
                    nc_.tensor_tensor(nmean[:, :], mv[:, :, 0], mone[:, :], ALU.mult).then_inc(prep_pool.sem, 1)
                    wait(pool, prep_pool, "nmean", p)
                    nc_.tensor_tensor(nmr[:, :], nmean[:, :], rstd[:, :], ALU.mult).then_inc(prep_pool.sem, 1)

                def prep_h(p):
                    wait(pool, prep_act, "xn3", p)
                    pool.wait_ge(moda_loaded, 16 * p + 16)
                    nc_.tensor_tensor(h[:, :, :], h[:, :, :], over_tiles(mod_a[:, 1, :]), ALU.mult).then_inc(prep_pool.sem, 1)
                    wait(pool, prep_pool, "scaled", p)
                    nc_.tensor_tensor(h[:, :, :], h[:, :, :], over_tiles(mod_a[:, 0, :]), ALU.add).then_inc(prep_pool.sem, 1)

                def prep_rms(p):
                    wait(pool, prep_act, "sq3", p)
                    nc_.tensor_tensor(nrm[:, :], ssq[:, :], half[:, :], ALU.pow).then_inc(prep_pool.sem, 1)
                    wait(pool, prep_pool, "nrm", p)
                    nc_.tensor_scalar(nrme[:, :], nrm[:, :], float(D) ** -0.5, RMS_EPS, ALU.mult, ALU.add).then_inc(prep_pool.sem, 1)
                    wait(pool, prep_pool, "nrme", p)
                    nc_.tensor_tensor(rinv[:, :], nrme[:, :], mone[:, :], ALU.pow).then_inc(prep_pool.sem, 1)

                def prep_xh(p):
                    wait(pool, prep_act, "hn3", p)
                    nc_.tensor_tensor(h[:, :, :], h[:, :, :], over_tiles(mod_a[:, 2, :]), ALU.mult).then_inc(prep_pool.sem, 1)
                    wait(pool, prep_pool, "gated", p)
                    nc_.tensor_tensor(x[:, :, :], x[:, :, :], h[:, :, :], ALU.add).then_inc(prep_pool.sem, 1)

                def close_gate(c):
                    pool.wait_ge(modc_loaded, 16 * c + 16)
                    wait(pool, close_pe, "wo1", c - 1)
                    nc_.tensor_tensor(wo_g[:, :, :], wo_t[:, :, :],
                                      mod_c[:, 0, :].unsqueeze(1).to_broadcast([P, KD, D]), ALU.mult).then_inc(close_pool.sem, 1)

                def close_stats(c):
                    wait(pool, close_dve, "ag3", c)
                    nc_.tensor_scalar(var2[:, :], mv2[:, :, 1], LN_EPS, None, ALU.add).then_inc(close_pool.sem, 1)
                    wait(pool, close_pool, "var", c)
                    nc_.tensor_tensor(rstd2[:, :], var2[:, :], mhalf[:, :], ALU.pow).then_inc(close_pool.sem, 1)
                    nc_.tensor_tensor(nmean2[:, :], mv2[:, :, 0], mone[:, :], ALU.mult).then_inc(close_pool.sem, 1)
                    wait(pool, close_pool, "nmean", c)
                    nc_.tensor_tensor(nmr2[:, :], nmean2[:, :], rstd2[:, :], ALU.mult).then_inc(close_pool.sem, 1)

                def close_h2(c):
                    wait(pool, close_act, "xn3", c)
                    nc_.tensor_tensor(rows[:, :, :], rows[:, :, :], over_tiles(mod_c[:, 2, :]), ALU.mult).then_inc(close_pool.sem, 1)
                    wait(pool, close_pool, "scaled", c)
                    nc_.tensor_tensor(rows[:, :, :], rows[:, :, :], over_tiles(mod_c[:, 1, :]), ALU.add).then_inc(close_pool.sem, 1)

                def close_slots(c):
                    wait(pool, close_dve, "slot", c)
                    if isinstance(c, int) and c == 0:
                        pool.wait_ge(slots_filled, 16)
                    for t in range(TPB):
                        nc_.indirect_dma_start(out=slots_d, out_offset=bass.IndirectOffsetOnAxis(ap=slot[:, t:t + 1], axis=0),
                                               in_=token[:, t:t + 1], in_offset=None).then_inc(slots_written, 16)
                    pool.wait_ge(slots_written, 16 * TPB * (c + 1))
                    nc_.tensor_scalar(token[:, :], token[:, :], float(S), None, ALU.add).then_inc(close_pool.sem, 1)

                def prep(p):
                    prep_stats(p)
                    prep_h(p)
                    prep_rms(p)
                    prep_xh(p)

                prep(0)

                def body(b, first, last):
                    if not last:
                        prep_stats(b + 1)
                    if not first:
                        close_stats(b - 1)
                    if not last:
                        prep_h(b + 1)
                        prep_rms(b + 1)
                        prep_xh(b + 1)
                    if not first:
                        close_h2(b - 1)
                        close_slots(b - 1)
                    close_gate(b)

                samples(pool, body)
                close_stats(B - 1)
                close_h2(B - 1)
                close_slots(B - 1)

            @block.scalar
            def _(act):
                A = nc.scalar.activation
                for e in range(E):
                    act.dma_start(w_gate[:, e, :, :], io["L0_ffn_gate_w"][e, :, :].rearrange("(k p) i -> p k i", p=P)).then_inc(w_loaded[0], 16)
                    act.dma_start(w_up[:, e, :, :], io["L0_ffn_up_w"][e, :, :].rearrange("(k p) i -> p k i", p=P)).then_inc(w_loaded[1], 16)
                act.wait_ge(c_loaded, 16)
                A(sc4, c4, ACT.Silu).then_inc(setup_act.sem, 1)
                act.wait_ge(setup_dve.sem, setup_dve.after("nss", 0))
                act.wait_ge(setup_pe.sem, setup_pe.after("w", 0))
                for k in range(KD):
                    A(wq_hi[:, k, :], O[k][:, 0:D], ACT.Copy, scale=nss[:, k:k + 1]).then_inc(setup_act.sem, 1)
                    for r in range(2):
                        A(wk_hi[:, k, :, r, :], O[k][:, D:D + P].rearrange("p (g c) -> p g c", g=GROUPS), ACT.Copy,
                          scale=nss[:, k:k + 1]).then_inc(setup_act.sem, 1)
                    A(wv_hi[:, k, :], O[k][:, D + P:D + 2 * P], ACT.Copy, scale=nss[:, k:k + 1]).then_inc(setup_act.sem, 1)
                A(wo_t[:, :, :].rearrange("p k d -> p (k d)"), ST[0][:, :], ACT.Copy).then_inc(setup_act.sem, 1)
                A(wr_hi[:, :, :], wr[:, :, :], ACT.Copy).then_inc(setup_act.sem, 1)

                def prep_norm(p):
                    act.wait_ge(x_loaded, 16 * p + 16)
                    wait(act, prep_pool, "nmr", p)
                    if isinstance(p, int) and p == 0:
                        act.wait_ge(zeros_stored, 16)
                    for t in range(TPB):
                        A(h[:, t, :], x[:, t, :], ACT.Identity, bias=nmr[:, t:t + 1], scale=rstd[:, t:t + 1]).then_inc(prep_act.sem, 1)

                def prep_square(p):
                    wait(act, prep_pool, "h", p)
                    if not isinstance(p, int) or p >= 3:
                        w(act, h2_stored, 16 * (p - 2))
                        wait(act, close_pe, "prefix", p - 3)
                    for t in range(TPB):
                        A(rows[:, t, :], h[:, t, :], ACT.Square, accum_out=ssq[:, t:t + 1]).then_inc(prep_act.sem, 1)

                def prep_rows(p):
                    wait(act, prep_pool, "rinv", p)
                    for t in range(TPB):
                        A(rows[:, t, :], h[:, t, :], ACT.Copy, scale=rinv[:, t:t + 1]).then_inc(prep_act.sem, 1)

                def prep_t(p):
                    for k in range(KD):
                        wait(act, prep_pe, f"t{k}", p)
                        A(t_hi[:, k, :], X[2 + k][:, :], ACT.Copy).then_inc(prep_act.sem, 1)

                def prep_q(p):
                    for g in range(GROUPS):
                        wait(act, prep_pe, f"q{g}", p)
                        for hh in (HPG * g, HPG * g + 1):
                            w(act, q_live[hh], 64 * p)
                        A(q_hi[:, g, :], X[g][:, :], ACT.Copy).then_inc(prep_act.sem, 1)

                def prep_kv(p):
                    for g in range(GROUPS):
                        wait(act, prep_pe, f"k{g}", p)
                        w(act, k_live[g], 64 * p)
                        A(k_hi[:, g, :], X[2 + g][:, :], ACT.Copy).then_inc(prep_act.sem, 1)
                    wait(act, prep_pe, "v", p)
                    A(v_new[:, :, :].rearrange("p t c -> p (t c)"), X[0][:, :], ACT.Copy).then_inc(prep_act.sem, 1)

                def close_norm(c, p):
                    wait(act, close_pool, "nmr", c)
                    w(act, h2_stored, 16 * c)
                    wait(act, prep_pe, "t1", p)
                    for t in range(TPB):
                        A(rows[:, t, :], x1[:, t, :], ACT.Identity, bias=nmr2[:, t:t + 1], scale=rstd2[:, t:t + 1]).then_inc(close_act.sem, 1)

                def close_t(c):
                    for k in range(KD):
                        wait(act, close_pe, f"t{k}", c)
                        A(t_hi[:, k, :], X[1 + k][:, :], ACT.Copy).then_inc(close_act.sem, 1)

                prep_norm(0)
                prep_square(0)
                prep_rows(0)
                prep_t(0)
                prep_q(0)
                prep_kv(0)
                act.wait_ge(mod_stored, 16)
                act.wait_ge(setup_dve.sem, setup_dve.after("wr", 0))
                for e in range(E):
                    act.dma_start(w_down[:, e, :, :], io["L0_ffn_down_w"][e, :, :].rearrange("(k p) d -> p k d", p=P)).then_inc(w_loaded[2], 16)

                def exp(b, s, first):
                    act.wait_ge(scored, STEPS * b + s + 1)
                    if not (first and s < 2):
                        act.wait_ge(pved, STEPS * b + s - 1)
                    A(prob[:, s % 2, :], ST[s % 2][:, :], ACT.Exp, scale=SCALE).then_inc(exped, 1)

                def body(b, first, last):
                    for s in range(STEPS):
                        exp(b, s, first)
                        if not last:
                            if s == 1:
                                prep_norm(b + 1)
                            if s == 3:
                                prep_square(b + 1)
                            if s == 4:
                                prep_rows(b + 1)
                            if s == 6:
                                prep_t(b + 1)
                            if s == 7:
                                prep_q(b + 1)
                            if s == 8:
                                prep_kv(b + 1)
                        if not first:
                            if s == 9:
                                close_norm(b - 1, b if last else b + 1)
                            if s == 14:
                                close_t(b - 1)

                samples(act, body)
                close_norm(B - 1, B - 1)
                close_t(B - 1)

            @block.vector
            def _(dve):
                V = nc.vector
                V.memset(kb[DH:MK, :, :].bitcast(f32), 1.0).then_inc(setup_dve.sem, 1)
                dve.wait_ge(setup_pool.sem, setup_pool.after("fill_iota", 0))
                V.tensor_scalar(fill_a[:, :], fill_a[:, :], P - 1, N, ALU.bitwise_and, ALU.bitwise_or).then_inc(setup_dve.sem, 1)
                V.tensor_copy(rev8[:, :, :], rev8i[:, :, :]).then_inc(setup_dve.sem, 1)
                dve.wait_ge(small_loaded, 48)
                V.tensor_tensor(nss[:, :], nsc[:, :], ssc[:, :], ALU.mult).then_inc(setup_dve.sem, 1)
                dve.wait_ge(setup_pe.sem, setup_pe.after("sc", 0))
                V.tensor_copy(sc_t[:, :, :], X[0][:, 0:2 * B].rearrange("p (k b) -> p k b", k=KD)).then_inc(setup_dve.sem, 1)
                dve.wait_ge(setup_pe.sem, setup_pe.after("mod", 0))
                seg = lambda r: mod_row[:, r * D:(r + 1) * D]
                src = lambda r: X[1 + r // 2][0:B, (r % 2) * D:(r % 2 + 1) * D]
                V.tensor_copy(seg(0), src(0)).then_inc(setup_dve.sem, 1)
                V.tensor_scalar(seg(1), src(1), 1.0, None, ALU.add).then_inc(setup_dve.sem, 1)
                V.tensor_copy(seg(3), src(3)).then_inc(setup_dve.sem, 1)
                V.tensor_scalar(seg(4), src(4), 1.0, None, ALU.add).then_inc(setup_dve.sem, 1)
                for r, name in ((2, "ga"), (5, "gb")):
                    V.tensor_copy(gate_raw, src(r)).then_inc(setup_dve.sem, 1)
                    dve.wait_ge(setup_dve.sem, setup_dve.after(name + "_raw", 0))
                    V.scalar_tensor_tensor(out=gate_abs, in0=gate_raw, scalar=-1.0, in1=gate_raw, op0=ALU.mult, op1=ALU.max).then_inc(setup_dve.sem, 1)
                    V.tensor_scalar(gate_sign, gate_raw, 0.0, 2.0, ALU.is_ge, ALU.mult).then_inc(setup_dve.sem, 1)
                    dve.wait_ge(setup_dve.sem, setup_dve.after(name + "_sign", 0))
                    V.tensor_scalar(gate_sign, gate_sign, -1.0, None, ALU.add).then_inc(setup_dve.sem, 1)
                    V.tensor_scalar(gate_abs, gate_abs, 0.25, None, ALU.max).then_inc(setup_dve.sem, 1)
                    dve.wait_ge(setup_dve.sem, setup_dve.after(name + "_max", 0))
                    V.tensor_tensor(seg(r), gate_abs, gate_sign, ALU.mult).then_inc(setup_dve.sem, 1)
                    dve.wait_ge(setup_dve.sem, setup_dve.after(name, 0))
                dve.wait_ge(setup_act.sem, setup_act.after("wr", 0))
                for k in range(KD):
                    V.scalar_tensor_tensor(out=wq_lo[:, k, :], in0=O[k][:, 0:D], scalar=nss[:, k:k + 1],
                                           in1=wq_hi[:, k, :].bitcast(f32), op0=ALU.mult, op1=ALU.subtract).then_inc(setup_dve.sem, 1)
                    for r in range(2):
                        V.scalar_tensor_tensor(out=wk_lo[:, k, :, r, :], in0=O[k][:, D:D + P].rearrange("p (g c) -> p g c", g=GROUPS),
                                               scalar=nss[:, k:k + 1], in1=wk_hi[:, k, :, r, :].bitcast(f32),
                                               op0=ALU.mult, op1=ALU.subtract).then_inc(setup_dve.sem, 1)
                    V.scalar_tensor_tensor(out=wv_lo[:, k, :], in0=O[k][:, D + P:D + 2 * P], scalar=nss[:, k:k + 1],
                                           in1=wv_hi[:, k, :].bitcast(f32), op0=ALU.mult, op1=ALU.subtract).then_inc(setup_dve.sem, 1)
                V.tensor_tensor(wr_lo[:, :, :], wr[:, :, :], wr_hi[:, :, :].bitcast(f32), ALU.subtract).then_inc(setup_dve.sem, 1)

                def prep_stats(p):
                    dve.wait_ge(x_loaded, 16 * p + 16)
                    for t in range(TPB):
                        V.bn_stats(stats[:, t, :], x[:, t, :]).then_inc(prep_dve.sem, 1)
                    wait(dve, prep_dve, "st3", p)
                    wait(dve, prep_pool, "xh", p - 1)
                    for t in range(TPB):
                        V.bn_aggr(mv[:, t, :], stats[:, t, :]).then_inc(prep_dve.sem, 1)

                def prep_t(p):
                    for k in range(KD):
                        wait(dve, prep_act, f"t{k}", p)
                        V.tensor_tensor(t_lo[:, k, :], X[2 + k][:, :], t_hi[:, k, :].bitcast(f32), ALU.subtract).then_inc(prep_dve.sem, 1)

                def prep_qk(p):
                    for g in range(GROUPS):
                        wait(dve, prep_act, f"q{g}", p)
                        V.tensor_tensor(q_lo[:, g, :], X[g][:, :], q_hi[:, g, :].bitcast(f32), ALU.subtract).then_inc(prep_dve.sem, 1)
                    for g in range(GROUPS):
                        wait(dve, prep_act, f"k{g}", p)
                        V.tensor_tensor(k_lo[DH:P, g, :], X[2 + g][DH:P, :], k_hi[DH:P, g, :].bitcast(f32), ALU.subtract).then_inc(prep_dve.sem, 1)

                def prep_max(p, i):
                    wait(dve, prep_pe, f"max{i}", p)
                    V.tensor_reduce(neg_max[:, i:i + 1], X[(i + 1) % 4][:, :], AX.X, ALU.max, negate=True).then_inc(prep_dve.sem, 1)

                def prep_maxrow(p):
                    wait(dve, prep_pe, "maxt", p)
                    for hh in range(HEADS):
                        w(dve, q_live[hh], 64 * p)
                    V.tensor_tensor(max_rows.rearrange("r (t c) -> r t c", t=TPB),
                                    X[0][0:STEPS, 0:P].unsqueeze(1).to_broadcast([STEPS, TPB, P]), mask[:, :, :],
                                    ALU.mult).then_inc(prep_dve.sem, 1)

                def norm(b, hh):
                    dve.wait_ge(pved, STEPS * b + (hh + 1) * TPB)
                    wait(dve, close_pe, "wo1", b - 1)
                    w(dve, normed, HEADS * b + hh)
                    V.reciprocal(inv[:, :], O[hh % 2][DH:P, :]).then_inc(inverted, 1)
                    dve.wait_ge(inverted, HEADS * b + hh + 1)
                    r = (hh % HPG) * DH
                    V.tensor_tensor(o_t[r:r + DH, hh // HPG, :], O[hh % 2][0:DH, :], inv[:, :], ALU.mult).then_inc(normed, 1)

                def close_x1(c):
                    dve.wait_ge(x1_loaded, 16 * c + 16)
                    for j in range(2):
                        wait(dve, close_pe, f"wo{j}", c)
                        V.tensor_tensor(x1[:, 2 * j:2 * j + 2, :].rearrange("p t d -> p (t d)"), X[j][:, :],
                                        x1[:, 2 * j:2 * j + 2, :].rearrange("p t d -> p (t d)"), ALU.add).then_inc(close_dve.sem, 1)
                    wait(dve, close_dve, "x1_1", c)
                    for t in range(TPB):
                        V.bn_stats(stats2[:, t, :], x1[:, t, :]).then_inc(close_dve.sem, 1)
                    wait(dve, close_dve, "st3", c)
                    for t in range(TPB):
                        V.bn_aggr(mv2[:, t, :], stats2[:, t, :]).then_inc(close_dve.sem, 1)

                def close_t(c):
                    for k in range(KD):
                        wait(dve, close_act, f"t{k}", c)
                        V.tensor_tensor(t_lo[:, k, :], X[1 + k][:, :], t_hi[:, k, :].bitcast(f32), ALU.subtract).then_inc(close_dve.sem, 1)

                def close_route(c):
                    logits = X[3][:, 0:TPB * E].rearrange("p (t e) -> p t e", e=E)
                    bcast = lambda ap: ap.unsqueeze(2).to_broadcast([P, TPB, E])
                    wait(dve, close_pe, "logits", c)
                    V.tensor_reduce(lmax[:, :], logits, AX.X, ALU.max).then_inc(close_dve.sem, 1)
                    wait(dve, close_dve, "lmax", c)
                    V.tensor_tensor(leq[:, :, :], logits, bcast(lmax[:, :]), ALU.is_equal).then_inc(close_dve.sem, 1)
                    wait(dve, close_dve, "leq", c)
                    V.tensor_tensor(lw[:, :, :], leq[:, :, :], rev8[:, :, :], ALU.mult).then_inc(close_dve.sem, 1)
                    wait(dve, close_dve, "lw", c)
                    V.tensor_reduce(erev[:, :], lw[:, :, :], AX.X, ALU.max).then_inc(close_dve.sem, 1)
                    wait(dve, close_dve, "erev", c)
                    V.tensor_tensor(onehot[:, :, :], rev8[:, :, :], bcast(erev[:, :]), ALU.is_equal).then_inc(close_dve.sem, 1)
                    V.tensor_copy(before[:, 0, :], before[:, TPB, :]).then_inc(close_dve.sem, 1)
                    for t in range(TPB):
                        dve.wait_ge(close_dve.sem, close_dve.after("carry", c) + t)
                        V.tensor_tensor(before[:, t + 1, :], before[:, t, :], onehot[:, t, :], ALU.add).then_inc(close_dve.sem, 1)

                def close_slot(c):
                    wait(dve, close_pe, "prefix", c)
                    V.tensor_tensor(prank[:, :, :], X[3][:, 64:64 + TPB * E].rearrange("p (t e) -> p t e", e=E),
                                    onehot[:, :, :], ALU.mult).then_inc(close_dve.sem, 1)
                    wait(dve, close_dve, "prank", c)
                    V.tensor_reduce(rank[:, :], prank[:, :, :], AX.X, ALU.add).then_inc(close_dve.sem, 1)
                    wait(dve, close_dve, "rank", c)
                    V.scalar_tensor_tensor(out=slot_f[:, :], in0=erev[:, :], scalar=float(-REGION), in1=rank[:, :],
                                           op0=ALU.mult, op1=ALU.add).then_inc(close_dve.sem, 1)
                    wait(dve, close_dve, "slot_f", c)
                    w(dve, slots_written, 16 * TPB * c)
                    V.tensor_scalar(slot[:, :], slot_f[:, :], float(E * REGION), None, ALU.add).then_inc(close_dve.sem, 1)

                prep_stats(0)
                prep_t(0)
                prep_qk(0)
                for i in range(STEPS):
                    prep_max(0, i)
                prep_maxrow(0)

                def body(b, first, last):
                    if not last:
                        prep_stats(b + 1)
                    if not first:
                        close_x1(b - 1)
                    norm(b, 0)
                    if not last:
                        prep_t(b + 1)
                        prep_qk(b + 1)
                    norm(b, 1)
                    if not last:
                        for i in range(STEPS):
                            prep_max(b + 1, i)
                            if i == 11:
                                norm(b, 2)
                        prep_maxrow(b + 1)
                    else:
                        norm(b, 2)
                    if not first:
                        close_t(b - 1)
                    norm(b, 3)
                    if not first:
                        close_route(b - 1)
                        close_slot(b - 1)

                samples(dve, body)
                close_x1(B - 1)
                close_t(B - 1)
                close_route(B - 1)
                close_slot(B - 1)

                link = [0]
                def step(ins):
                    ins.then_inc(counted, 1)
                    link[0] += 1
                    dve.wait_ge(counted, link[0])
                dve.wait_ge(table_ready, 1)
                step(V.tensor_scalar(counts[:, :], X[0][0:1, 0:E], float(P - 1), None, ALU.add))
                step(V.tensor_scalar(ntile_i[:, :], counts[:, :], P.bit_length() - 1, None, ALU.arith_shift_right))
                step(V.tensor_copy(ntile[:, :], ntile_i[:, :]))
                last = ntile
                for j, d in enumerate((1, 2, 4)):
                    step(V.tensor_copy(pre[j][:, 0:d], last[:, 0:d]))
                    step(V.tensor_tensor(pre[j][:, d:E], last[:, d:E], last[:, 0:E - d], ALU.add))
                    last = pre[j]
                over = lambda ap: ap[:, 0:E - 1].unsqueeze(1).to_broadcast([1, TILES + 1, E - 1])
                step(V.tensor_tensor(passed[:, :, :], over(last), tidx[:, :, :], ALU.is_le))
                step(V.tensor_reduce(te_f[:, :], passed[:, :, :], AX.X, ALU.add))
                step(V.tensor_tensor(passed_n[:, :, :], passed[:, :, :], over(ntile), ALU.mult))
                step(V.tensor_reduce(base_f[:, :], passed_n[:, :, :], AX.X, ALU.add))
                step(V.tensor_tensor(j_f[:, :], tidx[:, :, 0], base_f[:, :], ALU.subtract))
                step(V.tensor_scalar(j_f[:, :], j_f[:, :], float(REGION // P - 1), float(P), ALU.min, ALU.mult))
                step(V.scalar_tensor_tensor(out=ts_f[:, :], in0=te_f[:, :], scalar=float(REGION), in1=j_f[:, :], op0=ALU.mult, op1=ALU.add))
                step(V.tensor_copy(tile_slot[:, :], ts_f[:, :]))
                step(V.tensor_copy(tile_expert[:, :], te_f[:, :]))

            @block.tensor
            def _(pe):
                T = nc.tensor
                def split_products(out_ap, pairs):
                    terms = [(a, c) for a_hi, a_lo, c_hi, c_lo in pairs for a, c in ((a_hi, c_hi), (a_lo, c_hi), (a_hi, c_lo))]
                    for n, (a, c) in enumerate(terms):
                        last = T.matmul(out_ap, a, c, start=(n == 0), stop=(n == len(terms) - 1))
                    return last

                pe.wait_ge(setup_pool.sem, setup_pool.after("ident", 0))
                pe.wait_ge(setup_act.sem, setup_act.after("silu", 0))
                for k in range(KD):
                    last = T.transpose(X[0][:, k * B:(k + 1) * B], sc4[:, k * P:(k + 1) * P], ident[0:B, 0:B])
                last.then_inc(setup_pe.sem, 1)
                pe.wait_ge(setup_dve.sem, setup_dve.after("sc", 0))
                pe.wait_ge(wmod_loaded, 16)
                for r in range(3):
                    for k in range(KD):
                        last = T.matmul(X[1 + r][0:B, :], sc_t[:, k, :], wmod[:, k, r * 512:(r + 1) * 512], start=(k == 0), stop=(k == KD - 1))
                last.then_inc(setup_pe.sem, 1)
                pe.wait_ge(raw_loaded, 64)
                for k in range(KD):
                    for o in range(KD):
                        T.transpose(O[k][:, o * P:(o + 1) * P], wq_raw[:, o, k * P:(k + 1) * P], ident[:, :])
                        T.transpose(ST[0][:, k * D + o * P:k * D + (o + 1) * P], wo_raw[:, o, k * P:(k + 1) * P], ident[:, :])
                    T.transpose(O[k][:, D:D + P], wk_raw[:, k * P:(k + 1) * P], ident[:, :])
                    last = T.transpose(O[k][:, D + P:D + 2 * P], wv_raw[:, k * P:(k + 1) * P], ident[:, :])
                last.then_inc(setup_pe.sem, 1)
                pe.wait_ge(setup_act.sem, setup_act.after("wr", 0))
                pe.wait_ge(setup_dve.sem, setup_dve.after("wr", 0))

                def transposed_rows(stage, banks):
                    for k in range(KD):
                        for t in range(TPB):
                            last = T.transpose(banks[k][:, t * P:(t + 1) * P], rows[:, t, k * P:(k + 1) * P], ident[:, :])
                        last.then_inc(stage.sem, 1)

                def prep_t(p):
                    wait(pe, prep_act, "hn3", p)
                    wait(pe, prep_dve, "max15", p - 1)
                    if not isinstance(p, int) or p >= 3:
                        wait(pe, close_act, "t1", p - 3)
                        wait(pe, close_dve, "slot", p - 3)
                    transposed_rows(prep_pe, X[2:4])

                def prep_q(p):
                    wait(pe, prep_act, "t1", p)
                    wait(pe, prep_dve, "t1", p)
                    wait(pe, prep_dve, "maxrow", p - 1)
                    wait(pe, close_dve, "x1_1", p - 2)
                    for g in range(GROUPS):
                        c = slice(g * P, (g + 1) * P)
                        split_products(X[g][:, :], [(wq_hi[:, k, c], wq_lo[:, k, c], t_hi[:, k, :], t_lo[:, k, :])
                                                    for k in range(KD)]).then_inc(prep_pe.sem, 1)

                def prep_k(p):
                    for g in range(GROUPS):
                        flat = lambda a, k: a[:, k, g, :, :].rearrange("p r c -> p (r c)")
                        split_products(X[2 + g][:, :], [(flat(wk_hi, k), flat(wk_lo, k), t_hi[:, k, :], t_lo[:, k, :])
                                                        for k in range(KD)]).then_inc(prep_pe.sem, 1)

                def prep_v(p):
                    wait(pe, prep_act, "q0", p)
                    wait(pe, prep_dve, "q0", p)
                    for t in range(TPB):
                        c = slice(t * P, (t + 1) * P)
                        last = split_products(X[0][:, c], [(t_hi[:, k, c], t_lo[:, k, c], wv_hi[:, k, :], wv_lo[:, k, :])
                                                           for k in range(KD)])
                    last.then_inc(prep_pe.sem, 1)

                def prep_max(p, i):
                    if i == 0:
                        wait(pe, prep_act, "k1", p)
                        wait(pe, prep_dve, "k1", p)
                    if i == 3:
                        wait(pe, prep_act, "v", p)
                    if i >= 4:
                        wait(pe, prep_dve, f"max{i - 4}", p)
                    hh, st = i // TPB, i % TPB
                    r, g = (hh % HPG) * DH, hh // HPG
                    T.matmul(X[(i + 1) % 4][:, :], q_hi[r:r + DH, g, st * P:(st + 1) * P], k_hi[r:r + DH, g, :],
                             start=True, stop=True).then_inc(prep_pe.sem, 1)

                def prep_maxt(p):
                    wait(pe, prep_dve, f"max{STEPS - 1}", p)
                    T.transpose(X[0][0:STEPS, 0:P], neg_max[:, :], ident[:, :]).then_inc(prep_pe.sem, 1)

                def close_wo(c):
                    wait(pe, close_pool, "wo_g", c)
                    pe.wait_ge(normed, HEADS * (c + 1))
                    wait(pe, prep_dve, "maxrow", c + 1 if not isinstance(c, int) else min(c + 1, B - 1))
                    wait(pe, close_act, "t1", c - 1)
                    wait(pe, close_dve, "t1", c - 1)
                    for j in range(2):
                        for i in range(2):
                            t = 2 * j + i
                            for k in range(KD):
                                last = T.matmul(X[j][:, i * D:(i + 1) * D], o_t[:, k, t * P:(t + 1) * P], wo_g[:, k, :],
                                                start=(k == 0), stop=(k == KD - 1))
                        last.then_inc(close_pe.sem, 1)

                def close_t(c, p):
                    wait(pe, close_pool, "h2", c)
                    wait(pe, close_dve, "x1_1", c)
                    wait(pe, prep_dve, "max15", p)
                    transposed_rows(close_pe, X[1:3])

                def close_logits(c, p):
                    wait(pe, close_act, "t1", c)
                    wait(pe, close_dve, "t1", c)
                    wait(pe, close_dve, "slot", c - 1)
                    for t in range(TPB):
                        cs = slice(t * P, (t + 1) * P)
                        last = split_products(X[3][:, t * E:(t + 1) * E],
                                              [(t_hi[:, k, cs], t_lo[:, k, cs], wr_hi[:, k, :], wr_lo[:, k, :]) for k in range(KD)])
                    last.then_inc(close_pe.sem, 1)

                def close_prefix(c):
                    wait(pe, close_dve, f"add{TPB - 1}", c)
                    o = X[3][:, 64:64 + TPB * E]
                    T.matmul(o, upper[:, :], onehot[:, :, :].rearrange("p t e -> p (t e)"), start=True, stop=False)
                    T.matmul(o, ones[:, :], before[:, 0:TPB, :].rearrange("p t e -> p (t e)"), start=False, stop=True).then_inc(close_pe.sem, 1)

                def score(b, s, first):
                    hh, t = s // TPB, s % TPB
                    g = hh // HPG
                    if t == 0:
                        pe.wait_ge(k_live[g], 64 * b + 64)
                        pe.wait_ge(q_live[hh], 64 * b + 64)
                    if not (first and s < 2):
                        pe.wait_ge(exped, STEPS * b + s - 1)
                    c = slice(t * P, (t + 1) * P)
                    T.matmul(ST[s % 2][:, :], ka[:, g, c], qa[:, hh, :], start=True, stop=False)
                    T.matmul(ST[s % 2][:, :], kb[0:MK, g, c], qb[0:MK, hh, :], start=False, stop=True).then_inc(scored, 1)

                def weigh(b, s, first):
                    hh, t = s // TPB, s % TPB
                    if t == 0 and not (first and hh < 2):
                        pe.wait_ge(normed, HEADS * b + hh - 1)
                    pe.wait_ge(exped, STEPS * b + s + 1)
                    T.matmul(O[hh % 2][:, :], va[:, t, hh // HPG, :], prob[:, s % 2, :],
                             start=(t == 0), stop=(t == TPB - 1)).then_inc(pved, 1)

                prep_t(0)
                prep_q(0)
                prep_k(0)
                prep_v(0)
                for i in range(STEPS):
                    prep_max(0, i)
                prep_maxt(0)

                def body(b, first, last):
                    score(b, 0, first)
                    score(b, 1, first)
                    if not first:
                        close_wo(b - 1)
                    m = 0
                    for s in range(STEPS):
                        weigh(b, s, first)
                        if s + 2 < STEPS:
                            score(b, s + 2, first)
                        if not last:
                            if s == 5:
                                prep_t(b + 1)
                            if s == 6:
                                prep_q(b + 1)
                            if s == 7:
                                prep_k(b + 1)
                            if s == 8:
                                prep_v(b + 1)
                            if 8 <= s < 14:
                                for _i in range(3 if s < 12 else 2):
                                    prep_max(b + 1, m)
                                    m += 1
                        if s == 14:
                            if not last:
                                prep_maxt(b + 1)
                            if not first:
                                close_t(b - 1, b if last else b + 1)
                        if s == 15 and not first:
                            close_logits(b - 1, b + 1)
                    if not first:
                        close_prefix(b - 1)

                samples(pe, body)
                close_wo(B - 1)
                close_t(B - 1, B - 1)
                close_logits(B - 1, B - 1)
                close_prefix(B - 1)
                wait(pe, close_dve, "slot", B - 1)
                T.matmul(X[0][:, 0:E], ones[:, :], before[:, TPB, :], start=True, stop=True).then_inc(table_ready, 1)

        with ExitStack() as ffn:
            sf = lambda name, shape, dt: sb(name, shape, dt, ffn)
            ps = [ffn.enter_context(nc.psum_tensor(f"fbank{i}", [P, 512], f32)) for i in range(6)]
            HT, G, U, AT, Y = ps[0:5]
            idx_g = sf("idx_g", [P, 2], i32)
            idx_s = sf("idx_s", [P, 2], i32)
            idx_sp = [sf(f"idx_s{j}", [P, 1], i32) for j in range(2)]
            idx_gp = [sf(f"idx_g{j}", [P, 1], i32) for j in range(2)]
            hg = [sf(f"hg{j}", [P, D], f32) for j in range(2)]
            ht = [sf(f"ht{j}", [P, KD, P], f32) for j in range(2)]
            sg = sf("sg", [P, I], f32)
            a = sf("a", [P, I], f32)
            at_ = sf("a_t", [P, KI, P], f32)
            yb = [sf(f"yb{j}", [P, D], f32) for j in range(2)]
            x1f = sf("x1f", [P, NT, D], f32)
            yf = sf("yf", [P, NT, D], f32)
            gb_rows = sf("gb_rows", [P, B, D], f32)

            idxg_loaded = [sem(f"idxg_loaded{j}") for j in range(2)]
            idxs_loaded = [sem(f"idxs_loaded{j}") for j in range(2)]
            gathered = [sem(f"gathered{j}") for j in range(2)]
            scattered = [sem(f"scattered{j}") for j in range(2)]
            tr_done, gu_done, at_done, down_done = sem("tr_done"), sem("gu_done"), sem("at_done"), sem("down_done")
            gate_done = sem("gate_done")
            ht_ready, silu_done, a_ready, at_ready, y_ready = (sem("ht_ready"), sem("silu_done"), sem("a_ready"),
                                                               sem("at_ready"), sem("y_ready"))
            x1f_loaded, gb_loaded = sem("x1f_loaded"), sem("gb_loaded")
            yf_loaded = [sem(f"yf_loaded{b}") for b in range(B)]
            mul_done, add_done, add_pool = sem("mul_done"), sem("add_done"), sem("add_pool")
            out_stored = sem("out_stored")

            block = ffn.enter_context(nc.Block())

            def tiles(eng, body):
                with eng.Fori(0, TILES // 2) as q:
                    for par in range(2):
                        body(q, par, 2 * q + par)
                if TILES % 2:
                    body(TILES // 2, 0, TILES - 1)

            def w(eng, s, value):
                if not isinstance(value, int) or value > 0:
                    eng.wait_ge(s, value)

            def xrows2(ap, n):
                return ap[n * S:(n + 1) * S, :].rearrange("(t p) d -> p t d", p=P)

            @block.sync
            def _(sp):
                sp.dma_start(gb_rows[:, :, :], mod_d[:, 5 * D:6 * D].unsqueeze(0).to_broadcast([P, B, D])).then_inc(gb_loaded, 16)
                sp.dma_start(x1f[:, :, :], x1_d.rearrange("(t p) d -> p t d", p=P)).then_inc(x1f_loaded, 16)

                def body(q, par, i):
                    at0 = nc.values_load(tile_slot[0:1, ds(i, 1)], engines=[mybir.EngineType.SP], min_val=0,
                                         max_val=(E - 1) * REGION + REGION - P)
                    rows_ = slots_d[ds(at0, P), :]
                    w(sp, gathered[par], 16 * q)
                    sp.dma_start(idx_gp[par][:, :], rows_).then_inc(idxg_loaded[par], 16)
                    w(sp, scattered[par], 16 * q)
                    sp.dma_start(idx_sp[par][:, :], rows_).then_inc(idxs_loaded[par], 16)

                for i in range(TILES):
                    body(i // 2, i % 2, i)
                sp.wait_ge(scattered[0], 16 * ((TILES + 1) // 2))
                sp.wait_ge(scattered[1], 16 * (TILES // 2))
                for b in range(B):
                    sp.dma_start(yf[:, b * TPB:(b + 1) * TPB, :], xrows2(y_d, b)).then_inc(yf_loaded[b], 16)
                for b in range(B):
                    for j in range(2):
                        sp.wait_ge(add_done if j == 0 else add_pool, b + 1)
                        t = b * TPB + 2 * j
                        sp.dma_start(out.rearrange("b (t p) d -> p (b t) d", p=P)[:, t:t + 2, :], yf[:, t:t + 2, :]).then_inc(out_stored, 16)
                sp.wait_ge(out_stored, 16 * 2 * B)

            @block.gpsimd
            def _(pool):
                def gather(q, par):
                    pool.wait_ge(idxg_loaded[par], 16 * q + 16)
                    w(pool, tr_done, 2 * q + par - 1)
                    nc.gpsimd.indirect_dma_start(out=hg[par][:, :], out_offset=None, in_=h2_d,
                                                 in_offset=bass.IndirectOffsetOnAxis(ap=idx_gp[par][:, :], axis=0)).then_inc(gathered[par], 16)

                def scatter(q, par, i):
                    pool.wait_ge(idxs_loaded[par], 16 * q + 16)
                    pool.wait_ge(y_ready, i + 1)
                    w(pool, scattered[1 - par], 16 * ((i + 1) // 2))
                    nc.gpsimd.indirect_dma_start(out=y_d, out_offset=bass.IndirectOffsetOnAxis(ap=idx_sp[par][:, :], axis=0),
                                                 in_=yb[par][:, :], in_offset=None).then_inc(scattered[par], 16)

                for i in range(2):
                    gather(i // 2, i % 2)
                for i in range(TILES):
                    if i + 2 < TILES:
                        gather((i + 2) // 2, i % 2)
                    scatter(i // 2, i % 2, i)
                for b in range(B):
                    t = b * TPB + 2
                    pool.wait_ge(x1f_loaded, 16)
                    pool.wait_ge(mul_done, b + 1)
                    nc.gpsimd.tensor_tensor(yf[:, t:t + 2, :], yf[:, t:t + 2, :], x1f[:, t:t + 2, :], ALU.add).then_inc(add_pool, 1)

            @block.tensor
            def _(pe):
                T = nc.tensor

                def transpose_rows(q, par, i):
                    pe.wait_ge(gathered[par], 16 * q + 16)
                    w(pe, ht_ready, i)
                    for k in range(KD):
                        last = T.transpose(HT[:, k * P:(k + 1) * P], hg[par][:, k * P:(k + 1) * P], ident[:, :])
                    last.then_inc(tr_done, 1)

                def product(bank, wt, par, e):
                    for k in range(KD):
                        last = T.matmul(bank[:, :], ht[par][:, k, :], wt[:, ds(e, 1), k, :].rearrange("p e i -> p (e i)"),
                                        start=(k == 0), stop=(k == KD - 1))
                    return last

                def transpose_a(i):
                    pe.wait_ge(a_ready, i + 1)
                    w(pe, at_ready, i)
                    for k in range(KI):
                        last = T.transpose(AT[:, k * P:(k + 1) * P], a[:, k * P:(k + 1) * P], ident[:, :])
                    last.then_inc(at_done, 1)

                def down(i, e):
                    pe.wait_ge(at_ready, i + 1)
                    w(pe, y_ready, i)
                    for k in range(KI):
                        last = T.matmul(Y[:, 0:D], at_[:, k, :], w_down[:, ds(e, 1), k, :].rearrange("p e d -> p (e d)"),
                                        start=(k == 0), stop=(k == KI - 1))
                    last.then_inc(down_done, 1)

                for j in range(3):
                    pe.wait_ge(w_loaded[j], 16 * E)
                transpose_rows(0, 0, 0)

                def tile(q, par, i, next_):
                    e = nc.values_load(tile_expert[0:1, ds(i, 1)], engines=[mybir.EngineType.PE], min_val=0, max_val=E - 1)
                    pe.wait_ge(ht_ready, i + 1)
                    w(pe, silu_done, i)
                    product(G, w_gate, par, e).then_inc(gate_done, 1)
                    if next_ is not None:
                        transpose_rows(*next_)
                    w(pe, a_ready, i)
                    product(U, w_up, par, e).then_inc(gu_done, 1)
                    transpose_a(i)
                    down(i, e)

                with pe.Fori(0, TILES // 2) as q:
                    tile(q, 0, 2 * q, (q, 1, 2 * q + 1))
                    tile(q, 1, 2 * q + 1, (q + 1, 0, 2 * q + 2))
                tile(TILES // 2, 0, TILES - 1, None)

            @block.scalar
            def _(act):
                A = nc.scalar.activation

                def tile(q, par, i):
                    act.wait_ge(gate_done, i + 1)
                    w(act, a_ready, i)
                    A(sg[:, :], G[:, :], ACT.Silu).then_inc(silu_done, 1)
                    act.wait_ge(at_done, i + 1)
                    w(act, down_done, i)
                    A(at_[:, :, :].rearrange("p k c -> p (k c)"), AT[:, :], ACT.Copy).then_inc(at_ready, 1)

                tiles(act, tile)

            @block.vector
            def _(dve):
                V = nc.vector

                def copy_ht(q, par, i):
                    dve.wait_ge(tr_done, i + 1)
                    w(dve, gu_done, i - 1)
                    V.tensor_copy(ht[par][:, :, :].rearrange("p k c -> p (k c)"), HT[:, 0:KD * P]).then_inc(ht_ready, 1)

                def tile(q, par, i, next_):
                    if next_ is not None:
                        copy_ht(*next_)
                    dve.wait_ge(gu_done, i + 1)
                    dve.wait_ge(silu_done, i + 1)
                    w(dve, at_done, i)
                    V.tensor_tensor(a[:, :], sg[:, :], U[:, :], ALU.mult).then_inc(a_ready, 1)
                    dve.wait_ge(down_done, i + 1)
                    dve.wait_ge(scattered[par], 16 * q)
                    V.tensor_copy(yb[par][:, :], Y[:, 0:D]).then_inc(y_ready, 1)

                dve.wait_ge(tr_done, 1)
                V.tensor_copy(ht[0][:, :, :].rearrange("p k c -> p (k c)"), HT[:, 0:KD * P]).then_inc(ht_ready, 1)
                with dve.Fori(0, TILES // 2) as q:
                    tile(q, 0, 2 * q, (q, 1, 2 * q + 1))
                    tile(q, 1, 2 * q + 1, (q + 1, 0, 2 * q + 2))
                tile(TILES // 2, 0, TILES - 1, None)
                dve.wait_ge(gb_loaded, 16)
                dve.wait_ge(x1f_loaded, 16)
                for b in range(B):
                    t = b * TPB
                    dve.wait_ge(yf_loaded[b], 16)
                    V.tensor_tensor(yf[:, t:t + TPB, :], yf[:, t:t + TPB, :],
                                    gb_rows[:, b, :].unsqueeze(1).to_broadcast([P, TPB, D]), ALU.mult).then_inc(mul_done, 1)
                    dve.wait_ge(mul_done, b + 1)
                    V.tensor_tensor(yf[:, t:t + 2, :], yf[:, t:t + 2, :], x1f[:, t:t + 2, :], ALU.add).then_inc(add_done, 1)


_INS = ["L0_attn_x", "L0_attn_norm_scale", "L0_attn_split_scale", "L0_attn_Wq", "L0_attn_Wk", "L0_attn_Wv",
        "L0_attn_Wo", "L0_ffn_router_w", "L0_ffn_gate_w", "L0_ffn_up_w", "L0_ffn_down_w", "L0_c", "L0_wmod"]


def kernel(**inputs):
    import numpy as np
    import concourse.bacc as bacc
    from concourse import mybir
    from concourse.bass_utils import run_bass_kernel_spmd

    nc = bacc.Bacc("TRN2", target_bir_lowering=False, num_devices=1)
    arrays, io = {}, {}
    for name in _INS:
        arr = np.ascontiguousarray(inputs[name])
        arrays[name + "_dram"] = arr
        io[name] = nc.dram_tensor(name + "_dram", arr.shape, mybir.dt.from_np(arr.dtype), kind="ExternalInput").ap()
    shape = inputs["L0_attn_x"].shape
    io["out"] = nc.dram_tensor("out_dram", shape, mybir.dt.float32, kind="ExternalOutput").ap()
    build(nc, io)
    r = run_bass_kernel_spmd(nc, [arrays], core_ids=[0])
    return r.results[0]["out_dram"]
```

```python
def build(nc, io):
    import concourse.bass as bass
    import concourse.mybir as mybir
    from contextlib import ExitStack

    f32, f32r, bf16, i32 = (mybir.dt.float32, mybir.dt.float32r, mybir.dt.bfloat16,
                            mybir.dt.int32)
    ALU = mybir.AluOpType
    ACT = mybir.ActivationFunctionType
    AX = mybir.AxisListType
    ds = bass.ds

    x_in, out = io["L0_attn_x"], io["out"]
    P = 128
    B, S, D = x_in.shape
    HEADS, GROUPS, DH = 4, 2, 64
    HPG = HEADS // GROUPS
    E, _, I = io["L0_ffn_gate_w"].shape
    KD = D // P
    KI = I // P
    TPB = S // P
    N = B * S
    NT = N // P
    TILES = NT + E - 1
    REGION = N + P
    LN_EPS, RMS_EPS = 1e-5, 1e-8
    SCALE = 1.0 / float(DH) ** 0.5
    STEPS = HEADS * TPB
    MK = DH + TPB

    def dram(name, shape, dt):
        return nc.dram_tensor(name, shape, dt, kind="Internal").ap()

    mod_d = dram("mod_d", (B, 6 * D), f32)
    xh_d = dram("xh_d", (N, D), f32)
    x1_d = dram("x1_d", (N, D), f32)
    h2_d = dram("h2_d", (N + P, D), f32)
    slots_d = dram("slots_d", (E * REGION, 1), i32)
    y_d = dram("y_d", (N + P, D), f32)

    top = ExitStack()
    sem = lambda name: top.enter_context(nc.semaphore(name))

    class Stage:
        def __init__(self, name, steps):
            self.sem, self.steps = sem(name), steps
        def after(self, step, n):
            return n * len(self.steps) + self.steps.index(step) + 1

    def names(base, n):
        return [f"{base}{i}" for i in range(n)]

    with top:
        sb = lambda name, shape, dt, c=top: c.enter_context(nc.sbuf_tensor(name, shape, dt))
        w_gate = sb("w_gate", [P, E, KD, I], f32)
        w_up = sb("w_up", [P, E, KD, I], f32)
        w_down = sb("w_down", [P, E, KI, D], f32)
        ident = sb("ident", [P, P], f32)
        tile_expert = sb("tile_expert", [1, TILES + 1], i32)
        tile_slot = sb("tile_slot", [1, TILES + 1], i32)

        w_loaded = [sem(f"w_loaded{j}") for j in range(3)]

        with ExitStack() as att:
            sa_ = lambda name, shape, dt: sb(name, shape, dt, att)
            ps = [att.enter_context(nc.psum_tensor(f"bank{i}", [P, 512], f32)) for i in range(8)]
            ST, O, X = ps[0:2], ps[2:4], ps[4:8]

            late = lambda e: w_down[:, e, :, :]
            x, h, rows = late(E - 1), late(E - 2), late(E - 3)
            x1 = sa_("x1", [P, TPB, D], f32)
            crow = sa_("crow", [P, TPB, D], f32)
            mod_a = sa_("mod_a", [P, 3, D], f32)
            mod_c = sa_("mod_c", [P, 3, D], f32)
            t_hi = sa_("t_hi", [P, KD, S], f32r)
            t_lo = sa_("t_lo", [P, KD, S], f32r)
            t_c = sa_("t_c", [P, KD, S], f32)
            pair = lambda name, shape, dt: [sa_(f"{name}{j}", shape, dt) for j in range(2)]
            qa = pair("qa", [P, HEADS, S], f32r)
            qb = pair("qb", [P, HEADS, S], f32r)
            ka = pair("ka", [P, GROUPS, S], f32r)
            kb = pair("kb", [P, GROUPS, S], f32r)
            va = pair("va", [P, TPB, GROUPS, DH + 1], f32)
            k_hi = sa_("k_hi", [P, S], f32r)
            prob = sa_("prob", [P, 2, S], f32)
            inv = sa_("inv", [P, TPB], f32)
            o_row = sa_("o_row", [P, TPB, P], f32)
            o_t = sa_("o_t", [P, HEADS // 2, S], f32)
            spare = w_up[:, :, :, :].rearrange("p e k d -> p (e k d)")
            at = [0]
            def temp(parts, n):
                at[0] += n
                return spare[0:parts, at[0] - n:at[0]]
            wmod = temp(P, KD * 6 * D).rearrange("p (k n) -> p k n", k=KD)
            wq_raw = temp(P, 2 * D).rearrange("p (o d) -> p o d", d=D)
            wk_raw, wv_raw = temp(P, D), temp(P, D)
            wo_raw = temp(P, 2 * D).rearrange("p (o d) -> p o d", d=D)
            mod_row = temp(B, 6 * D)
            c4, sc4 = temp(B, D), temp(B, D)
            gate_raw, gate_abs, gate_sign = (temp(B, 2 * D).rearrange("p (r d) -> p r d", d=D) for _ in range(3))
            w_hi = sa_("w_hi", [P, KD, 2 * D], f32r)
            w_lo = sa_("w_lo", [P, KD, 2 * D], f32r)
            wo_t = sa_("wo_t", [P, KD, D], f32)
            wo_g = sa_("wo_g", [P, KD, D], f32)
            wr = sa_("wr", [P, KD, E], f32)
            mask = sa_("mask", [TPB, TPB, P], f32)
            upper = sa_("upper", [P, P], bf16)
            ones = sa_("ones", [P, P], bf16)
            rev8 = sa_("rev8", [P, TPB, E], f32)
            rev8i = sa_("rev8i", [P, TPB, E], i32)
            mhalf = sa_("mhalf", [P, TPB], f32)
            half = sa_("half", [P, TPB], f32)
            mone = sa_("mone", [P, TPB], f32)
            nsc = sa_("nsc", [P, KD], f32)
            ssc = sa_("ssc", [P, KD], f32)
            nss = sa_("nss", [P, KD], f32)
            stats = sa_("stats", [P, TPB, 6], f32)
            mv = sa_("mv", [P, TPB, 2], f32)
            var = sa_("var", [P, TPB], f32)
            rstd = sa_("rstd", [P, TPB], f32)
            nmean = sa_("nmean", [P, TPB], f32)
            nmr = sa_("nmr", [P, TPB], f32)
            ssq = sa_("ssq", [P, TPB], f32)
            nrm = sa_("nrm", [P, TPB], f32)
            nrme = sa_("nrme", [P, TPB], f32)
            rinv = sa_("rinv", [P, TPB], f32)
            stats2 = sa_("stats2", [P, TPB, 6], f32)
            mv2 = sa_("mv2", [P, TPB, 2], f32)
            var2 = sa_("var2", [P, TPB], f32)
            rstd2 = sa_("rstd2", [P, TPB], f32)
            nmean2 = sa_("nmean2", [P, TPB], f32)
            nmr2 = sa_("nmr2", [P, TPB], f32)
            neg_max = sa_("neg_max", [P, HEADS * TPB], f32)
            lmax = sa_("lmax", [P, TPB], f32)
            leq = sa_("leq", [P, TPB, E], f32)
            lw = sa_("lw", [P, TPB, E], f32)
            erev = sa_("erev", [P, TPB], f32)
            onehot = sa_("onehot", [P, TPB, E], bf16)
            before = sa_("before", [P, TPB + 1, E], bf16)
            prank = sa_("prank", [P, TPB, E], f32)
            rank = sa_("rank", [P, TPB], f32)
            slot_f = sa_("slot_f", [P, TPB], f32)
            slot = sa_("slot", [P, TPB], i32)
            token = sa_("token", [P, NT], i32)
            fill_a = sa_("fill_a", [P, E * REGION // P], i32)
            fill = sa_("fill", [P, E * REGION // P], i32)
            counts = sa_("counts", [1, E], i32)
            ntile_i = sa_("ntile_i", [1, E], i32)
            ntile = sa_("ntile", [1, E], f32)
            pre = [sa_(f"pre{j}", [1, E], f32) for j in range(3)]
            tidx = sa_("tidx", [1, TILES + 1, E - 1], i32)
            passed = sa_("passed", [1, TILES + 1, E - 1], f32)
            passed_n = sa_("passed_n", [1, TILES + 1, E - 1], f32)
            te_f = sa_("te_f", [1, TILES + 1], f32)
            base_f = sa_("base_f", [1, TILES + 1], f32)
            j_f = sa_("j_f", [1, TILES + 1], f32)
            ts_f = sa_("ts_f", [1, TILES + 1], f32)
            sc_t = sa_("sc_t", [P, KD, B], f32)

            c_loaded, wmod_loaded, raw_loaded, small_loaded = (sem("c_loaded"), sem("wmod_loaded"),
                                                               sem("raw_loaded"), sem("small_loaded"))
            mod_stored, zeros_stored = sem("mod_stored"), sem("zeros_stored")
            x_loaded, moda_loaded, modc_loaded, x1_loaded = (sem("x_loaded"), sem("moda_loaded"),
                                                             sem("modc_loaded"), sem("x1_loaded"))
            xh_stored, x1_stored, h2_stored = sem("xh_stored"), sem("x1_stored"), sem("h2_stored")
            slots_filled, slots_written = sem("slots_filled"), sem("slots_written")
            scored, exped, pved = sem("scored"), sem("exped"), sem("pved")
            inverted, normed = sem("inverted"), sem("normed")
            o_turned, o_live = sem("o_turned"), sem("o_live")
            table_ready = sem("table_ready")
            counted = sem("counted")

            row_dve = Stage("row_dve", names("st", TPB) + names("ag", TPB))
            row_act = Stage("row_act", names("xn", TPB) + names("sq", TPB) + names("hn", TPB))
            row_pool = Stage("row_pool", ["var", "rstd", "nmean", "nmr", "nrm", "nrme", "rinv", "gated", "xh"])
            row_mod = Stage("row_mod", ["scaled", "h"])
            in_order = (["t0", "t1", "q0", "k", "max0", "max1", "q1", "max2", "max3", "v", "max4", "max5", "maxt0"]
                        + ["max6", "max7", "max8", "max9", "maxt1", "max10", "max11", "max12", "max13", "maxt2",
                           "max14", "max15", "maxt3"])
            before_attention = in_order.index("maxt0") + 1
            left = [(0, step) for step in in_order[before_attention:]]

            def deal(steps_, counts_):
                assert sum(counts_) == len(steps_)
                at_ = [sum(counts_[:s_]) for s_ in range(STEPS + 1)]
                return [steps_[at_[s_]:at_[s_ + 1]] for s_ in range(STEPS)]
            usual = [2, 1, 0, 1, 0, 3, 2, 2, 3, 2, 3, 2, 3, 2, 0, 0]
            PREP = [deal(left + [(1, step) for step in in_order],
                         [2, 3, 2, 3, 2, 3, 1, 3, 3, 4, 3, 3, 3, 2, 1, 1])]
            PREP += [deal([(b + 1, step) for step in in_order], usual) for b in range(1, B - 1)]
            PREP += [[[] for _ in range(STEPS)]]
            prep_pe = Stage("prep_pe", in_order)
            prep_act = Stage("prep_act", ["t0", "t1", "q0", "q0_again", "q1", "q1_again", "ka0", "kb0", "ka1", "kb1", "k_hi",
                                          "q2", "q2_again", "q3", "q3_again", "v"])
            parts = {"q0": ["q0", "q1"], "q1": ["q2", "q3"], "k": ["k0", "k1"], "v": []}
            prep_dve = Stage("prep_dve", [part for step in in_order for part in parts.get(step, [step])])
            close_pe = Stage("close_pe", ["wo0", "wo1", "t0", "t1", "logits", "prefix"])
            close_act = Stage("close_act", names("xn", TPB) + names("t", 2))
            close_dve = Stage("close_dve", ["x1_0", "x1_1"] + names("st", TPB) + names("ag", TPB)
                              + ["lmax", "leq", "lw", "erev", "onehot", "carry"]
                              + names("add", TPB) + ["prank", "rank", "slot_f", "slot"])
            close_pool = Stage("close_pool", ["wo_g", "var", "rstd", "nmean", "nmr"])
            close_mod = Stage("close_mod", ["scaled", "h2"])

            setup_pe = Stage("setup_pe", ["sc", "mod0", "mod", "w"])
            setup_act = Stage("setup_act", ["silu"] + names("w", KD) + ["wo"])
            setup_dve = Stage("setup_dve", ["kb0", "kb1", "fill", "rev8", "nss", "sc", "sa0", "ca0", "sa", "ca", "sb", "cb",
                                            "ga_raw", "gb_raw", "abs", "sign", "pm", "max", "ga", "gb"]
                              + names("w", KD))
            setup_pool = Stage("setup_pool", names("memset", 11) + ["ident", "upper", "mask",
                                                                    "rev8", "token", "tidx", "fill_iota", "fill"])

            def over_tiles(row):
                return row.unsqueeze(1).to_broadcast([P, TPB, D])

            def w(eng, s, value):
                if not isinstance(value, int) or value > 0:
                    eng.wait_ge(s, value)

            def wait(eng, stage, step, n):
                if n >= 0:
                    w(eng, stage.sem, stage.after(step, n))

            block = att.enter_context(nc.Block())

            def xrows(ap, n):
                return ap[n * S:(n + 1) * S, :].rearrange("(t p) d -> p t d", p=P)

            x_rows = x_in.rearrange("b s d -> (b s) d")

            def load_weights(eng, j, e):
                dst, src, pat = ((w_gate, "L0_ffn_gate_w", "(k p) i -> p k i"), (w_up, "L0_ffn_up_w", "(k p) i -> p k i"),
                                 (w_down, "L0_ffn_down_w", "(k p) d -> p k d"))[j]
                eng.dma_start(dst[:, e, :, :], io[src][e, :, :].rearrange(pat, p=P)).then_inc(w_loaded[j], 16)

            @block.sync
            def _(sp):
                sp.dma_start(c4, io["L0_c"]).then_inc(c_loaded, 16)
                sp.dma_start(wmod, io["L0_wmod"].rearrange("(k p) n -> p k n", p=P)).then_inc(wmod_loaded, 16)
                sp.dma_start(x[:, :, :], xrows(x_rows, 0)).then_inc(x_loaded, 16)
                sp.dma_start(wk_raw, io["L0_attn_Wk"]).then_inc(raw_loaded, 16)
                sp.dma_start(wv_raw, io["L0_attn_Wv"]).then_inc(raw_loaded, 16)
                sp.dma_start(wo_raw, io["L0_attn_Wo"].rearrange("(o p) d -> p o d", p=P)).then_inc(raw_loaded, 16)
                for e in range(2):
                    load_weights(sp, 0, e)
                sp.wait_ge(setup_dve.sem, setup_dve.after("gb", 0))
                sp.dma_start(mod_d, mod_row).then_inc(mod_stored, 16)
                sp.wait_ge(setup_pool.sem, setup_pool.after("fill", 0))
                sp.dma_start(slots_d.rearrange("(p j) o -> p (j o)", p=P), fill[:, :]).then_inc(slots_filled, 16)
                sp.dma_start(h2_d[N:N + P, :], crow[:, 0, :]).then_inc(zeros_stored, 16)

                def load_row(p):
                    r = 2 if p == 0 else 0
                    wait(sp, row_pool, "xh", p - 1)
                    if p == 0:
                        sp.wait_ge(mod_stored, 16)
                    sp.dma_start(mod_a[:, r:3, :].rearrange("p r d -> p (r d)"),
                                 mod_d[p:p + 1, r * D:3 * D].partition_broadcast(P)).then_inc(moda_loaded, 16)
                    if p > 0:
                        sp.wait_ge(xh_stored, 16 * p)
                        sp.dma_start(x[:, :, :], xrows(x_rows, p)).then_inc(x_loaded, 16)

                def store_xh(p):
                    wait(sp, row_pool, "xh", p)
                    sp.dma_start(xrows(xh_d, p), x[:, :, :]).then_inc(xh_stored, 16)

                def load_x1(c):
                    sp.wait_ge(xh_stored, 16 * c + 16)
                    w(sp, x1_stored, 16 * c)
                    sp.dma_start(x1[:, :, :], xrows(xh_d, c)).then_inc(x1_loaded, 16)

                def store_x1(c):
                    wait(sp, close_dve, "x1_1", c)
                    sp.dma_start(xrows(x1_d, c), x1[:, :, :]).then_inc(x1_stored, 16)

                def store_h2(c):
                    wait(sp, close_mod, "h2", c)
                    sp.dma_start(xrows(h2_d, c), crow[:, :, :]).then_inc(h2_stored, 16)

                def load_modc(b):
                    wait(sp, close_mod, "h2", b - 1)
                    sp.dma_start(mod_c[:, :, :].rearrange("p r d -> p (r d)"),
                                 mod_d[b:b + 1, 2 * D:5 * D].partition_broadcast(P)).then_inc(modc_loaded, 16)

                load_row(0)
                for e in range(2, 4):
                    load_weights(sp, 0, e)
                store_xh(0)
                load_row(1)
                load_modc(0)
                load_x1(0)
                for e in range(4, 8):
                    load_weights(sp, 0, e)
                sp.wait_ge(setup_pe.sem, setup_pe.after("w", 0))
                sp.wait_ge(setup_dve.sem, setup_dve.after("gb", 0))
                for e in range(2):
                    load_weights(sp, 1, e)
                store_xh(1)

                batches = [[(1, e) for e in range(2, 8)], [(2, e) for e in range(E - 3)], [], []]
                for b in range(B):
                    if b + 2 < B:
                        load_row(b + 2)
                    if b > 1:
                        load_x1(b - 1)
                    if b + 2 == B:
                        sp.wait_ge(xh_stored, 16 * B)
                        load_weights(sp, 2, E - 1)
                        load_weights(sp, 2, E - 2)
                        wait(sp, prep_pe, "t1", B - 1)
                        load_weights(sp, 2, E - 3)
                    for j, e in batches[b]:
                        load_weights(sp, j, e)
                    if b > 0:
                        store_x1(b - 1)
                        store_h2(b - 1)
                        load_modc(b)
                    if b + 2 < B:
                        store_xh(b + 2)
                load_x1(B - 1)
                store_x1(B - 1)
                store_h2(B - 1)
                sp.wait_ge(x1_stored, 16 * B)
                sp.wait_ge(h2_stored, 16 * B)
                sp.wait_ge(zeros_stored, 16)

            @block.gpsimd
            def _(pool):
                nc_ = nc.gpsimd
                nc_.memset(ident[:, :], 0.0).then_inc(setup_pool.sem, 1)
                nc_.memset(mask[:, :, :], 0.0).then_inc(setup_pool.sem, 1)
                nc_.memset(upper[:, :], 1.0).then_inc(setup_pool.sem, 1)
                nc_.memset(mhalf[:, :], -0.5).then_inc(setup_pool.sem, 1)
                nc_.memset(half[:, :], 0.5).then_inc(setup_pool.sem, 1)
                nc_.memset(mone[:, :], -1.0).then_inc(setup_pool.sem, 1)
                pool.wait_ge(setup_pool.sem, 3)
                nc_.memset(ones[:, :], 1.0).then_inc(setup_pool.sem, 1)
                nc_.memset(crow[:, 0, :], 0.0).then_inc(setup_pool.sem, 1)
                nc_.memset(va[0][:, :, :, DH:DH + 1], 1.0).then_inc(setup_pool.sem, 1)
                nc_.memset(va[1][:, :, :, DH:DH + 1], 1.0).then_inc(setup_pool.sem, 1)
                nc_.memset(before[:, TPB, :], 0.0).then_inc(setup_pool.sem, 1)
                nc_.affine_select(out=ident[:, :], in_=ident[:, :], compare_op=ALU.not_equal, fill=1.0, base=0,
                                  pattern=[[-1, P]], channel_multiplier=1).then_inc(setup_pool.sem, 1)
                nc_.affine_select(out=upper[:, :], in_=upper[:, :], compare_op=ALU.is_gt, fill=0.0, base=0,
                                  pattern=[[1, P]], channel_multiplier=-1).then_inc(setup_pool.sem, 1)
                nc_.affine_select(out=mask[:, :, :], in_=mask[:, :, :], compare_op=ALU.not_equal, fill=1.0,
                                  base=0, pattern=[[1, TPB], [0, P]], channel_multiplier=-1).then_inc(setup_pool.sem, 1)
                nc_.iota(rev8i[:, :, :], pattern=[[0, TPB], [-1, E]], base=E, channel_multiplier=0).then_inc(setup_pool.sem, 1)
                nc_.iota(token[:, :], pattern=[[P, NT]], base=0, channel_multiplier=1).then_inc(setup_pool.sem, 1)
                nc_.iota(tidx[:, :, :], pattern=[[1, TILES + 1], [0, E - 1]], base=0, channel_multiplier=0).then_inc(setup_pool.sem, 1)
                nc_.iota(fill_a[:, :], pattern=[[1, E * REGION // P]], base=0,
                         channel_multiplier=E * REGION // P).then_inc(setup_pool.sem, 1)
                pool.wait_ge(setup_dve.sem, setup_dve.after("fill", 0))
                nc_.tensor_copy(fill[:, :], fill_a[:, :]).then_inc(setup_pool.sem, 1)

                def row_stats(p):
                    wait(pool, row_dve, "ag3", p)
                    nc_.tensor_scalar(var[:, :], mv[:, :, 1], LN_EPS, None, ALU.add).then_inc(row_pool.sem, 1)
                    wait(pool, row_pool, "var", p)
                    nc_.tensor_tensor(rstd[:, :], var[:, :], mhalf[:, :], ALU.pow).then_inc(row_pool.sem, 1)
                    nc_.tensor_tensor(nmean[:, :], mv[:, :, 0], mone[:, :], ALU.mult).then_inc(row_pool.sem, 1)
                    wait(pool, row_pool, "nmean", p)
                    nc_.tensor_tensor(nmr[:, :], nmean[:, :], rstd[:, :], ALU.mult).then_inc(row_pool.sem, 1)

                def row_h(p):
                    wait(pool, row_act, "xn3", p)
                    pool.wait_ge(moda_loaded, 16 * p + 16)
                    nc_.tensor_tensor(h[:, :, :], h[:, :, :], over_tiles(mod_a[:, 1, :]), ALU.mult).then_inc(row_mod.sem, 1)
                    wait(pool, row_mod, "scaled", p)
                    nc_.tensor_tensor(h[:, :, :], h[:, :, :], over_tiles(mod_a[:, 0, :]), ALU.add).then_inc(row_mod.sem, 1)

                def row_rms(p):
                    wait(pool, row_act, "sq3", p)
                    nc_.tensor_tensor(nrm[:, :], ssq[:, :], half[:, :], ALU.pow).then_inc(row_pool.sem, 1)
                    wait(pool, row_pool, "nrm", p)
                    nc_.tensor_scalar(nrme[:, :], nrm[:, :], float(D) ** -0.5, RMS_EPS, ALU.mult, ALU.add).then_inc(row_pool.sem, 1)
                    wait(pool, row_pool, "nrme", p)
                    nc_.tensor_tensor(rinv[:, :], nrme[:, :], mone[:, :], ALU.pow).then_inc(row_pool.sem, 1)

                def row_xh(p):
                    wait(pool, row_act, "hn3", p)
                    pool.wait_ge(moda_loaded, 16 * p + 16)
                    nc_.tensor_tensor(h[:, :, :], h[:, :, :], over_tiles(mod_a[:, 2, :]), ALU.mult).then_inc(row_pool.sem, 1)
                    wait(pool, row_pool, "gated", p)
                    nc_.tensor_tensor(x[:, :, :], x[:, :, :], h[:, :, :], ALU.add).then_inc(row_pool.sem, 1)

                def close_gate(c):
                    pool.wait_ge(modc_loaded, 16 * c + 16)
                    if c == 0:
                        pool.wait_ge(setup_act.sem, setup_act.after("wo", 0))
                    wait(pool, close_pe, "wo1", c - 1)
                    nc_.tensor_tensor(wo_g[:, :, :], wo_t[:, :, :],
                                      mod_c[:, 0, :].unsqueeze(1).to_broadcast([P, KD, D]), ALU.mult).then_inc(close_pool.sem, 1)

                def close_stats(c):
                    wait(pool, close_dve, "ag3", c)
                    nc_.tensor_scalar(var2[:, :], mv2[:, :, 1], LN_EPS, None, ALU.add).then_inc(close_pool.sem, 1)
                    wait(pool, close_pool, "var", c)
                    nc_.tensor_tensor(rstd2[:, :], var2[:, :], mhalf[:, :], ALU.pow).then_inc(close_pool.sem, 1)
                    nc_.tensor_tensor(nmean2[:, :], mv2[:, :, 0], mone[:, :], ALU.mult).then_inc(close_pool.sem, 1)
                    wait(pool, close_pool, "nmean", c)
                    nc_.tensor_tensor(nmr2[:, :], nmean2[:, :], rstd2[:, :], ALU.mult).then_inc(close_pool.sem, 1)

                def close_h2(c):
                    wait(pool, close_act, "xn3", c)
                    nc_.tensor_tensor(crow[:, :, :], crow[:, :, :], over_tiles(mod_c[:, 2, :]), ALU.mult).then_inc(close_mod.sem, 1)
                    wait(pool, close_mod, "scaled", c)
                    nc_.tensor_tensor(crow[:, :, :], crow[:, :, :], over_tiles(mod_c[:, 1, :]), ALU.add).then_inc(close_mod.sem, 1)

                def close_slots(c):
                    wait(pool, close_dve, "slot", c)
                    if c == 0:
                        pool.wait_ge(slots_filled, 16)
                    for t in range(TPB):
                        nc_.indirect_dma_start(out=slots_d, out_offset=bass.IndirectOffsetOnAxis(ap=slot[:, t:t + 1], axis=0),
                                               in_=token[:, c * TPB + t:c * TPB + t + 1], in_offset=None).then_inc(slots_written, 16)

                row_stats(0)
                row_rms(0)
                row_xh(0)
                row_stats(1)
                row_h(1)
                row_rms(1)
                row_xh(1)
                for b in range(B):
                    if b > 0:
                        close_stats(b - 1)
                    if b + 2 < B:
                        row_stats(b + 2)
                    if b > 0:
                        close_h2(b - 1)
                    if b + 2 < B:
                        row_h(b + 2)
                        row_rms(b + 2)
                        row_xh(b + 2)
                    close_gate(b)
                    if b > 0:
                        close_slots(b - 1)
                close_stats(B - 1)
                close_slots(B - 1)
                pool.wait_ge(slots_written, 16 * TPB * B)

            @block.scalar
            def _(act):
                A = nc.scalar.activation
                act.dma_start(wq_raw, io["L0_attn_Wq"].rearrange("(o p) d -> p o d", p=P)).then_inc(raw_loaded, 16)
                act.dma_start(nsc[:, :], io["L0_attn_norm_scale"].rearrange("(k p) -> p k", p=P), allow_slow_non_contiguous=True).then_inc(small_loaded, 16)
                act.dma_start(ssc[:, :], io["L0_attn_split_scale"].rearrange("(k p) -> p k", p=P), allow_slow_non_contiguous=True).then_inc(small_loaded, 16)
                act.dma_start(wr[:, :, :], io["L0_ffn_router_w"].rearrange("(k p) e -> p k e", p=P)).then_inc(small_loaded, 16)
                act.wait_ge(c_loaded, 16)
                A(sc4, c4, ACT.Silu).then_inc(setup_act.sem, 1)

                def row_norm(p):
                    act.wait_ge(x_loaded, 16 * p + 16)
                    wait(act, row_pool, "nmr", p)
                    wait(act, row_pool, "xh", p - 1)
                    for t in range(TPB):
                        A(h[:, t, :], x[:, t, :], ACT.Identity, bias=nmr[:, t:t + 1], scale=rstd[:, t:t + 1]).then_inc(row_act.sem, 1)

                def row_square(p):
                    wait(act, row_mod, "h", p)
                    wait(act, prep_pe, "t1", p - 1)
                    for t in range(TPB):
                        A(rows[:, t, :], h[:, t, :], ACT.Square, accum_out=ssq[:, t:t + 1]).then_inc(row_act.sem, 1)

                def row_scale(p):
                    wait(act, row_pool, "rinv", p)
                    for t in range(TPB):
                        A(rows[:, t, :], h[:, t, :], ACT.Copy, scale=rinv[:, t:t + 1]).then_inc(row_act.sem, 1)

                def prep_t(p):
                    for k in range(KD):
                        wait(act, prep_pe, f"t{k}", p)
                        A(t_hi[:, k, :], X[k][:, :], ACT.Copy).then_inc(prep_act.sem, 1)

                def prep_q(p, g):
                    wait(act, prep_pe, f"q{g}", p)
                    if g == 0:
                        w(act, scored, STEPS * (p - 1))
                    for i in range(HPG):
                        for r in (0, DH):
                            A(qa[p % 2][r:r + DH, HPG * g + i, :], X[0][i * DH:(i + 1) * DH, :], ACT.Copy).then_inc(prep_act.sem, 1)

                def prep_k(p):
                    wait(act, prep_pe, "k", p)
                    for g in range(GROUPS):
                        for dst in (ka, kb):
                            A(dst[p % 2][0:DH, g, :], X[1][g * DH:(g + 1) * DH, :], ACT.Copy).then_inc(prep_act.sem, 1)
                    wait(act, prep_dve, "k1", p - 1)
                    A(k_hi[DH:P, :], X[1][DH:P, :], ACT.Copy).then_inc(prep_act.sem, 1)

                def prep_v(p):
                    wait(act, prep_pe, "v", p)
                    w(act, pved, STEPS * (p - 1))
                    A(va[p % 2][:, :, :, 0:DH], X[1][:, :].rearrange("p (t g c) -> p t g c", t=TPB, g=GROUPS),
                      ACT.Copy).then_inc(prep_act.sem, 1)

                def evacuate_o(n, j):
                    act.wait_ge(o_turned, 2 * n + j + 1)
                    wait(act, close_pe, "wo1", n - 1)
                    A(o_t[:, j, :], O[1][:, :], ACT.Copy).then_inc(o_live, 1)

                def close_norm(c):
                    wait(act, close_pool, "nmr", c)
                    w(act, h2_stored, 16 * c)
                    if c == 0:
                        act.wait_ge(zeros_stored, 16)
                    wait(act, close_pe, "t1", c - 1)
                    for t in range(TPB):
                        A(crow[:, t, :], x1[:, t, :], ACT.Identity, bias=nmr2[:, t:t + 1], scale=rstd2[:, t:t + 1]).then_inc(close_act.sem, 1)

                def close_t(c):
                    for k in range(KD):
                        wait(act, close_pe, f"t{k}", c)
                        A(t_c[:, k, :], X[k][:, :], ACT.Copy).then_inc(close_act.sem, 1)

                row_norm(0)
                act.wait_ge(setup_dve.sem, setup_dve.after("nss", 0))
                act.wait_ge(setup_pe.sem, setup_pe.after("w", 0))
                for k in range(KD):
                    A(w_hi[:, k, :], O[k][:, :], ACT.Copy, scale=nss[:, k:k + 1]).then_inc(setup_act.sem, 1)
                A(wo_t[:, :, :].rearrange("p k d -> p (k d)"), ST[0][:, :], ACT.Copy).then_inc(setup_act.sem, 1)
                row_square(0)
                row_scale(0)
                prep_t(0)
                prep_q(0, 0)
                prep_k(0)
                prep_q(0, 1)
                row_norm(1)
                prep_v(0)
                row_square(1)
                row_scale(1)

                act_prep = {"t0": lambda p: prep_t(p), "q0": lambda p: prep_q(p, 0), "k": prep_k,
                            "q1": lambda p: prep_q(p, 1), "v": prep_v}

                def beside(b, s):
                    close, row = b > 0, b + 2 < B
                    if s == 1 and close:
                        evacuate_o(b - 1, 1)
                    for p, step in PREP[b][s]:
                        if step in act_prep:
                            act_prep[step](p)
                    if s == 8 and close:
                        close_norm(b - 1)
                    if s == 9:
                        evacuate_o(b, 0)
                    if s == 9 and row:
                        row_norm(b + 2)
                    if s == 13 and close:
                        close_t(b - 1)
                    if s == 13 and row:
                        row_square(b + 2)
                    if s == 15 and row:
                        row_scale(b + 2)

                for b in range(B):
                    for s in range(STEPS):
                        act.wait_ge(scored, STEPS * b + s + 1)
                        w(act, pved, STEPS * b + s - 1)
                        A(prob[:, s % 2, :], ST[s % 2][:, :], ACT.Exp, scale=SCALE).then_inc(exped, 1)
                        if s > 0:
                            beside(b, s - 1)
                    beside(b, STEPS - 1)
                evacuate_o(B - 1, 1)
                close_norm(B - 1)
                close_t(B - 1)

            @block.vector
            def _(dve):
                V = nc.vector
                for j in range(2):
                    V.memset(kb[j][DH:MK, :, :].bitcast(f32), 1.0).then_inc(setup_dve.sem, 1)
                dve.wait_ge(setup_pool.sem, setup_pool.after("fill_iota", 0))
                V.tensor_scalar(fill_a[:, :], fill_a[:, :], P - 1, N, ALU.bitwise_and, ALU.bitwise_or).then_inc(setup_dve.sem, 1)
                V.tensor_copy(rev8[:, :, :], rev8i[:, :, :]).then_inc(setup_dve.sem, 1)
                dve.wait_ge(small_loaded, 48)
                V.tensor_tensor(nss[:, :], nsc[:, :], ssc[:, :], ALU.mult).then_inc(setup_dve.sem, 1)
                dve.wait_ge(setup_pe.sem, setup_pe.after("sc", 0))
                V.tensor_copy(sc_t[:, :, :], X[0][:, 0:2 * B].rearrange("p (k b) -> p k b", k=KD)).then_inc(setup_dve.sem, 1)

                def row_stats(p):
                    dve.wait_ge(x_loaded, 16 * p + 16)
                    for t in range(TPB):
                        V.bn_stats(stats[:, t, :], x[:, t, :]).then_inc(row_dve.sem, 1)
                    wait(dve, row_dve, "st3", p)
                    wait(dve, row_pool, "nmr", p - 1)
                    for t in range(TPB):
                        V.bn_aggr(mv[:, t, :], stats[:, t, :]).then_inc(row_dve.sem, 1)

                row_stats(0)
                dve.wait_ge(setup_pe.sem, setup_pe.after("mod0", 0))
                V.tensor_copy(mod_a[:, 0, :], ST[1][:, 0:D]).then_inc(setup_dve.sem, 1)
                V.tensor_scalar(mod_a[:, 1, :], ST[1][:, D:2 * D], 1.0, None, ALU.add).then_inc(setup_dve.sem, 1)
                wait(dve, row_act, "xn3", 0)
                dve.wait_ge(setup_dve.sem, setup_dve.after("ca0", 0))
                V.tensor_tensor(h[:, :, :], h[:, :, :], over_tiles(mod_a[:, 1, :]), ALU.mult).then_inc(row_mod.sem, 1)
                wait(dve, row_mod, "scaled", 0)
                V.tensor_tensor(h[:, :, :], h[:, :, :], over_tiles(mod_a[:, 0, :]), ALU.add).then_inc(row_mod.sem, 1)

                dve.wait_ge(setup_pe.sem, setup_pe.after("mod", 0))
                seg = lambda r: mod_row[:, r * D:(r + 1) * D]
                src = lambda r: X[1 + r // 2][0:B, (r % 2) * D:(r % 2 + 1) * D]
                V.tensor_copy(seg(0), src(0)).then_inc(setup_dve.sem, 1)
                V.tensor_scalar(seg(1), src(1), 1.0, None, ALU.add).then_inc(setup_dve.sem, 1)
                V.tensor_copy(seg(3), src(3)).then_inc(setup_dve.sem, 1)
                V.tensor_scalar(seg(4), src(4), 1.0, None, ALU.add).then_inc(setup_dve.sem, 1)
                for j, r in enumerate((2, 5)):
                    V.tensor_copy(gate_raw[:, j, :], src(r)).then_inc(setup_dve.sem, 1)
                dve.wait_ge(setup_dve.sem, setup_dve.after("gb_raw", 0))
                V.scalar_tensor_tensor(out=gate_abs, in0=gate_raw, scalar=-1.0, in1=gate_raw, op0=ALU.mult, op1=ALU.max).then_inc(setup_dve.sem, 1)
                V.tensor_scalar(gate_sign, gate_raw, 0.0, 2.0, ALU.is_ge, ALU.mult).then_inc(setup_dve.sem, 1)
                dve.wait_ge(setup_dve.sem, setup_dve.after("sign", 0))
                V.tensor_scalar(gate_sign, gate_sign, -1.0, None, ALU.add).then_inc(setup_dve.sem, 1)
                V.tensor_scalar(gate_abs, gate_abs, 0.25, None, ALU.max).then_inc(setup_dve.sem, 1)
                dve.wait_ge(setup_dve.sem, setup_dve.after("max", 0))
                for j, r in enumerate((2, 5)):
                    V.tensor_tensor(seg(r), gate_abs[:, j, :], gate_sign[:, j, :], ALU.mult).then_inc(setup_dve.sem, 1)
                dve.wait_ge(setup_act.sem, setup_act.after("w1", 0))
                for k in range(KD):
                    V.scalar_tensor_tensor(out=w_lo[:, k, :], in0=O[k][:, :], scalar=nss[:, k:k + 1],
                                           in1=w_hi[:, k, :].bitcast(f32), op0=ALU.mult, op1=ALU.subtract).then_inc(setup_dve.sem, 1)

                def prep(p, step):
                    if step == "v":
                        return
                    i = 0 if step == "k" else int(step[-1])
                    if step.startswith("maxt"):
                        wait(dve, prep_pe, step, p)
                        V.tensor_tensor(qb[p % 2][DH:MK, i, :].rearrange("r (t c) -> r t c", t=TPB),
                                        X[1][0:TPB, i * P:(i + 1) * P].unsqueeze(1).to_broadcast([TPB, TPB, P]), mask[:, :, :],
                                        ALU.mult).then_inc(prep_dve.sem, 1)
                    elif step.startswith("max"):
                        i = int(step[3:])
                        wait(dve, prep_pe, step, p)
                        V.tensor_reduce(neg_max[:, i:i + 1], X[2 + i % 2][:, :], AX.X, ALU.max, negate=True).then_inc(prep_dve.sem, 1)
                    elif step[0] == "t":
                        wait(dve, prep_act, step, p)
                        V.tensor_tensor(t_lo[:, i, :], X[i][:, :], t_hi[:, i, :].bitcast(f32), ALU.subtract).then_inc(prep_dve.sem, 1)
                    elif step[0] == "q":
                        wait(dve, prep_act, f"q{HPG * i + 1}_again", p)
                        for r in range(HPG):
                            hh, half_ = HPG * i + r, slice(r * DH, (r + 1) * DH)
                            V.tensor_tensor(qb[p % 2][0:DH, hh, :], X[0][half_, :], qa[p % 2][half_, hh, :].bitcast(f32),
                                            ALU.subtract).then_inc(prep_dve.sem, 1)
                    else:
                        wait(dve, prep_act, "k_hi", p)
                        V.tensor_tensor(ka[p % 2][DH:P, 0, :], X[1][0:DH, :], ka[p % 2][0:DH, 0, :].bitcast(f32),
                                        ALU.subtract).then_inc(prep_dve.sem, 1)
                        V.tensor_tensor(ka[p % 2][DH:P, 1, :], X[1][DH:P, :], k_hi[DH:P, :].bitcast(f32),
                                        ALU.subtract).then_inc(prep_dve.sem, 1)

                def norm(b, hh):
                    acc = O[hh % 2][:, 0:TPB * (DH + 1)].rearrange("p (t c) -> p t c", t=TPB)
                    dve.wait_ge(pved, STEPS * b + (hh + 1) * TPB)
                    w(dve, normed, HEADS * b + hh)
                    V.reciprocal(inv[:, :], acc[:, :, DH]).then_inc(inverted, 1)
                    dve.wait_ge(inverted, HEADS * b + hh + 1)
                    w(dve, o_turned, 2 * b + hh // 2)
                    V.tensor_tensor(o_row[:, :, (hh % 2) * DH:(hh % 2 + 1) * DH], acc[:, :, 0:DH],
                                    inv[:, :].unsqueeze(2).to_broadcast([P, TPB, DH]), ALU.mult).then_inc(normed, 1)

                def close_x1(c, j):
                    if j == 0:
                        dve.wait_ge(x1_loaded, 16 * c + 16)
                    wait(dve, close_pe, f"wo{j}", c)
                    V.tensor_tensor(x1[:, 2 * j:2 * j + 2, :].rearrange("p t d -> p (t d)"), X[2 + j][:, :],
                                    x1[:, 2 * j:2 * j + 2, :].rearrange("p t d -> p (t d)"), ALU.add).then_inc(close_dve.sem, 1)

                def close_stats(c):
                    wait(dve, close_dve, "x1_1", c)
                    for t in range(TPB):
                        V.bn_stats(stats2[:, t, :], x1[:, t, :]).then_inc(close_dve.sem, 1)
                    wait(dve, close_dve, "st3", c)
                    for t in range(TPB):
                        V.bn_aggr(mv2[:, t, :], stats2[:, t, :]).then_inc(close_dve.sem, 1)

                def close_route(c):
                    logits = X[3][:, 0:TPB * E].rearrange("p (t e) -> p t e", e=E)
                    bcast = lambda ap: ap.unsqueeze(2).to_broadcast([P, TPB, E])
                    wait(dve, close_pe, "logits", c)
                    V.tensor_reduce(lmax[:, :], logits, AX.X, ALU.max).then_inc(close_dve.sem, 1)
                    wait(dve, close_dve, "lmax", c)
                    V.tensor_tensor(leq[:, :, :], logits, bcast(lmax[:, :]), ALU.is_equal).then_inc(close_dve.sem, 1)
                    wait(dve, close_dve, "leq", c)
                    V.tensor_tensor(lw[:, :, :], leq[:, :, :], rev8[:, :, :], ALU.mult).then_inc(close_dve.sem, 1)
                    wait(dve, close_dve, "lw", c)
                    V.tensor_reduce(erev[:, :], lw[:, :, :], AX.X, ALU.max).then_inc(close_dve.sem, 1)
                    wait(dve, close_dve, "erev", c)
                    V.tensor_tensor(onehot[:, :, :], rev8[:, :, :], bcast(erev[:, :]), ALU.is_equal).then_inc(close_dve.sem, 1)
                    V.tensor_copy(before[:, 0, :], before[:, TPB, :]).then_inc(close_dve.sem, 1)
                    for t in range(TPB):
                        dve.wait_ge(close_dve.sem, close_dve.after("carry", c) + t)
                        V.tensor_tensor(before[:, t + 1, :], before[:, t, :], onehot[:, t, :], ALU.add).then_inc(close_dve.sem, 1)

                def close_slot(c):
                    wait(dve, close_pe, "prefix", c)
                    V.tensor_tensor(prank[:, :, :], X[3][:, 64:64 + TPB * E].rearrange("p (t e) -> p t e", e=E),
                                    onehot[:, :, :], ALU.mult).then_inc(close_dve.sem, 1)
                    wait(dve, close_dve, "prank", c)
                    V.tensor_reduce(rank[:, :], prank[:, :, :], AX.X, ALU.add).then_inc(close_dve.sem, 1)
                    wait(dve, close_dve, "rank", c)
                    V.scalar_tensor_tensor(out=slot_f[:, :], in0=erev[:, :], scalar=float(-REGION), in1=rank[:, :],
                                           op0=ALU.mult, op1=ALU.add).then_inc(close_dve.sem, 1)
                    wait(dve, close_dve, "slot_f", c)
                    w(dve, slots_written, 16 * TPB * c)
                    V.tensor_scalar(slot[:, :], slot_f[:, :], float(E * REGION), None, ALU.add).then_inc(close_dve.sem, 1)

                row_stats(1)
                for step in in_order[:before_attention]:
                    prep(0, step)

                for b in range(B):
                    close, row = b > 0, b + 2 < B
                    for s in range(STEPS):
                        if s == 0 and b > 1:
                            close_slot(b - 2)
                        for p, step in PREP[b][s]:
                            prep(p, step)
                        if s == 2 and close:
                            close_x1(b - 1, 0)
                        if s == 3 and close:
                            close_x1(b - 1, 1)
                        if s == 4 and close:
                            close_stats(b - 1)
                        if s == 6 and row:
                            row_stats(b + 2)
                        if s == 15 and close:
                            close_route(b - 1)
                        if s % TPB == TPB - 1:
                            norm(b, s // TPB)
                close_slot(B - 2)
                c = B - 1
                for j in range(2):
                    close_x1(c, j)
                close_stats(c)
                wait(dve, close_act, "xn3", c)
                dve.wait_ge(modc_loaded, 16 * c + 16)
                V.tensor_tensor(crow[:, :, :], crow[:, :, :], over_tiles(mod_c[:, 2, :]), ALU.mult).then_inc(close_mod.sem, 1)
                wait(dve, close_mod, "scaled", c)
                V.tensor_tensor(crow[:, :, :], crow[:, :, :], over_tiles(mod_c[:, 1, :]), ALU.add).then_inc(close_mod.sem, 1)
                close_route(c)
                close_slot(c)

                link = [0]
                def step(ins):
                    ins.then_inc(counted, 1)
                    link[0] += 1
                    dve.wait_ge(counted, link[0])
                dve.wait_ge(table_ready, 1)
                step(V.tensor_scalar(counts[:, :], X[0][0:1, 0:E], float(P - 1), None, ALU.add))
                step(V.tensor_scalar(ntile_i[:, :], counts[:, :], P.bit_length() - 1, None, ALU.arith_shift_right))
                step(V.tensor_copy(ntile[:, :], ntile_i[:, :]))
                last = ntile
                for j, d in enumerate((1, 2, 4)):
                    step(V.tensor_copy(pre[j][:, 0:d], last[:, 0:d]))
                    step(V.tensor_tensor(pre[j][:, d:E], last[:, d:E], last[:, 0:E - d], ALU.add))
                    last = pre[j]
                over = lambda ap: ap[:, 0:E - 1].unsqueeze(1).to_broadcast([1, TILES + 1, E - 1])
                step(V.tensor_tensor(passed[:, :, :], over(last), tidx[:, :, :], ALU.is_le))
                step(V.tensor_reduce(te_f[:, :], passed[:, :, :], AX.X, ALU.add))
                step(V.tensor_tensor(passed_n[:, :, :], passed[:, :, :], over(ntile), ALU.mult))
                step(V.tensor_reduce(base_f[:, :], passed_n[:, :, :], AX.X, ALU.add))
                step(V.tensor_tensor(j_f[:, :], tidx[:, :, 0], base_f[:, :], ALU.subtract))
                step(V.tensor_scalar(j_f[:, :], j_f[:, :], float(REGION // P - 1), float(P), ALU.min, ALU.mult))
                step(V.scalar_tensor_tensor(out=ts_f[:, :], in0=te_f[:, :], scalar=float(REGION), in1=j_f[:, :], op0=ALU.mult, op1=ALU.add))
                step(V.tensor_copy(tile_slot[:, :], ts_f[:, :]))
                step(V.tensor_copy(tile_expert[:, :], te_f[:, :]))

            @block.tensor
            def _(pe):
                T = nc.tensor
                def split_products(out_ap, pairs):
                    terms = [(a, c) for a_hi, a_lo, c_hi, c_lo in pairs for a, c in ((a_hi, c_hi), (a_lo, c_hi), (a_hi, c_lo))]
                    for n, (a, c) in enumerate(terms):
                        last = T.matmul(out_ap, a, c, start=(n == 0), stop=(n == len(terms) - 1))
                    return last

                pe.wait_ge(setup_pool.sem, setup_pool.after("ident", 0))
                pe.wait_ge(setup_act.sem, setup_act.after("silu", 0))
                for k in range(KD):
                    last = T.transpose(X[0][:, k * B:(k + 1) * B], sc4[:, k * P:(k + 1) * P], ident[0:B, 0:B])
                last.then_inc(setup_pe.sem, 1)
                pe.wait_ge(setup_dve.sem, setup_dve.after("sc", 0))
                pe.wait_ge(wmod_loaded, 16)
                for k in range(KD):
                    last = T.matmul(ST[1][:, :], sc_t[:, k, 0:1].to_broadcast([P, P]), wmod[:, k, 0:512], start=(k == 0), stop=(k == KD - 1))
                last.then_inc(setup_pe.sem, 1)
                for r in range(3):
                    for k in range(KD):
                        last = T.matmul(X[1 + r][0:B, :], sc_t[:, k, :], wmod[:, k, r * 512:(r + 1) * 512], start=(k == 0), stop=(k == KD - 1))
                last.then_inc(setup_pe.sem, 1)
                pe.wait_ge(raw_loaded, 64)
                for k in range(KD):
                    for o in range(KD):
                        T.transpose(O[k][:, o * P:(o + 1) * P], wq_raw[:, o, k * P:(k + 1) * P], ident[:, :])
                        T.transpose(ST[0][:, k * D + o * P:k * D + (o + 1) * P], wo_raw[:, o, k * P:(k + 1) * P], ident[:, :])
                    T.transpose(O[k][:, D:D + P], wk_raw[:, k * P:(k + 1) * P], ident[:, :])
                    last = T.transpose(O[k][:, D + P:D + 2 * P], wv_raw[:, k * P:(k + 1) * P], ident[:, :])
                last.then_inc(setup_pe.sem, 1)

                def turn(stage, src_, k):
                    for t in range(TPB):
                        last = T.transpose(X[k][:, t * P:(t + 1) * P], src_[:, t, k * P:(k + 1) * P], ident[:, :])
                    last.then_inc(stage.sem, 1)

                def projection(bank, at_col):
                    c = slice(at_col, at_col + P)
                    return split_products(X[bank][:, :], [(w_hi[:, k, c], w_lo[:, k, c], t_hi[:, k, :], t_lo[:, k, :])
                                                          for k in range(KD)])

                def prep(p, step):
                    if step in ("t0", "t1"):
                        if step == "t0":
                            wait(pe, row_act, "hn3", p)
                            wait(pe, prep_dve, "maxt3", p - 1)
                            wait(pe, prep_dve, "q3", p - 1)
                            wait(pe, close_act, "t1", p - 3)
                            if p == 0:
                                pe.wait_ge(setup_dve.sem, setup_dve.after("gb", 0))
                        turn(prep_pe, rows, int(step[1]))
                    elif step.startswith("maxt"):
                        hh = int(step[4])
                        wait(pe, prep_dve, f"max{TPB * hh + TPB - 1}", p)
                        wait(pe, prep_act, "v", p)
                        T.transpose(X[1][0:TPB, hh * P:(hh + 1) * P], neg_max[:, TPB * hh:TPB * (hh + 1)], ident[:, :]).then_inc(prep_pe.sem, 1)
                    elif step.startswith("max"):
                        i = int(step[3:])
                        hh, st = i // TPB, i % TPB
                        wait(pe, prep_act, f"q{hh}_again", p)
                        wait(pe, prep_act, f"ka{hh // HPG}", p)
                        if i == 0:
                            wait(pe, prep_dve, f"max{STEPS - 2}", p - 1)
                            wait(pe, close_dve, "x1_1", p - 2)
                        elif i == 1:
                            wait(pe, prep_dve, f"max{STEPS - 1}", p - 1)
                            wait(pe, close_dve, "slot", p - 3)
                        else:
                            wait(pe, prep_dve, f"max{i - 2}", p)
                        T.matmul(X[2 + i % 2][:, :], qa[p % 2][0:DH, hh, st * P:(st + 1) * P], ka[p % 2][0:DH, hh // HPG, :],
                                 start=True, stop=True).then_inc(prep_pe.sem, 1)
                    elif step[0] == "q":
                        g = int(step[1])
                        wait(pe, prep_act, ("t1", "q1_again")[g], p)
                        wait(pe, prep_dve, ("t1", "q1")[g], p)
                        if p == 0 and g == 0:
                            pe.wait_ge(setup_dve.sem, setup_dve.after(f"w{KD - 1}", 0))
                        projection(0, g * P).then_inc(prep_pe.sem, 1)
                    elif step == "k":
                        projection(1, D).then_inc(prep_pe.sem, 1)
                    else:
                        wait(pe, prep_act, "k_hi", p)
                        wait(pe, prep_dve, "k1", p)
                        for t in range(TPB):
                            c = slice(t * P, (t + 1) * P)
                            last = split_products(X[1][:, c], [(t_hi[:, k, c], t_lo[:, k, c], w_hi[:, k, D + P:], w_lo[:, k, D + P:])
                                                               for k in range(KD)])
                        last.then_inc(prep_pe.sem, 1)

                def turn_o(n, j):
                    pe.wait_ge(normed, HEADS * n + 2 * j + 2)
                    for t in range(TPB):
                        last = T.transpose(O[1][:, t * P:(t + 1) * P], o_row[:, t, :], ident[:, :])
                    last.then_inc(o_turned, 1)

                def close_wo(c, j):
                    if j == 0:
                        wait(pe, close_pool, "wo_g", c)
                        pe.wait_ge(o_live, 2 * c + 2)
                        wait(pe, prep_dve, f"max{STEPS - 1}", min(c + 1, B - 1))
                        wait(pe, close_dve, "slot", c - 1)
                    for i in range(2):
                        t = 2 * j + i
                        for k in range(KD):
                            last = T.matmul(X[2 + j][:, i * D:(i + 1) * D], o_t[:, k, t * P:(t + 1) * P], wo_g[:, k, :],
                                            start=(k == 0), stop=(k == KD - 1))
                    last.then_inc(close_pe.sem, 1)

                def close_t(c):
                    wait(pe, close_mod, "h2", c)
                    p = min(c + 2, B - 1)
                    wait(pe, prep_dve, "maxt3", p)
                    wait(pe, close_act, "t1", c - 1)
                    for k in range(KD):
                        turn(close_pe, crow, k)

                def close_logits(c):
                    wait(pe, close_act, "t1", c)
                    wait(pe, prep_dve, f"max{STEPS - 1}", min(c + 2, B - 1))
                    wait(pe, close_dve, "x1_1", c)
                    for t in range(TPB):
                        for k in range(KD):
                            last = T.matmul(X[3][:, t * E:(t + 1) * E], t_c[:, k, t * P:(t + 1) * P], wr[:, k, :],
                                            start=(k == 0), stop=(k == KD - 1))
                    last.then_inc(close_pe.sem, 1)

                def close_prefix(c):
                    wait(pe, close_dve, f"add{TPB - 1}", c)
                    o = X[3][:, 64:64 + TPB * E]
                    T.matmul(o, upper[:, :], onehot[:, :, :].rearrange("p t e -> p (t e)"), start=True, stop=False)
                    T.matmul(o, ones[:, :], before[:, 0:TPB, :].rearrange("p t e -> p (t e)"), start=False, stop=True).then_inc(close_pe.sem, 1)

                def score(b, s):
                    hh, t = s // TPB, s % TPB
                    if s == 0:
                        wait(pe, prep_act, "v", b)
                    if t == 0:
                        wait(pe, prep_dve, f"maxt{hh}", b)
                    w(pe, exped, STEPS * b + s - 1)
                    c = slice(t * P, (t + 1) * P)
                    T.matmul(ST[s % 2][:, :], ka[b % 2][:, hh // HPG, c], qa[b % 2][:, hh, :], start=True, stop=False)
                    T.matmul(ST[s % 2][:, :], kb[b % 2][0:MK, hh // HPG, c], qb[b % 2][0:MK, hh, :], start=False, stop=True).then_inc(scored, 1)

                def weigh(b, s):
                    hh, t = s // TPB, s % TPB
                    if t == 0:
                        w(pe, normed, HEADS * b + hh - 1)
                        if hh % 2:
                            w(pe, o_live, 2 * b + hh // 2)
                    pe.wait_ge(exped, STEPS * b + s + 1)
                    for q in range(TPB):
                        last = T.matmul(O[hh % 2][:, q * (DH + 1):(q + 1) * (DH + 1)], prob[:, s % 2, q * P:(q + 1) * P],
                                        va[b % 2][:, t, hh // HPG, :], start=(t == 0 and q == 0), stop=(t == TPB - 1),
                                        skip_group_check=True)
                    last.then_inc(pved, 1)

                for step in in_order[:before_attention]:
                    prep(0, step)

                for b in range(B):
                    close = b > 0
                    score(b, 0)
                    score(b, 1)
                    for s in range(STEPS):
                        if s == 1 and close:
                            turn_o(b - 1, 1)
                        if s == 9:
                            turn_o(b, 0)
                        weigh(b, s)
                        if s + 2 < STEPS:
                            score(b, s + 2)
                        if s == 0 and b > 1:
                            close_prefix(b - 2)
                        for p, step in PREP[b][s]:
                            prep(p, step)
                        if s == 2 and close:
                            close_wo(b - 1, 0)
                        if s == 3 and close:
                            close_wo(b - 1, 1)
                        if s == 13 and close:
                            close_t(b - 1)
                        if s == 14 and close:
                            close_logits(b - 1)
                close_prefix(B - 2)
                c = B - 1
                turn_o(c, 1)
                close_wo(c, 0)
                close_wo(c, 1)
                close_t(c)
                close_logits(c)
                close_prefix(c)
                wait(pe, close_dve, "slot", c)
                T.matmul(X[0][:, 0:E], ones[:, :], before[:, TPB, :], start=True, stop=True).then_inc(table_ready, 1)

        with ExitStack() as ffn:
            sf = lambda name, shape, dt: sb(name, shape, dt, ffn)
            ps = [ffn.enter_context(nc.psum_tensor(f"fbank{i}", [P, 512], f32)) for i in range(5)]
            HT, G, U, AT, Y = ps
            RING = 6
            idx = [sf(f"idx{j}", [P, 1], i32) for j in range(RING)]
            hg = [sf(f"hg{j}", [P, D], f32) for j in range(2)]
            ht = [sf(f"ht{j}", [P, KD, P], f32) for j in range(2)]
            sg = sf("sg", [P, I], f32)
            a = sf("a", [P, I], f32)
            at_ = sf("a_t", [P, KI, P], f32)
            yb = [sf(f"yb{j}", [P, D], f32) for j in range(2)]
            x1f = sf("x1f", [P, NT, D], f32)
            yf = sf("yf", [P, NT, D], f32)
            gb_rows = sf("gb_rows", [P, B, D], f32)

            idx_loaded = [sem(f"idx_loaded{j}") for j in range(RING)]
            gathered = [sem(f"gathered{j}") for j in range(2)]
            scattered = [sem(f"scattered{j}") for j in range(2)]
            tr_done, up_done, at_done, down_done = sem("tr_done"), sem("up_done"), sem("at_done"), sem("down_done")
            gate_done = sem("gate_done")
            ht_ready, silu_done, a_ready, at_ready, y_ready = (sem("ht_ready"), sem("silu_done"), sem("a_ready"),
                                                               sem("at_ready"), sem("y_ready"))
            x1f_loaded, gb_loaded = sem("x1f_loaded"), sem("gb_loaded")
            yf_loaded = [sem(f"yf_loaded{b}") for b in range(B)]
            mul_done, add_done, add_pool = sem("mul_done"), sem("add_done"), sem("add_pool")
            out_stored = sem("out_stored")

            block = ffn.enter_context(nc.Block())

            assert TILES % 2 == 1

            def steps(eng, body):
                with eng.Fori(0, TILES // 2) as q:
                    body(q, 1, 2 * q + 1)
                    body(q + 1, 0, 2 * q + 2)

            def xrows2(ap, n):
                return ap[n * S:(n + 1) * S, :].rearrange("(t p) d -> p t d", p=P)

            @block.sync
            def _(sp):
                for i in range(TILES):
                    at0 = nc.values_load(tile_slot[0:1, i:i + 1], engines=[mybir.EngineType.SP], min_val=0,
                                         max_val=(E - 1) * REGION + REGION - P)
                    if i >= RING:
                        sp.wait_ge(scattered[i % 2], 16 * ((i - RING) // 2) + 16)
                    sp.dma_start(idx[i % RING][:, :], slots_d[ds(at0, P), :]).then_inc(idx_loaded[i % RING], 16)
                    if i == 3:
                        sp.dma_start(gb_rows[:, :, :], mod_d[:, 5 * D:6 * D].unsqueeze(0).to_broadcast([P, B, D])).then_inc(gb_loaded, 16)
                        sp.dma_start(x1f[:, :, :], x1_d.rearrange("(t p) d -> p t d", p=P)).then_inc(x1f_loaded, 16)
                sp.wait_ge(scattered[0], 16 * ((TILES + 1) // 2))
                sp.wait_ge(scattered[1], 16 * (TILES // 2))
                for b in range(B):
                    sp.dma_start(yf[:, b * TPB:(b + 1) * TPB, :], xrows2(y_d, b)).then_inc(yf_loaded[b], 16)
                for b in range(B):
                    for j in range(2):
                        sp.wait_ge(add_done if j == 0 else add_pool, b + 1)
                        t = b * TPB + 2 * j
                        sp.dma_start(out.rearrange("b (t p) d -> p (b t) d", p=P)[:, t:t + 2, :], yf[:, t:t + 2, :]).then_inc(out_stored, 16)
                sp.wait_ge(out_stored, 16 * 2 * B)

            @block.gpsimd
            def _(pool):
                def gather(i):
                    par = i % 2
                    pool.wait_ge(idx_loaded[i % RING], 16 * (i // RING) + 16)
                    if i >= 2:
                        pool.wait_ge(tr_done, i - 1)
                    nc.gpsimd.indirect_dma_start(out=hg[par][:, :], out_offset=None, in_=h2_d,
                                                 in_offset=bass.IndirectOffsetOnAxis(ap=idx[i % RING][:, :], axis=0)).then_inc(gathered[par], 16)

                def scatter(i):
                    par = i % 2
                    pool.wait_ge(y_ready, i + 1)
                    if i >= 1:
                        pool.wait_ge(scattered[1 - par], 16 * ((i + 1) // 2))
                    nc.gpsimd.indirect_dma_start(out=y_d, out_offset=bass.IndirectOffsetOnAxis(ap=idx[i % RING][:, :], axis=0),
                                                 in_=yb[par][:, :], in_offset=None).then_inc(scattered[par], 16)

                gather(0)
                gather(1)
                for i in range(TILES + 2):
                    if i + 2 < TILES:
                        gather(i + 2)
                    if i >= 2:
                        scatter(i - 2)
                pool.wait_ge(x1f_loaded, 16)
                for b in range(B):
                    t = b * TPB + 2
                    pool.wait_ge(mul_done, b + 1)
                    nc.gpsimd.tensor_tensor(yf[:, t:t + 2, :], yf[:, t:t + 2, :], x1f[:, t:t + 2, :], ALU.add).then_inc(add_pool, 1)

            @block.tensor
            def _(pe):
                T = nc.tensor

                def expert(i):
                    return nc.values_load(tile_expert[0:1, ds(i, 1)], engines=[mybir.EngineType.PE], min_val=0, max_val=E - 1)

                def transpose_rows(q, par, i):
                    pe.wait_ge(gathered[par], 16 * q + 16)
                    w(pe, ht_ready, i)
                    for k in range(KD):
                        last = T.transpose(HT[:, k * P:(k + 1) * P], hg[par][:, k * P:(k + 1) * P], ident[:, :])
                    last.then_inc(tr_done, 1)

                def gate(par, i, e):
                    pe.wait_ge(ht_ready, i + 1)
                    w(pe, silu_done, i)
                    for k in range(KD):
                        last = T.matmul(G[:, :], ht[par][:, k, :], w_gate[:, ds(e, 1), k, :].rearrange("p e i -> p (e i)"),
                                        start=(k == 0), stop=(k == KD - 1))
                    last.then_inc(gate_done, 1)

                def up(par, i, e):
                    w(pe, a_ready, i)
                    for k in range(KD):
                        last = T.matmul(U[:, :], ht[par][:, k, :], w_up[:, ds(e, 1), k, :].rearrange("p e i -> p (e i)"),
                                        start=(k == 0), stop=(k == KD - 1))
                    last.then_inc(up_done, 1)

                def transpose_a(i):
                    pe.wait_ge(a_ready, i + 1)
                    w(pe, at_ready, i)
                    for k in range(KI):
                        last = T.transpose(AT[:, k * P:(k + 1) * P], a[:, k * P:(k + 1) * P], ident[:, :])
                    last.then_inc(at_done, 1)

                def down(i, e):
                    pe.wait_ge(at_ready, i + 1)
                    w(pe, y_ready, i)
                    for k in range(KI):
                        last = T.matmul(Y[:, 0:D], at_[:, k, :], w_down[:, ds(e, 1), k, :].rearrange("p e d -> p (e d)"),
                                        start=(k == 0), stop=(k == KI - 1))
                    last.then_inc(down_done, 1)

                for j in range(3):
                    pe.wait_ge(w_loaded[j], 16 * E)
                transpose_rows(0, 0, 0)
                transpose_rows(0, 1, 1)
                e = expert(0)
                gate(0, 0, e)
                up(0, 0, e)

                def step(q, par, i, next_):
                    e = expert(i)
                    gate(par, i, e)
                    transpose_a(i - 1)
                    if next_ is not None:
                        transpose_rows(*next_)
                    up(par, i, e)
                    down(i - 1, expert(i - 1))

                with pe.Fori(0, TILES // 2 - 1) as q:
                    step(q, 1, 2 * q + 1, (q + 1, 0, 2 * q + 2))
                    step(q + 1, 0, 2 * q + 2, (q + 1, 1, 2 * q + 3))
                q = TILES // 2 - 1
                step(q, 1, 2 * q + 1, (q + 1, 0, 2 * q + 2))
                step(q + 1, 0, 2 * q + 2, None)
                transpose_a(TILES - 1)
                down(TILES - 1, expert(TILES - 1))

            @block.scalar
            def _(act):
                A = nc.scalar.activation

                def silu(i):
                    act.wait_ge(gate_done, i + 1)
                    w(act, a_ready, i)
                    A(sg[:, :], G[:, :], ACT.Silu).then_inc(silu_done, 1)

                def evacuate_a(i):
                    act.wait_ge(at_done, i + 1)
                    w(act, down_done, i)
                    A(at_[:, :, :].rearrange("p k c -> p (k c)"), AT[:, :], ACT.Copy).then_inc(at_ready, 1)

                def step(q, par, i):
                    silu(i)
                    evacuate_a(i - 1)

                silu(0)
                steps(act, step)
                evacuate_a(TILES - 1)

            @block.vector
            def _(dve):
                V = nc.vector

                def copy_ht(q, par, i):
                    dve.wait_ge(tr_done, i + 1)
                    w(dve, up_done, i - 1)
                    V.tensor_copy(ht[par][:, :, :].rearrange("p k c -> p (k c)"), HT[:, 0:KD * P]).then_inc(ht_ready, 1)

                def product(i):
                    dve.wait_ge(up_done, i + 1)
                    dve.wait_ge(silu_done, i + 1)
                    w(dve, at_done, i)
                    V.tensor_tensor(a[:, :], sg[:, :], U[:, :], ALU.mult).then_inc(a_ready, 1)

                def copy_y(q, par, i):
                    dve.wait_ge(down_done, i + 1)
                    w(dve, scattered[par], 16 * q)
                    V.tensor_copy(yb[par][:, :], Y[:, 0:D]).then_inc(y_ready, 1)

                copy_ht(0, 0, 0)
                copy_ht(0, 1, 1)
                product(0)

                def step(i, previous, next_):
                    if next_ is not None:
                        copy_ht(*next_)
                    product(i)
                    copy_y(*previous)

                with dve.Fori(0, TILES // 2 - 1) as q:
                    step(2 * q + 1, (q, 0, 2 * q), (q + 1, 0, 2 * q + 2))
                    step(2 * q + 2, (q, 1, 2 * q + 1), (q + 1, 1, 2 * q + 3))
                q = TILES // 2 - 1
                step(2 * q + 1, (q, 0, 2 * q), (q + 1, 0, 2 * q + 2))
                step(2 * q + 2, (q, 1, 2 * q + 1), None)
                copy_y(TILES // 2, 0, TILES - 1)
                dve.wait_ge(gb_loaded, 16)
                dve.wait_ge(x1f_loaded, 16)
                for b in range(B):
                    t = b * TPB
                    dve.wait_ge(yf_loaded[b], 16)
                    V.tensor_tensor(yf[:, t:t + TPB, :], yf[:, t:t + TPB, :],
                                    gb_rows[:, b, :].unsqueeze(1).to_broadcast([P, TPB, D]), ALU.mult).then_inc(mul_done, 1)
                    dve.wait_ge(mul_done, b + 1)
                    V.tensor_tensor(yf[:, t:t + 2, :], yf[:, t:t + 2, :], x1f[:, t:t + 2, :], ALU.add).then_inc(add_done, 1)


_INS = ["L0_attn_x", "L0_attn_norm_scale", "L0_attn_split_scale", "L0_attn_Wq", "L0_attn_Wk", "L0_attn_Wv",
        "L0_attn_Wo", "L0_ffn_router_w", "L0_ffn_gate_w", "L0_ffn_up_w", "L0_ffn_down_w", "L0_c", "L0_wmod"]


def kernel(**inputs):
    import numpy as np
    import concourse.bacc as bacc
    from concourse import mybir
    from concourse.bass_utils import run_bass_kernel_spmd

    nc = bacc.Bacc("TRN2", target_bir_lowering=False, num_devices=1)
    arrays, io = {}, {}
    for name in _INS:
        arr = np.ascontiguousarray(inputs[name])
        arrays[name + "_dram"] = arr
        io[name] = nc.dram_tensor(name + "_dram", arr.shape, mybir.dt.from_np(arr.dtype), kind="ExternalInput").ap()
    shape = inputs["L0_attn_x"].shape
    io["out"] = nc.dram_tensor("out_dram", shape, mybir.dt.float32, kind="ExternalOutput").ap()
    build(nc, io)
    r = run_bass_kernel_spmd(nc, [arrays], core_ids=[0])
    return r.results[0]["out_dram"]
```

```python
def build(nc, io):
    import concourse.bass as bass
    import concourse.mybir as mybir
    from contextlib import ExitStack

    f32, f32r, bf16, i32 = (mybir.dt.float32, mybir.dt.float32r, mybir.dt.bfloat16,
                            mybir.dt.int32)
    ALU = mybir.AluOpType
    ACT = mybir.ActivationFunctionType
    AX = mybir.AxisListType
    ds = bass.ds

    x_in, out = io["L0_attn_x"], io["out"]
    P = 128
    B, S, D = x_in.shape
    HEADS, GROUPS, DH = 4, 2, 64
    HPG = HEADS // GROUPS
    E, _, I = io["L0_ffn_gate_w"].shape
    KD = D // P
    KI = I // P
    TPB = S // P
    N = B * S
    NT = N // P
    TILES = NT + E - 1
    REGION = N + P
    LN_EPS, RMS_EPS = 1e-5, 1e-8
    SCALE = 1.0 / float(DH) ** 0.5
    STEPS = HEADS * TPB
    MK = DH + TPB

    def dram(name, shape, dt):
        return nc.dram_tensor(name, shape, dt, kind="Internal").ap()

    mod_d = dram("mod_d", (B, 6 * D), f32)
    xh_d = dram("xh_d", (N, D), f32)
    res_d = dram("res_d", (N + P, 2 * D), f32)
    h2_d = dram("h2_d", (N + P, D), f32)
    slots_d = dram("slots_d", (E * REGION, 1), i32)

    top = ExitStack()
    sem = lambda name: top.enter_context(nc.semaphore(name))

    class Stage:
        def __init__(self, name, steps):
            self.sem, self.steps = sem(name), steps
        def after(self, step, n):
            return n * len(self.steps) + self.steps.index(step) + 1

    def names(base, n):
        return [f"{base}{i}" for i in range(n)]

    with top:
        sb = lambda name, shape, dt, c=top: c.enter_context(nc.sbuf_tensor(name, shape, dt))
        w_gate = sb("w_gate", [P, E, KD, I], f32)
        w_up = sb("w_up", [P, E, KD, I], f32)
        w_down = sb("w_down", [P, E, KI, D], f32)
        ident = sb("ident", [P, P], f32)
        tile_expert = sb("tile_expert", [1, TILES + 1], i32)
        tile_slot = sb("tile_slot", [1, TILES + 1], i32)

        w_loaded = [sem(f"w_loaded{j}") for j in range(3)]

        with ExitStack() as att:
            sa_ = lambda name, shape, dt: sb(name, shape, dt, att)
            ps = [att.enter_context(nc.psum_tensor(f"bank{i}", [P, 512], f32)) for i in range(8)]
            ST, O, X = ps[0:2], ps[2:4], ps[4:8]

            late = lambda e: w_down[:, e, :, :]
            x, h, rows = late(E - 1), late(E - 2), late(E - 3)
            x1 = sa_("x1", [P, TPB, D], f32)
            crow = sa_("crow", [P, TPB, D], f32)
            mod_a = sa_("mod_a", [P, 3, D], f32)
            mod_c = sa_("mod_c", [P, 3, D], f32)
            t_hi = sa_("t_hi", [P, KD, S], f32r)
            t_lo = sa_("t_lo", [P, KD, S], f32r)
            t_c = sa_("t_c", [P, KD, S], f32)
            pair = lambda name, shape, dt: [sa_(f"{name}{j}", shape, dt) for j in range(2)]
            qa = pair("qa", [P, HEADS, S], f32r)
            qb = pair("qb", [P, HEADS, S], f32r)
            ka = pair("ka", [P, GROUPS, S], f32r)
            kb = pair("kb", [P, GROUPS, S], f32r)
            va = pair("va", [P, TPB, GROUPS, DH + 1], f32)
            k_hi = sa_("k_hi", [P, S], f32r)
            prob = sa_("prob", [P, 2, S], f32)
            inv = sa_("inv", [P, TPB], f32)
            o_cols = sa_("o_cols", [DH + 1, S], f32)
            o_row = sa_("o_row", [P, TPB, P], f32)
            o_t = sa_("o_t", [P, HEADS // 2, S], f32)
            spare = w_up[:, :, :, :].rearrange("p e k d -> p (e k d)")
            at = [0]
            def temp(parts, n):
                at[0] += n
                return spare[0:parts, at[0] - n:at[0]]
            wmod = temp(P, KD * 6 * D).rearrange("p (k n) -> p k n", k=KD)
            wq_raw = temp(P, 2 * D).rearrange("p (o d) -> p o d", d=D)
            wk_raw, wv_raw = temp(P, D), temp(P, D)
            wo_raw = temp(P, 2 * D).rearrange("p (o d) -> p o d", d=D)
            mod_row = temp(B, 6 * D)
            c4, sc4 = temp(B, D), temp(B, D)
            gate_raw, gate_abs, gate_sign = (temp(B, 2 * D).rearrange("p (r d) -> p r d", d=D) for _ in range(3))
            w_hi = sa_("w_hi", [P, KD, 2 * D], f32r)
            w_lo = sa_("w_lo", [P, KD, 2 * D], f32r)
            wo_t = sa_("wo_t", [P, KD, D], f32)
            wo_g = sa_("wo_g", [P, KD, D], f32)
            wr = sa_("wr", [P, KD, E], f32)
            mask = sa_("mask", [TPB, TPB, P], bf16)
            upper = sa_("upper", [P, P], bf16)
            ones = sa_("ones", [P, P], bf16)
            rev8 = sa_("rev8", [P, TPB, E], f32)
            rev8i = sa_("rev8i", [P, TPB, E], i32)
            nsc = sa_("nsc", [P, KD], f32)
            ssc = sa_("ssc", [P, KD], f32)
            nss = sa_("nss", [P, KD], f32)
            stats = sa_("stats", [P, TPB, 6], f32)
            mv = sa_("mv", [P, TPB, 2], f32)
            var = sa_("var", [P, TPB], f32)
            nrme = sa_("nrme", [P, TPB], f32)
            var2 = sa_("var2", [P, TPB], f32)
            mhalf = sa_("mhalf", [P, TPB], f32)
            half = sa_("half", [P, TPB], f32)
            rstd = sa_("rstd", [P, TPB], f32)
            nmr = sa_("nmr", [P, TPB], f32)
            ssq = sa_("ssq", [P, TPB], f32)
            nrm = sa_("nrm", [P, TPB], f32)
            rinv = sa_("rinv", [P, TPB], f32)
            stats2 = sa_("stats2", [P, TPB, 6], f32)
            mv2 = sa_("mv2", [P, TPB, 2], f32)
            rstd2 = sa_("rstd2", [P, TPB], f32)
            nmr2 = sa_("nmr2", [P, TPB], f32)
            neg_max = sa_("neg_max", [P, HEADS * TPB], f32)
            lmax = sa_("lmax", [P, TPB], f32)
            leq = sa_("leq", [P, TPB, E], f32)
            lw = sa_("lw", [P, TPB, E], f32)
            erev = sa_("erev", [P, TPB], f32)
            onehot = sa_("onehot", [P, TPB, E], bf16)
            before = sa_("before", [P, TPB + 1, E], bf16)
            prank = sa_("prank", [P, TPB, E], f32)
            rank = sa_("rank", [P, TPB], f32)
            slot_f = sa_("slot_f", [P, TPB], f32)
            slot = sa_("slot", [P, TPB], i32)
            token = sa_("token", [P, NT], i32)
            fill = sa_("fill", [P, E * REGION // P], i32)
            counts = sa_("counts", [1, E], i32)
            ntile_i = sa_("ntile_i", [1, E], i32)
            ntile = sa_("ntile", [1, E], f32)
            pre = [sa_(f"pre{j}", [1, E], f32) for j in range(3)]
            tidx = sa_("tidx", [1, TILES + 1, E - 1], i32)
            cells = (TILES + 1) * (E - 1)
            passed, passed_n = (o_cols[0:1, j * cells:(j + 1) * cells].rearrange("o (t e) -> o t e", e=E - 1) for j in range(2))
            te_f = sa_("te_f", [1, TILES + 1], f32)
            base_f = sa_("base_f", [1, TILES + 1], f32)
            j_f = sa_("j_f", [1, TILES + 1], f32)
            ts_f = sa_("ts_f", [1, TILES + 1], f32)
            sc_t = sa_("sc_t", [P, KD, B], f32)

            c_loaded, wmod_loaded, raw_loaded, small_loaded = (sem("c_loaded"), sem("wmod_loaded"),
                                                               sem("raw_loaded"), sem("small_loaded"))
            wmod0_loaded = sem("wmod0_loaded")
            mod_stored, zeros_stored = sem("mod_stored"), sem("zeros_stored")
            x_loaded, moda_loaded, modc_loaded, x1_loaded = (sem("x_loaded"), sem("moda_loaded"),
                                                             sem("modc_loaded"), sem("x1_loaded"))
            xh_stored, x1_stored, h2_stored = sem("xh_stored"), sem("x1_stored"), sem("h2_stored")
            gb_stored = sem("gb_stored")
            slots_filled, slots_written = sem("slots_filled"), sem("slots_written")
            scored, exped, pved = sem("scored"), sem("exped"), sem("pved")
            inverted, normed = sem("inverted"), sem("normed")
            o_copied, o_by_row = sem("o_copied"), sem("o_by_row")
            o_turned, o_live = sem("o_turned"), sem("o_live")
            table_ready = sem("table_ready")
            last_scaled = sem("last_scaled")
            counted = sem("counted")

            row_dve = Stage("row_dve", names("st", TPB) + names("ag", TPB) + ["var", "nmr", "nrme", "rinv"])
            row_act = Stage("row_act", names("xn", TPB) + names("sq", TPB) + names("hn", TPB))
            row_pow = Stage("row_pow", ["rstd", "nrm"])
            close_pow = Stage("close_pow", ["rstd"])
            row_pool = Stage("row_pool", ["gated", "xh"])
            row_mod = Stage("row_mod", ["scaled", "h"])
            in_order = (["t0", "t1", "q0", "k", "max0", "max1", "q1", "max2", "max3", "v", "max4", "max5", "maxt0"]
                        + ["max6", "max7", "max8", "max9", "maxt1", "max10", "max11", "max12", "max13", "maxt2",
                           "max14", "max15", "maxt3"])
            before_attention = in_order.index("maxt0") + 1
            later = [(0, step) for step in in_order[before_attention:]]

            def deal(steps_, counts_):
                assert sum(counts_) == len(steps_)
                at_ = [sum(counts_[:s_]) for s_ in range(STEPS + 1)]
                return [steps_[at_[s_]:at_[s_ + 1]] for s_ in range(STEPS)]
            usual = [2, 1, 1, 0, 0, 3, 2, 2, 2, 2, 3, 2, 3, 2, 1, 0]
            PREP = [deal(later + [(1, step) for step in in_order],
                         [2, 3, 2, 3, 2, 1, 3, 3, 3, 4, 3, 3, 4, 2, 1, 0])]
            PREP += [deal([(b + 1, step) for step in in_order], usual) for b in range(1, B - 1)]
            PREP += [[[] for _ in range(STEPS)]]
            first_row = dict(norm=0, square=4, rms=5, scale=5)
            ROW = [dict(stats=7, nmr=8, norm=9, square=12, rms=14, scale=15)] + [dict(stats=3, nmr=4, norm=5, square=9, rms=12, scale=13)] * (B - 3)
            CLOSE_T = [None] + [14] * (B - 2) + [12]
            ROUTE = [[] for _ in range(B)]
            for b_ in range(2, B):
                ROUTE[b_].append((b_ - 2, 0))
            ROUTE[B - 1].append((B - 2, 13))
            prep_pe = Stage("prep_pe", in_order)
            prep_act = Stage("prep_act", ["t0", "t1", "q0", "q0_again", "q1", "q1_again", "ka0", "kb0", "ka1", "kb1", "k_hi",
                                          "q2", "q2_again", "q3", "q3_again", "v"])
            parts = {"q0": ["q0", "q1"], "q1": ["q2", "q3"], "k": ["k0", "k1"], "v": []}
            prep_dve = Stage("prep_dve", [part for step in in_order for part in parts.get(step, [step])])
            close_pe = Stage("close_pe", ["wo0", "wo1", "t0", "t1", "logits", "prefix"])
            close_act = Stage("close_act", names("xn", TPB) + names("t", 2))
            close_dve = Stage("close_dve", ["x1_0", "st0", "st1", "x1_1", "st2", "st3"] + names("ag", TPB) + ["var", "nmr"]
                              + ["lmax", "leq", "lw", "erev", "onehot", "carry"]
                              + names("add", TPB) + ["prank", "rank", "slot_f", "slot"])
            close_pool = Stage("close_pool", ["wo_g"])
            close_mod = Stage("close_mod", ["scaled", "h2"])

            setup_pe = Stage("setup_pe", ["sc", "mod0", "mod", "w"])
            setup_act = Stage("setup_act", ["silu"] + names("w", KD) + ["wo"])
            setup_dve = Stage("setup_dve", ["kb0", "kb1", "fill", "rev8", "sc", "nss", "sa0", "ca0", "sa", "ca", "sb", "cb",
                                            "ga_raw", "gb_raw"] + names("w", KD) + ["abs", "sign", "pm", "max", "ga", "gb"])
            setup_pool = Stage("setup_pool", names("memset", 10) + ["ident", "upper", "mask",
                                                                    "rev8", "token", "tidx", "fill_iota"])

            def over_tiles(row):
                return row.unsqueeze(1).to_broadcast([P, TPB, D])

            def w(eng, s, value):
                if not isinstance(value, int) or value > 0:
                    eng.wait_ge(s, value)

            def wait(eng, stage, step, n):
                if n >= 0:
                    w(eng, stage.sem, stage.after(step, n))

            block = att.enter_context(nc.Block())

            def xrows(ap, n):
                return ap[n * S:(n + 1) * S, :].rearrange("(t p) d -> p t d", p=P)

            x_rows = x_in.rearrange("b s d -> (b s) d")

            def load_weights(eng, j, e):
                dst, src, pat = ((w_gate, "L0_ffn_gate_w", "(k p) i -> p k i"), (w_up, "L0_ffn_up_w", "(k p) i -> p k i"),
                                 (w_down, "L0_ffn_down_w", "(k p) d -> p k d"))[j]
                eng.dma_start(dst[:, e, :, :], io[src][e, :, :].rearrange(pat, p=P)).then_inc(w_loaded[j], 16)

            @block.sync
            def _(sp):
                sp.dma_start(c4, io["L0_c"]).then_inc(c_loaded, 16)
                wmod_cols = lambda c: (wmod[:, :, c], io["L0_wmod"].rearrange("(k p) n -> p k n", p=P)[:, :, c])
                sp.dma_start(*wmod_cols(slice(0, 512))).then_inc(wmod0_loaded, 16)
                sp.dma_start(x[:, :, :], xrows(x_rows, 0)).then_inc(x_loaded, 16)
                sp.dma_start(*wmod_cols(slice(512, 6 * D))).then_inc(wmod_loaded, 16)
                sp.dma_start(wk_raw, io["L0_attn_Wk"]).then_inc(raw_loaded, 16)
                sp.dma_start(wv_raw, io["L0_attn_Wv"]).then_inc(raw_loaded, 16)
                sp.dma_start(wo_raw, io["L0_attn_Wo"].rearrange("(o p) d -> p o d", p=P)).then_inc(raw_loaded, 16)
                for e in range(2):
                    load_weights(sp, 0, e)
                sp.wait_ge(setup_dve.sem, setup_dve.after("gb", 0))
                sp.dma_start(mod_d, mod_row).then_inc(mod_stored, 16)
                sp.wait_ge(setup_dve.sem, setup_dve.after("fill", 0))
                sp.dma_start(slots_d.rearrange("(p j) o -> p (j o)", p=P), fill[:, :]).then_inc(slots_filled, 16)
                sp.dma_start(h2_d[N:N + P, :], crow[:, 0, :]).then_inc(zeros_stored, 16)
                sp.dma_start(res_d[N:N + P, :], crow[:, 1:3, :].rearrange("p t d -> p (t d)")).then_inc(zeros_stored, 16)

                def load_row(p):
                    r = 2 if p == 0 else 0
                    wait(sp, row_pool, "xh", p - 1)
                    if p == 0:
                        sp.wait_ge(mod_stored, 16)
                    sp.dma_start(mod_a[:, r:3, :].rearrange("p r d -> p (r d)"),
                                 mod_d[p:p + 1, r * D:3 * D].partition_broadcast(P)).then_inc(moda_loaded, 16)
                    if p > 0:
                        sp.dma_start(x[:, :, :], xrows(x_rows, p)).then_inc(x_loaded, 16)

                def store_xh(p):
                    wait(sp, row_pool, "xh", p)
                    sp.dma_start(xrows(xh_d, p), h[:, :, :]).then_inc(xh_stored, 16)

                def load_x1(c):
                    sp.wait_ge(xh_stored, 16 * c + 16)
                    w(sp, x1_stored, 16 * c)
                    sp.dma_start(x1[:, :, :], xrows(xh_d, c)).then_inc(x1_loaded, 16)

                def store_x1(c):
                    wait(sp, close_dve, "x1_1", c)
                    sp.dma_start(xrows(res_d, c)[:, :, 0:D], x1[:, :, :]).then_inc(x1_stored, 16)

                def store_h2(c):
                    wait(sp, close_mod, "h2", c)
                    sp.dma_start(xrows(h2_d, c), crow[:, :, :]).then_inc(h2_stored, 16)

                def load_modc(b):
                    wait(sp, close_mod, "h2", b - 1)
                    sp.dma_start(mod_c[:, :, :].rearrange("p r d -> p (r d)"),
                                 mod_d[b:b + 1, 2 * D:5 * D].partition_broadcast(P)).then_inc(modc_loaded, 16)

                load_row(0)
                for e in range(2, 4):
                    load_weights(sp, 0, e)
                load_row(1)
                store_xh(0)
                load_modc(0)
                load_x1(0)
                sp.dma_start(res_d[0:N, D:2 * D].rearrange("(b s) d -> b s d", s=S),
                             mod_d[:, 5 * D:6 * D].unsqueeze(1).to_broadcast([B, S, D])).then_inc(gb_stored, 16)
                for e in range(4, 8):
                    load_weights(sp, 0, e)
                sp.wait_ge(setup_pe.sem, setup_pe.after("w", 0))
                sp.wait_ge(setup_dve.sem, setup_dve.after("gb", 0))
                for e in range(2):
                    load_weights(sp, 1, e)
                load_row(2)
                store_xh(1)

                batches = [[(1, e) for e in range(2, 8)], [(2, e) for e in range(E - 3)], [], []]
                for b in range(B):
                    if b > 1:
                        load_x1(b - 1)
                    if b + 2 == B:
                        sp.wait_ge(xh_stored, 16 * B)
                        load_weights(sp, 2, E - 1)
                        load_weights(sp, 2, E - 2)
                        wait(sp, prep_pe, "t1", B - 1)
                        load_weights(sp, 2, E - 3)
                    for j, e in batches[b]:
                        load_weights(sp, j, e)
                    if b > 0:
                        store_x1(b - 1)
                        store_h2(b - 1)
                        load_modc(b)
                    if b + 2 < B:
                        if b + 3 < B:
                            load_row(b + 3)
                        store_xh(b + 2)
                load_x1(B - 1)
                store_x1(B - 1)
                store_h2(B - 1)
                sp.wait_ge(x1_stored, 16 * B)
                sp.wait_ge(h2_stored, 16 * B)
                sp.wait_ge(zeros_stored, 32)
                sp.wait_ge(gb_stored, 16)

            @block.gpsimd
            def _(pool):
                nc_ = nc.gpsimd
                nc_.memset(ident[:, :], 0.0).then_inc(setup_pool.sem, 1)
                nc_.memset(mask[:, :, :], 0.0).then_inc(setup_pool.sem, 1)
                nc_.memset(upper[:, :], 1.0).then_inc(setup_pool.sem, 1)
                nc_.memset(mhalf[:, :], -0.5).then_inc(setup_pool.sem, 1)
                nc_.memset(half[:, :], 0.5).then_inc(setup_pool.sem, 1)
                pool.wait_ge(setup_pool.sem, 3)
                nc_.memset(ones[:, :], 1.0).then_inc(setup_pool.sem, 1)
                nc_.memset(crow[:, 0:3, :], 0.0).then_inc(setup_pool.sem, 1)
                nc_.memset(va[0][:, :, :, DH:DH + 1], 1.0).then_inc(setup_pool.sem, 1)
                nc_.memset(va[1][:, :, :, DH:DH + 1], 1.0).then_inc(setup_pool.sem, 1)
                nc_.memset(before[:, TPB, :], 0.0).then_inc(setup_pool.sem, 1)
                nc_.affine_select(out=ident[:, :], in_=ident[:, :], compare_op=ALU.not_equal, fill=1.0, base=0,
                                  pattern=[[-1, P]], channel_multiplier=1).then_inc(setup_pool.sem, 1)
                nc_.affine_select(out=upper[:, :], in_=upper[:, :], compare_op=ALU.is_gt, fill=0.0, base=0,
                                  pattern=[[1, P]], channel_multiplier=-1).then_inc(setup_pool.sem, 1)
                nc_.affine_select(out=mask[:, :, :], in_=mask[:, :, :], compare_op=ALU.not_equal, fill=1.0,
                                  base=0, pattern=[[1, TPB], [0, P]], channel_multiplier=-1).then_inc(setup_pool.sem, 1)
                nc_.iota(rev8i[:, :, :], pattern=[[0, TPB], [-1, E]], base=E, channel_multiplier=0).then_inc(setup_pool.sem, 1)
                nc_.iota(token[:, :], pattern=[[P, NT]], base=0, channel_multiplier=1).then_inc(setup_pool.sem, 1)
                nc_.iota(tidx[:, :, :], pattern=[[1, TILES + 1], [0, E - 1]], base=0, channel_multiplier=0).then_inc(setup_pool.sem, 1)
                nc_.iota(fill[:, :], pattern=[[1, E * REGION // P]], base=0,
                         channel_multiplier=E * REGION // P).then_inc(setup_pool.sem, 1)

                def row_rstd(p):
                    wait(pool, row_dve, "var", p)
                    nc_.tensor_tensor(rstd[:, :], var[:, :], mhalf[:, :], ALU.pow).then_inc(row_pow.sem, 1)

                def row_nrm(p):
                    wait(pool, row_act, "sq3", p)
                    nc_.tensor_tensor(nrm[:, :], ssq[:, :], half[:, :], ALU.pow).then_inc(row_pow.sem, 1)

                def close_rstd(c):
                    wait(pool, close_dve, "var", c)
                    nc_.tensor_tensor(rstd2[:, :], var2[:, :], mhalf[:, :], ALU.pow).then_inc(close_pow.sem, 1)

                def row_h(p):
                    wait(pool, row_act, "xn3", p)
                    pool.wait_ge(moda_loaded, 16 * p + 16)
                    nc_.tensor_tensor(h[:, :, :], h[:, :, :], over_tiles(mod_a[:, 1, :]), ALU.mult).then_inc(row_mod.sem, 1)
                    wait(pool, row_mod, "scaled", p)
                    nc_.tensor_tensor(h[:, :, :], h[:, :, :], over_tiles(mod_a[:, 0, :]), ALU.add).then_inc(row_mod.sem, 1)

                def row_xh(p):
                    wait(pool, row_act, "hn3", p)
                    pool.wait_ge(moda_loaded, 16 * p + 16)
                    nc_.tensor_tensor(h[:, :, :], h[:, :, :], over_tiles(mod_a[:, 2, :]), ALU.mult).then_inc(row_pool.sem, 1)
                    wait(pool, row_pool, "gated", p)
                    nc_.tensor_tensor(h[:, :, :], x[:, :, :], h[:, :, :], ALU.add).then_inc(row_pool.sem, 1)

                def close_gate(c):
                    pool.wait_ge(modc_loaded, 16 * c + 16)
                    if c == 0:
                        pool.wait_ge(setup_act.sem, setup_act.after("wo", 0))
                    wait(pool, close_pe, "wo1", c - 1)
                    nc_.tensor_tensor(wo_g[:, :, :], wo_t[:, :, :],
                                      mod_c[:, 0, :].unsqueeze(1).to_broadcast([P, KD, D]), ALU.mult).then_inc(close_pool.sem, 1)

                def close_h2(c):
                    wait(pool, close_act, "xn3", c)
                    nc_.tensor_tensor(crow[:, :, :], crow[:, :, :], over_tiles(mod_c[:, 2, :]), ALU.mult).then_inc(close_mod.sem, 1)
                    wait(pool, close_mod, "scaled", c)
                    nc_.tensor_tensor(crow[:, :, :], crow[:, :, :], over_tiles(mod_c[:, 1, :]), ALU.add).then_inc(close_mod.sem, 1)

                def close_slots(c):
                    wait(pool, close_dve, "slot", c)
                    if c == 0:
                        pool.wait_ge(slots_filled, 16)
                    for t in range(TPB):
                        nc_.indirect_dma_start(out=slots_d, out_offset=bass.IndirectOffsetOnAxis(ap=slot[:, t:t + 1], axis=0),
                                               in_=token[:, c * TPB + t:c * TPB + t + 1], in_offset=None).then_inc(slots_written, 16)

                row_rstd(0)
                row_nrm(0)
                row_xh(0)
                row_rstd(1)
                row_h(1)
                row_nrm(1)
                row_xh(1)
                for b in range(B):
                    for c, at_ in ROUTE[b]:
                        if at_ == 0:
                            close_slots(c)
                    if b + 2 < B:
                        row_rstd(b + 2)
                    if b > 0:
                        close_rstd(b - 1)
                    if b + 2 < B:
                        row_h(b + 2)
                    if b > 0:
                        close_h2(b - 1)
                    if b + 2 < B:
                        row_nrm(b + 2)
                        row_xh(b + 2)
                    close_gate(b)
                close_slots(B - 2)
                close_rstd(B - 1)
                close_slots(B - 1)
                pool.wait_ge(slots_written, 16 * TPB * B)

            @block.scalar
            def _(act):
                A = nc.scalar.activation
                act.dma_start(wq_raw, io["L0_attn_Wq"].rearrange("(o p) d -> p o d", p=P)).then_inc(raw_loaded, 16)
                act.dma_start(nsc[:, :], io["L0_attn_norm_scale"].rearrange("(k p) -> p k", p=P), allow_slow_non_contiguous=True).then_inc(small_loaded, 16)
                act.dma_start(ssc[:, :], io["L0_attn_split_scale"].rearrange("(k p) -> p k", p=P), allow_slow_non_contiguous=True).then_inc(small_loaded, 16)
                act.dma_start(wr[:, :, :], io["L0_ffn_router_w"].rearrange("(k p) e -> p k e", p=P)).then_inc(small_loaded, 16)
                act.wait_ge(c_loaded, 16)
                A(sc4, c4, ACT.Silu).then_inc(setup_act.sem, 1)

                first_half, second_half = range(TPB // 2), range(TPB // 2, TPB)

                def row_norm(p, tiles_=range(TPB)):
                    act.wait_ge(x_loaded, 16 * p + 16)
                    wait(act, row_dve, "nmr", p)
                    w(act, xh_stored, 16 * p)
                    for t in tiles_:
                        A(h[:, t, :], x[:, t, :], ACT.Identity, bias=nmr[:, t:t + 1], scale=rstd[:, t:t + 1]).then_inc(row_act.sem, 1)

                def row_square(p):
                    wait(act, row_mod, "h", p)
                    wait(act, prep_pe, "t1", p - 1)
                    for t in range(TPB):
                        A(rows[:, t, :], h[:, t, :], ACT.Square, accum_out=ssq[:, t:t + 1]).then_inc(row_act.sem, 1)

                def row_scale(p):
                    wait(act, row_dve, "rinv", p)
                    for t in range(TPB):
                        A(rows[:, t, :], h[:, t, :], ACT.Copy, scale=rinv[:, t:t + 1]).then_inc(row_act.sem, 1)

                def prep_t(p):
                    for k in range(KD):
                        wait(act, prep_pe, f"t{k}", p)
                        A(t_hi[:, k, :], X[k][:, :], ACT.Copy).then_inc(prep_act.sem, 1)

                def prep_q(p, g):
                    wait(act, prep_pe, f"q{g}", p)
                    if g == 0:
                        w(act, scored, STEPS * (p - 1))
                    for i in range(HPG):
                        for r in (0, DH):
                            A(qa[p % 2][r:r + DH, HPG * g + i, :], X[0][i * DH:(i + 1) * DH, :], ACT.Copy).then_inc(prep_act.sem, 1)

                def prep_k(p):
                    wait(act, prep_pe, "k", p)
                    for g in range(GROUPS):
                        for dst in (ka, kb):
                            A(dst[p % 2][0:DH, g, :], X[1][g * DH:(g + 1) * DH, :], ACT.Copy).then_inc(prep_act.sem, 1)
                    wait(act, prep_dve, "k1", p - 1)
                    A(k_hi[DH:P, :], X[1][DH:P, :], ACT.Copy).then_inc(prep_act.sem, 1)

                def prep_v(p):
                    wait(act, prep_pe, "v", p)
                    w(act, pved, STEPS * (p - 1))
                    A(va[p % 2][:, :, :, 0:DH], X[1][:, :].rearrange("p (t g c) -> p t g c", t=TPB, g=GROUPS),
                      ACT.Copy).then_inc(prep_act.sem, 1)

                def copy_o(n, hh):
                    act.wait_ge(pved, STEPS * n + (hh + 1) * TPB)
                    w(act, o_by_row, HEADS * n + hh)
                    A(o_cols[:, :], O[hh % 2][0:DH + 1, :], ACT.Copy).then_inc(o_copied, 1)

                def evacuate_o(n, j):
                    act.wait_ge(o_turned, 2 * n + j + 1)
                    wait(act, close_pe, "wo1", n - 1)
                    A(o_t[:, j, :], O[1][:, :], ACT.Copy).then_inc(o_live, 1)

                def close_norm(c, tiles_=range(TPB)):
                    wait(act, close_dve, "nmr", c)
                    w(act, h2_stored, 16 * c)
                    if c == 0:
                        act.wait_ge(zeros_stored, 32)
                    wait(act, close_pe, "t1", c - 1)
                    for t in tiles_:
                        A(crow[:, t, :], x1[:, t, :], ACT.Identity, bias=nmr2[:, t:t + 1], scale=rstd2[:, t:t + 1]).then_inc(close_act.sem, 1)

                def close_t(c):
                    for k in range(KD):
                        wait(act, close_pe, f"t{k}", c)
                        A(t_c[:, k, :], X[k][:, :], ACT.Copy).then_inc(close_act.sem, 1)

                row_norm(0)
                row_square(0)
                act.wait_ge(setup_dve.sem, setup_dve.after("nss", 0))
                act.wait_ge(setup_pe.sem, setup_pe.after("w", 0))
                for k in range(KD):
                    A(w_hi[:, k, :], O[k][:, :], ACT.Copy, scale=nss[:, k:k + 1]).then_inc(setup_act.sem, 1)
                A(wo_t[:, :, :].rearrange("p k d -> p (k d)"), ST[0][:, :], ACT.Copy).then_inc(setup_act.sem, 1)
                row_scale(0)
                prep_t(0)
                prep_q(0, 0)
                prep_k(0)
                prep_q(0, 1)
                prep_v(0)

                act_prep = {"t0": lambda p: prep_t(p), "q0": lambda p: prep_q(p, 0), "k": prep_k,
                            "q1": lambda p: prep_q(p, 1), "v": prep_v}

                def beside(b, s):
                    close, row = b > 0, b + 2 < B
                    if s % TPB == TPB - 1:
                        copy_o(b, s // TPB)
                    if s == 2 and close:
                        evacuate_o(b - 1, 1)
                    for p, step in PREP[b][s]:
                        if step in act_prep:
                            act_prep[step](p)
                    for p, at_ in ([(1, first_row)] if b == 0 else []) + ([(b + 2, ROW[b])] if row else []):
                        if s == at_["norm"]:
                            row_norm(p, first_half)
                        if s == at_["norm"] + 1:
                            row_norm(p, second_half)
                        if s == at_["square"]:
                            row_square(p)
                        if s == at_["scale"]:
                            row_scale(p)
                    if s == 7 and close:
                        close_norm(b - 1, first_half)
                    if s == 8 and close:
                        close_norm(b - 1, second_half)
                    if s == 10:
                        evacuate_o(b, 0)
                    if close and s == CLOSE_T[b]:
                        close_t(b - 1)

                for b in range(B):
                    for s in range(STEPS):
                        act.wait_ge(scored, STEPS * b + s + 1)
                        w(act, pved, STEPS * b + s - 1)
                        A(prob[:, s % 2, :], ST[s % 2][:, :], ACT.Exp, scale=SCALE).then_inc(exped, 1)
                        if s > 0:
                            beside(b, s - 1)
                        elif b > 0:
                            beside(b - 1, STEPS - 1)
                beside(B - 1, STEPS - 1)
                evacuate_o(B - 1, 1)
                close_norm(B - 1)
                close_t(B - 1)

            @block.vector
            def _(dve):
                V = nc.vector
                for j in range(2):
                    V.memset(kb[j][DH:MK, :, :].bitcast(f32), 1.0).then_inc(setup_dve.sem, 1)
                dve.wait_ge(setup_pool.sem, setup_pool.after("fill_iota", 0))
                V.tensor_scalar(fill[:, :], fill[:, :], P - 1, N, ALU.bitwise_and, ALU.bitwise_or).then_inc(setup_dve.sem, 1)
                V.tensor_copy(rev8[:, :, :], rev8i[:, :, :]).then_inc(setup_dve.sem, 1)
                dve.wait_ge(setup_pe.sem, setup_pe.after("sc", 0))
                V.tensor_copy(sc_t[:, :, :], X[0][:, 0:2 * B].rearrange("p (k b) -> p k b", k=KD)).then_inc(setup_dve.sem, 1)

                def row_stats(p):
                    dve.wait_ge(x_loaded, 16 * p + 16)
                    for t in range(TPB):
                        V.bn_stats(stats[:, t, :], x[:, t, :]).then_inc(row_dve.sem, 1)
                    wait(dve, row_dve, "st3", p)
                    for t in range(TPB):
                        V.bn_aggr(mv[:, t, :], stats[:, t, :]).then_inc(row_dve.sem, 1)
                    wait(dve, row_dve, "ag3", p)
                    wait(dve, row_act, "xn3", p - 1)
                    V.tensor_scalar(var[:, :], mv[:, :, 1], LN_EPS, None, ALU.add).then_inc(row_dve.sem, 1)

                def row_nmr(p):
                    wait(dve, row_pow, "rstd", p)
                    V.scalar_tensor_tensor(out=nmr[:, :], in0=mv[:, :, 0], scalar=-1.0, in1=rstd[:, :], op0=ALU.mult, op1=ALU.mult).then_inc(row_dve.sem, 1)

                def row_rms(p):
                    wait(dve, row_pow, "nrm", p)
                    V.tensor_scalar(nrme[:, :], nrm[:, :], float(D) ** -0.5, RMS_EPS, ALU.mult, ALU.add).then_inc(row_dve.sem, 1)
                    wait(dve, row_dve, "nrme", p)
                    wait(dve, row_act, "hn3", p - 1)
                    V.reciprocal(rinv[:, :], nrme[:, :]).then_inc(row_dve.sem, 1)

                row_stats(0)
                row_nmr(0)
                dve.wait_ge(small_loaded, 48)
                V.tensor_tensor(nss[:, :], nsc[:, :], ssc[:, :], ALU.mult).then_inc(setup_dve.sem, 1)
                dve.wait_ge(setup_pe.sem, setup_pe.after("mod0", 0))
                V.tensor_copy(mod_a[:, 0, :], ST[1][:, 0:D]).then_inc(setup_dve.sem, 1)
                V.tensor_scalar(mod_a[:, 1, :], ST[1][:, D:2 * D], 1.0, None, ALU.add).then_inc(setup_dve.sem, 1)
                wait(dve, row_act, "xn3", 0)
                dve.wait_ge(setup_dve.sem, setup_dve.after("ca0", 0))
                V.tensor_tensor(h[:, :, :], h[:, :, :], over_tiles(mod_a[:, 1, :]), ALU.mult).then_inc(row_mod.sem, 1)
                wait(dve, row_mod, "scaled", 0)
                V.tensor_tensor(h[:, :, :], h[:, :, :], over_tiles(mod_a[:, 0, :]), ALU.add).then_inc(row_mod.sem, 1)
                dve.wait_ge(setup_pe.sem, setup_pe.after("mod", 0))
                seg = lambda r: mod_row[:, r * D:(r + 1) * D]
                src = lambda r: X[1 + r // 2][0:B, (r % 2) * D:(r % 2 + 1) * D]
                V.tensor_copy(seg(0), src(0)).then_inc(setup_dve.sem, 1)
                V.tensor_scalar(seg(1), src(1), 1.0, None, ALU.add).then_inc(setup_dve.sem, 1)
                V.tensor_copy(seg(3), src(3)).then_inc(setup_dve.sem, 1)
                V.tensor_scalar(seg(4), src(4), 1.0, None, ALU.add).then_inc(setup_dve.sem, 1)
                row_rms(0)
                for j, r in enumerate((2, 5)):
                    V.tensor_copy(gate_raw[:, j, :], src(r)).then_inc(setup_dve.sem, 1)
                dve.wait_ge(setup_act.sem, setup_act.after("w1", 0))
                for k in range(KD):
                    V.scalar_tensor_tensor(out=w_lo[:, k, :], in0=O[k][:, :], scalar=nss[:, k:k + 1],
                                           in1=w_hi[:, k, :].bitcast(f32), op0=ALU.mult, op1=ALU.subtract).then_inc(setup_dve.sem, 1)
                dve.wait_ge(setup_dve.sem, setup_dve.after("gb_raw", 0))
                V.scalar_tensor_tensor(out=gate_abs, in0=gate_raw, scalar=-1.0, in1=gate_raw, op0=ALU.mult, op1=ALU.max).then_inc(setup_dve.sem, 1)
                V.tensor_scalar(gate_sign, gate_raw, 0.0, 2.0, ALU.is_ge, ALU.mult).then_inc(setup_dve.sem, 1)
                dve.wait_ge(setup_dve.sem, setup_dve.after("sign", 0))
                V.tensor_scalar(gate_sign, gate_sign, -1.0, None, ALU.add).then_inc(setup_dve.sem, 1)
                V.tensor_scalar(gate_abs, gate_abs, 0.25, None, ALU.max).then_inc(setup_dve.sem, 1)
                dve.wait_ge(setup_dve.sem, setup_dve.after("max", 0))
                for j, r in enumerate((2, 5)):
                    V.tensor_tensor(seg(r), gate_abs[:, j, :], gate_sign[:, j, :], ALU.mult).then_inc(setup_dve.sem, 1)

                def prep(p, step):
                    if step == "v":
                        return
                    i = 0 if step == "k" else int(step[-1])
                    if step.startswith("maxt"):
                        wait(dve, prep_pe, step, p)
                        V.tensor_tensor(qb[p % 2][DH:MK, i, :].rearrange("r (t c) -> r t c", t=TPB),
                                        X[1][0:TPB, i * P:(i + 1) * P].unsqueeze(1).to_broadcast([TPB, TPB, P]), mask[:, :, :],
                                        ALU.mult).then_inc(prep_dve.sem, 1)
                    elif step.startswith("max"):
                        i = int(step[3:])
                        wait(dve, prep_pe, step, p)
                        V.tensor_reduce(neg_max[:, i:i + 1], X[2 + i % 2][:, :], AX.X, ALU.max, negate=True).then_inc(prep_dve.sem, 1)
                    elif step[0] == "t":
                        wait(dve, prep_act, step, p)
                        V.tensor_tensor(t_lo[:, i, :], X[i][:, :], t_hi[:, i, :].bitcast(f32), ALU.subtract).then_inc(prep_dve.sem, 1)
                    elif step[0] == "q":
                        wait(dve, prep_act, f"q{HPG * i + 1}_again", p)
                        for r in range(HPG):
                            hh, half_ = HPG * i + r, slice(r * DH, (r + 1) * DH)
                            V.tensor_tensor(qb[p % 2][0:DH, hh, :], X[0][half_, :], qa[p % 2][half_, hh, :].bitcast(f32),
                                            ALU.subtract).then_inc(prep_dve.sem, 1)
                    else:
                        wait(dve, prep_act, "k_hi", p)
                        V.tensor_tensor(ka[p % 2][DH:P, 0, :], X[1][0:DH, :], ka[p % 2][0:DH, 0, :].bitcast(f32),
                                        ALU.subtract).then_inc(prep_dve.sem, 1)
                        V.tensor_tensor(ka[p % 2][DH:P, 1, :], X[1][DH:P, :], k_hi[DH:P, :].bitcast(f32),
                                        ALU.subtract).then_inc(prep_dve.sem, 1)

                def norm(b, hh):
                    acc = O[hh % 2][:, 0:TPB * (DH + 1)].rearrange("p (t c) -> p t c", t=TPB)
                    dve.wait_ge(o_by_row, HEADS * b + hh + 1)
                    w(dve, normed, HEADS * b + hh)
                    V.reciprocal(inv[:, :], acc[:, :, DH]).then_inc(inverted, 1)
                    dve.wait_ge(inverted, HEADS * b + hh + 1)
                    w(dve, o_turned, 2 * b + hh // 2)
                    V.tensor_tensor(o_row[:, :, (hh % 2) * DH:(hh % 2 + 1) * DH], acc[:, :, 0:DH],
                                    inv[:, :].unsqueeze(2).to_broadcast([P, TPB, DH]), ALU.mult).then_inc(normed, 1)

                def close_x1(c, j):
                    if j == 0:
                        dve.wait_ge(x1_loaded, 16 * c + 16)
                    wait(dve, close_pe, f"wo{j}", c)
                    V.tensor_tensor(x1[:, 2 * j:2 * j + 2, :].rearrange("p t d -> p (t d)"), X[2 + j][:, :],
                                    x1[:, 2 * j:2 * j + 2, :].rearrange("p t d -> p (t d)"), ALU.add).then_inc(close_dve.sem, 1)
                    wait(dve, close_dve, f"x1_{j}", c)
                    for t in (2 * j, 2 * j + 1):
                        V.bn_stats(stats2[:, t, :], x1[:, t, :]).then_inc(close_dve.sem, 1)

                def close_stats(c):
                    wait(dve, close_dve, "st3", c)
                    for t in range(TPB):
                        V.bn_aggr(mv2[:, t, :], stats2[:, t, :]).then_inc(close_dve.sem, 1)
                    wait(dve, close_dve, "ag3", c)
                    wait(dve, close_act, "xn3", c - 1)
                    V.tensor_scalar(var2[:, :], mv2[:, :, 1], LN_EPS, None, ALU.add).then_inc(close_dve.sem, 1)

                def close_nmr(c):
                    wait(dve, close_pow, "rstd", c)
                    V.scalar_tensor_tensor(out=nmr2[:, :], in0=mv2[:, :, 0], scalar=-1.0, in1=rstd2[:, :], op0=ALU.mult, op1=ALU.mult).then_inc(close_dve.sem, 1)

                def close_route(c):
                    logits = X[3][:, 0:TPB * E].rearrange("p (t e) -> p t e", e=E)
                    bcast = lambda ap: ap.unsqueeze(2).to_broadcast([P, TPB, E])
                    wait(dve, close_pe, "logits", c)
                    V.tensor_reduce(lmax[:, :], logits, AX.X, ALU.max).then_inc(close_dve.sem, 1)
                    wait(dve, close_dve, "lmax", c)
                    V.tensor_tensor(leq[:, :, :], logits, bcast(lmax[:, :]), ALU.is_equal).then_inc(close_dve.sem, 1)
                    wait(dve, close_dve, "leq", c)
                    V.tensor_tensor(lw[:, :, :], leq[:, :, :], rev8[:, :, :], ALU.mult).then_inc(close_dve.sem, 1)
                    wait(dve, close_dve, "lw", c)
                    V.tensor_reduce(erev[:, :], lw[:, :, :], AX.X, ALU.max).then_inc(close_dve.sem, 1)
                    wait(dve, close_dve, "erev", c)
                    V.tensor_tensor(onehot[:, :, :], rev8[:, :, :], bcast(erev[:, :]), ALU.is_equal).then_inc(close_dve.sem, 1)
                    V.tensor_copy(before[:, 0, :], before[:, TPB, :]).then_inc(close_dve.sem, 1)
                    for t in range(TPB):
                        dve.wait_ge(close_dve.sem, close_dve.after("carry", c) + t)
                        V.tensor_tensor(before[:, t + 1, :], before[:, t, :], onehot[:, t, :], ALU.add).then_inc(close_dve.sem, 1)

                def close_slot(c):
                    wait(dve, close_pe, "prefix", c)
                    V.tensor_tensor(prank[:, :, :], X[3][:, 64:64 + TPB * E].rearrange("p (t e) -> p t e", e=E),
                                    onehot[:, :, :], ALU.mult).then_inc(close_dve.sem, 1)
                    wait(dve, close_dve, "prank", c)
                    V.tensor_reduce(rank[:, :], prank[:, :, :], AX.X, ALU.add).then_inc(close_dve.sem, 1)
                    wait(dve, close_dve, "rank", c)
                    V.scalar_tensor_tensor(out=slot_f[:, :], in0=erev[:, :], scalar=float(-REGION), in1=rank[:, :],
                                           op0=ALU.mult, op1=ALU.add).then_inc(close_dve.sem, 1)
                    wait(dve, close_dve, "slot_f", c)
                    w(dve, slots_written, 16 * TPB * c)
                    V.tensor_scalar(slot[:, :], slot_f[:, :], float(E * REGION), None, ALU.add).then_inc(close_dve.sem, 1)

                for step in in_order[:before_attention]:
                    prep(0, step)
                row_stats(1)
                row_nmr(1)

                for b in range(B):
                    close, row = b > 0, b + 2 < B
                    for s in range(STEPS):
                        if row and s == ROW[b]["rms"]:
                            row_rms(b + 2)
                        if s % TPB == 1 and s > 1:
                            norm(b, s // TPB - 1)
                        if s == 1 and b > 0:
                            norm(b - 1, HEADS - 1)
                        for c, at_ in ROUTE[b]:
                            if s == at_ + 1:
                                close_route(c)
                        for c, at_ in ROUTE[b]:
                            if s == at_ + 2:
                                close_slot(c)
                        for p, step in PREP[b][s]:
                            prep(p, step)
                        if s == 3 and close:
                            close_x1(b - 1, 0)
                        if s == 4 and close:
                            close_x1(b - 1, 1)
                        if s == 4 and close:
                            close_stats(b - 1)
                        if s == 5 and close:
                            close_nmr(b - 1)
                        if s == first_row["rms"] and b == 0:
                            row_rms(1)
                        if row and s == ROW[b]["stats"]:
                            row_stats(b + 2)
                        if row and s == ROW[b]["nmr"]:
                            row_nmr(b + 2)
                norm(B - 1, HEADS - 1)
                c = B - 1
                for j in range(2):
                    close_x1(c, j)
                close_stats(c)
                close_nmr(c)
                dve.wait_ge(modc_loaded, 16 * c + 16)
                for j in range(2):
                    half_ = crow[:, 2 * j:2 * j + 2, :]
                    over_half = lambda row: row.unsqueeze(1).to_broadcast([P, 2, D])
                    wait(dve, close_act, f"xn{2 * j + 1}", c)
                    V.tensor_tensor(half_, half_, over_half(mod_c[:, 2, :]), ALU.mult).then_inc(last_scaled, 1)
                    dve.wait_ge(last_scaled, j + 1)
                    V.tensor_tensor(half_, half_, over_half(mod_c[:, 1, :]), ALU.add).then_inc(close_mod.sem, 1)
                close_route(c)
                close_slot(c)

                link = [0]
                def step(ins):
                    ins.then_inc(counted, 1)
                    link[0] += 1
                    dve.wait_ge(counted, link[0])
                dve.wait_ge(table_ready, 1)
                step(V.tensor_scalar(counts[:, :], X[0][0:1, 0:E], float(P - 1), None, ALU.add))
                step(V.tensor_scalar(ntile_i[:, :], counts[:, :], P.bit_length() - 1, None, ALU.arith_shift_right))
                step(V.tensor_copy(ntile[:, :], ntile_i[:, :]))
                last = ntile
                for j, d in enumerate((1, 2, 4)):
                    step(V.tensor_copy(pre[j][:, 0:d], last[:, 0:d]))
                    step(V.tensor_tensor(pre[j][:, d:E], last[:, d:E], last[:, 0:E - d], ALU.add))
                    last = pre[j]
                over = lambda ap: ap[:, 0:E - 1].unsqueeze(1).to_broadcast([1, TILES + 1, E - 1])
                step(V.tensor_tensor(passed[:, :, :], over(last), tidx[:, :, :], ALU.is_le))
                step(V.tensor_reduce(te_f[:, :], passed[:, :, :], AX.X, ALU.add))
                step(V.tensor_tensor(passed_n[:, :, :], passed[:, :, :], over(ntile), ALU.mult))
                step(V.tensor_reduce(base_f[:, :], passed_n[:, :, :], AX.X, ALU.add))
                step(V.tensor_tensor(j_f[:, :], tidx[:, :, 0], base_f[:, :], ALU.subtract))
                step(V.tensor_scalar(j_f[:, :], j_f[:, :], float(REGION // P - 1), float(P), ALU.min, ALU.mult))
                step(V.scalar_tensor_tensor(out=ts_f[:, :], in0=te_f[:, :], scalar=float(REGION), in1=j_f[:, :], op0=ALU.mult, op1=ALU.add))
                step(V.tensor_copy(tile_slot[:, :], ts_f[:, :]))
                step(V.tensor_copy(tile_expert[:, :], te_f[:, :]))

            @block.tensor
            def _(pe):
                T = nc.tensor
                def split_products(out_ap, pairs):
                    terms = [(a, c) for a_hi, a_lo, c_hi, c_lo in pairs for a, c in ((a_hi, c_hi), (a_lo, c_hi), (a_hi, c_lo))]
                    for n, (a, c) in enumerate(terms):
                        last = T.matmul(out_ap, a, c, start=(n == 0), stop=(n == len(terms) - 1))
                    return last

                pe.wait_ge(setup_pool.sem, setup_pool.after("ident", 0))
                pe.wait_ge(setup_act.sem, setup_act.after("silu", 0))
                for k in range(KD):
                    last = T.transpose(X[0][:, k * B:(k + 1) * B], sc4[:, k * P:(k + 1) * P], ident[0:B, 0:B])
                last.then_inc(setup_pe.sem, 1)
                pe.wait_ge(setup_dve.sem, setup_dve.after("sc", 0))
                pe.wait_ge(wmod0_loaded, 16)
                for k in range(KD):
                    last = T.matmul(ST[1][:, :], sc_t[:, k, 0:1].to_broadcast([P, P]), wmod[:, k, 0:512], start=(k == 0), stop=(k == KD - 1))
                last.then_inc(setup_pe.sem, 1)
                pe.wait_ge(wmod_loaded, 16)
                for r in range(3):
                    for k in range(KD):
                        last = T.matmul(X[1 + r][0:B, :], sc_t[:, k, :], wmod[:, k, r * 512:(r + 1) * 512], start=(k == 0), stop=(k == KD - 1))
                last.then_inc(setup_pe.sem, 1)
                pe.wait_ge(raw_loaded, 64)
                for k in range(KD):
                    for o in range(KD):
                        T.transpose(O[k][:, o * P:(o + 1) * P], wq_raw[:, o, k * P:(k + 1) * P], ident[:, :])
                        T.transpose(ST[0][:, k * D + o * P:k * D + (o + 1) * P], wo_raw[:, o, k * P:(k + 1) * P], ident[:, :])
                    T.transpose(O[k][:, D:D + P], wk_raw[:, k * P:(k + 1) * P], ident[:, :])
                    last = T.transpose(O[k][:, D + P:D + 2 * P], wv_raw[:, k * P:(k + 1) * P], ident[:, :])
                last.then_inc(setup_pe.sem, 1)

                def turn(stage, src_, k):
                    for t in range(TPB):
                        last = T.transpose(X[k][:, t * P:(t + 1) * P], src_[:, t, k * P:(k + 1) * P], ident[:, :])
                    last.then_inc(stage.sem, 1)

                def projection(bank, at_col):
                    c = slice(at_col, at_col + P)
                    return split_products(X[bank][:, :], [(w_hi[:, k, c], w_lo[:, k, c], t_hi[:, k, :], t_lo[:, k, :])
                                                          for k in range(KD)])

                def prep(p, step):
                    if step in ("t0", "t1"):
                        if step == "t0":
                            wait(pe, row_act, "hn3", p)
                            wait(pe, prep_dve, "maxt3", p - 1)
                            wait(pe, prep_dve, "q3", p - 1)
                            wait(pe, close_act, "t1", p - 3)
                            if p == 0:
                                pe.wait_ge(setup_dve.sem, setup_dve.after("gb_raw", 0))
                        turn(prep_pe, rows, int(step[1]))
                    elif step.startswith("maxt"):
                        hh = int(step[4])
                        wait(pe, prep_dve, f"max{TPB * hh + TPB - 1}", p)
                        wait(pe, prep_act, "v", p)
                        T.transpose(X[1][0:TPB, hh * P:(hh + 1) * P], neg_max[:, TPB * hh:TPB * (hh + 1)], ident[:, :]).then_inc(prep_pe.sem, 1)
                    elif step.startswith("max"):
                        i = int(step[3:])
                        hh, st = i // TPB, i % TPB
                        wait(pe, prep_act, f"q{hh}_again", p)
                        wait(pe, prep_act, f"ka{hh // HPG}", p)
                        if i == 0:
                            wait(pe, prep_dve, f"max{STEPS - 2}", p - 1)
                            wait(pe, close_dve, "x1_1", p - 2)
                        elif i == 1:
                            wait(pe, prep_dve, f"max{STEPS - 1}", p - 1)
                            wait(pe, close_dve, "slot", p - 3)
                        else:
                            wait(pe, prep_dve, f"max{i - 2}", p)
                        T.matmul(X[2 + i % 2][:, :], qa[p % 2][0:DH, hh, st * P:(st + 1) * P], ka[p % 2][0:DH, hh // HPG, :],
                                 start=True, stop=True).then_inc(prep_pe.sem, 1)
                    elif step[0] == "q":
                        g = int(step[1])
                        wait(pe, prep_act, ("t1", "q1_again")[g], p)
                        wait(pe, prep_dve, ("t1", "q1")[g], p)
                        if p == 0 and g == 0:
                            pe.wait_ge(setup_dve.sem, setup_dve.after(f"w{KD - 1}", 0))
                        projection(0, g * P).then_inc(prep_pe.sem, 1)
                    elif step == "k":
                        projection(1, D).then_inc(prep_pe.sem, 1)
                    else:
                        wait(pe, prep_act, "k_hi", p)
                        wait(pe, prep_dve, "k1", p)
                        for t in range(TPB):
                            c = slice(t * P, (t + 1) * P)
                            last = split_products(X[1][:, c], [(t_hi[:, k, c], t_lo[:, k, c], w_hi[:, k, D + P:], w_lo[:, k, D + P:])
                                                               for k in range(KD)])
                        last.then_inc(prep_pe.sem, 1)

                def turn_head(n, hh):
                    pe.wait_ge(o_copied, HEADS * n + hh + 1)
                    for t in range(TPB):
                        last = T.transpose(O[hh % 2][:, t * (DH + 1):(t + 1) * (DH + 1)], o_cols[:, t * P:(t + 1) * P],
                                           ident[0:DH + 1, 0:DH + 1])
                    last.then_inc(o_by_row, 1)

                def turn_o(n, j):
                    pe.wait_ge(normed, HEADS * n + 2 * j + 2)
                    for t in range(TPB):
                        last = T.transpose(O[1][:, t * P:(t + 1) * P], o_row[:, t, :], ident[:, :])
                    last.then_inc(o_turned, 1)

                def close_wo(c, j, k):
                    if k == 0:
                        if j == 0:
                            wait(pe, close_pool, "wo_g", c)
                            pe.wait_ge(o_live, 2 * c + 1)
                            wait(pe, prep_dve, f"max{STEPS - 1}", min(c + 1, B - 1))
                        else:
                            wait(pe, close_dve, "slot", c - 1)
                    elif j == 0:
                        pe.wait_ge(o_live, 2 * c + 2)
                    for i in range(2):
                        t = 2 * j + i
                        last = T.matmul(X[2 + j][:, i * D:(i + 1) * D], o_t[:, k, t * P:(t + 1) * P], wo_g[:, k, :],
                                        start=(k == 0 and i == 0), stop=(k == KD - 1), skip_group_check=True)
                    if k == KD - 1:
                        last.then_inc(close_pe.sem, 1)

                def close_t(c):
                    wait(pe, close_mod, "h2", c)
                    p = min(c + 2, B - 1)
                    wait(pe, prep_dve, "maxt3", p)
                    wait(pe, close_act, "t1", c - 1)
                    for k in range(KD):
                        turn(close_pe, crow, k)

                def close_logits(c):
                    wait(pe, close_act, "t1", c)
                    wait(pe, prep_dve, f"max{STEPS - 1}", min(c + 2, B - 1))
                    wait(pe, close_dve, "x1_1", c)
                    for t in range(TPB):
                        for k in range(KD):
                            last = T.matmul(X[3][:, t * E:(t + 1) * E], t_c[:, k, t * P:(t + 1) * P], wr[:, k, :],
                                            start=(k == 0), stop=(k == KD - 1))
                    last.then_inc(close_pe.sem, 1)

                def close_prefix(c):
                    wait(pe, close_dve, f"add{TPB - 1}", c)
                    o = X[3][:, 64:64 + TPB * E]
                    T.matmul(o, upper[:, :], onehot[:, :, :].rearrange("p t e -> p (t e)"), start=True, stop=False)
                    T.matmul(o, ones[:, :], before[:, 0:TPB, :].rearrange("p t e -> p (t e)"), start=False, stop=True).then_inc(close_pe.sem, 1)

                def score(b, s):
                    hh, t = s // TPB, s % TPB
                    if t == 0:
                        wait(pe, prep_act, f"q{hh}_again", b)
                        wait(pe, prep_act, "k_hi", b)
                        wait(pe, prep_dve, f"maxt{hh}", b)
                    w(pe, exped, STEPS * b + s - 1)
                    c = slice(t * P, (t + 1) * P)
                    T.matmul(ST[s % 2][:, :], ka[b % 2][:, hh // HPG, c], qa[b % 2][:, hh, :], start=True, stop=False)
                    T.matmul(ST[s % 2][:, :], kb[b % 2][0:MK, hh // HPG, c], qb[b % 2][0:MK, hh, :], start=False, stop=True).then_inc(scored, 1)

                def weigh(b, s):
                    hh, t = s // TPB, s % TPB
                    if t == 0:
                        w(pe, normed, HEADS * b + hh - 1)
                        if hh % 2:
                            w(pe, o_live, 2 * b + hh // 2)
                    if s == 0:
                        wait(pe, prep_act, "v", b)
                    pe.wait_ge(exped, STEPS * b + s + 1)
                    T.matmul(O[hh % 2][0:DH + 1, :], va[b % 2][:, t, hh // HPG, :], prob[:, s % 2, :],
                             start=(t == 0), stop=(t == TPB - 1)).then_inc(pved, 1)

                for step in in_order[:before_attention]:
                    prep(0, step)

                for b in range(B):
                    close = b > 0
                    if b == 0:
                        score(0, 0)
                        score(0, 1)
                    for s in range(STEPS):
                        if s == 1 and close:
                            turn_head(b - 1, HEADS - 1)
                        if s % TPB == 1 and s > 1:
                            turn_head(b, s // TPB - 1)
                        weigh(b, s)
                        if s + 2 < STEPS:
                            score(b, s + 2)
                        elif b + 1 < B:
                            score(b + 1, s + 2 - STEPS)
                        for c, at_ in ROUTE[b]:
                            if s == at_ + 2:
                                close_prefix(c)
                        for p, step in PREP[b][s]:
                            prep(p, step)
                        if s == 2 and close:
                            turn_o(b - 1, 1)
                        if s == 3 and close:
                            for k in range(KD):
                                close_wo(b - 1, 0, k)
                        if s == 4 and close:
                            for k in range(KD):
                                close_wo(b - 1, 1, k)
                        if s == 10:
                            turn_o(b, 0)
                        if close and s == CLOSE_T[b]:
                            close_t(b - 1)
                        for c, at_ in ROUTE[b]:
                            if s == at_:
                                close_logits(c)
                c = B - 1
                close_wo(c, 0, 0)
                turn_head(c, HEADS - 1)
                close_wo(c, 1, 0)
                turn_o(c, 1)
                close_wo(c, 0, 1)
                close_wo(c, 1, 1)
                close_t(c)
                close_logits(c)
                close_prefix(c)
                wait(pe, close_dve, "slot", c)
                T.matmul(X[0][:, 0:E], ones[:, :], before[:, TPB, :], start=True, stop=True).then_inc(table_ready, 1)

        with ExitStack() as ffn:
            sf = lambda name, shape, dt: sb(name, shape, dt, ffn)
            ps = [ffn.enter_context(nc.psum_tensor(f"fbank{i}", [P, 512], f32)) for i in range(5)]
            HT, G, U, AT, Y = ps
            RING = 6
            idx = [sf(f"idx{j}", [P, 1], i32) for j in range(RING)]
            hg = [sf(f"hg{j}", [P, D], f32) for j in range(2)]
            ht_hi = [sf(f"ht_hi{j}", [P, KD, P], f32r) for j in range(2)]
            ht_lo = [sf(f"ht_lo{j}", [P, KD, P], f32r) for j in range(2)]
            wg_hi, wg_lo, wu_hi, wu_lo = ([sf(f"{name}{j}", [P, KD, I], f32r) for j in range(2)]
                                          for name in ("wg_hi", "wg_lo", "wu_hi", "wu_lo"))
            sg = sf("sg", [P, I], f32)
            a = sf("a", [P, I], f32)
            at_ = sf("a_t", [P, KI, P], f32)
            yb = [sf(f"yb{j}", [P, D], f32) for j in range(2)]
            res = [sf(f"res{j}", [P, 2 * D], f32) for j in range(2)]

            idx_loaded = [sem(f"idx_loaded{j}") for j in range(RING)]
            gathered = [sem(f"gathered{j}") for j in range(2)]
            scattered = [sem(f"scattered{j}") for j in range(2)]
            tr_done, up_done, at_done, down_done = sem("tr_done"), sem("up_done"), sem("at_done"), sem("down_done")
            gate_done = sem("gate_done")
            ht_ready, silu_done, a_ready, at_ready, y_ready = (sem("ht_ready"), sem("silu_done"), sem("a_ready"),
                                                               sem("at_ready"), sem("y_ready"))
            res_gathered = [sem(f"res_gathered{j}") for j in range(2)]
            gated = sem("gated")
            gate_hi_done, gate_split, up_hi_done, up_split, ht_hi_done = (sem("gate_hi_done"), sem("gate_split"), sem("up_hi_done"),
                                                                          sem("up_split"), sem("ht_hi_done"))

            block = ffn.enter_context(nc.Block())

            assert TILES % 2 == 1

            def steps(eng, body):
                body(1, 1, 0, (1, 0, 2))
                body(2, 0, 0, (1, 1, 3))
                with eng.Fori(1, TILES // 2 - 1) as q:
                    body(2 * q + 1, 1, q, (q + 1, 0, 2 * q + 2))
                    body(2 * q + 2, 0, q, (q + 1, 1, 2 * q + 3))
                q = TILES // 2 - 1
                body(2 * q + 1, 1, q, (q + 1, 0, 2 * q + 2))
                body(2 * q + 2, 0, q, None)

            def expert(engine, i):
                return nc.values_load(tile_expert[0:1, ds(i, 1)], engines=[engine], min_val=0, max_val=E - 1)

            def weights_of(tensor, e):
                return tensor[:, ds(e, 1), :, :].rearrange("p e k i -> p (e k i)")

            def flat(a):
                return a[:, :, :].rearrange("p k i -> p (k i)")

            @block.sync
            def _(sp):
                for i in range(TILES):
                    at0 = nc.values_load(tile_slot[0:1, i:i + 1], engines=[mybir.EngineType.SP], min_val=0,
                                         max_val=(E - 1) * REGION + REGION - P)
                    if i >= RING:
                        sp.wait_ge(scattered[i % 2], 16 * ((i - RING) // 2) + 16)
                    sp.dma_start(idx[i % RING][:, :], slots_d[ds(at0, P), :]).then_inc(idx_loaded[i % RING], 16)
                sp.wait_ge(scattered[0], 16 * ((TILES + 1) // 2))
                sp.wait_ge(scattered[1], 16 * (TILES // 2))

            @block.gpsimd
            def _(pool):
                def gather(i):
                    par = i % 2
                    pool.wait_ge(idx_loaded[i % RING], 16 * (i // RING) + 16)
                    if i >= 2:
                        pool.wait_ge(tr_done, i - 1)
                    nc.gpsimd.indirect_dma_start(out=hg[par][:, :], out_offset=None, in_=h2_d,
                                                 in_offset=bass.IndirectOffsetOnAxis(ap=idx[i % RING][:, :], axis=0)).then_inc(gathered[par], 16)

                def gather_residual(i):
                    par = i % 2
                    pool.wait_ge(idx_loaded[i % RING], 16 * (i // RING) + 16)
                    if i >= 2:
                        pool.wait_ge(y_ready, i - 1)
                    nc.gpsimd.indirect_dma_start(out=res[par][:, :], out_offset=None, in_=res_d,
                                                 in_offset=bass.IndirectOffsetOnAxis(ap=idx[i % RING][:, :], axis=0)).then_inc(res_gathered[par], 16)

                def scatter(i):
                    par = i % 2
                    pool.wait_ge(y_ready, i + 1)
                    nc.gpsimd.indirect_dma_start(out=out.rearrange("b s d -> (b s) d"),
                                                 out_offset=bass.IndirectOffsetOnAxis(ap=idx[i % RING][:, :], axis=0),
                                                 in_=yb[par][:, :], in_offset=None,
                                                 bounds_check=N - 1, oob_is_err=False).then_inc(scattered[par], 16)

                gather(0)
                gather(1)
                for i in range(TILES + 2):
                    if i + 2 < TILES:
                        gather(i + 2)
                    if i >= 2:
                        scatter(i - 2)
                    if i < TILES:
                        gather_residual(i)

            @block.tensor
            def _(pe):
                T = nc.tensor

                def transpose_rows(q, par, i):
                    pe.wait_ge(gathered[par], 16 * q + 16)
                    w(pe, ht_ready, i)
                    for k in range(KD):
                        last = T.transpose(HT[:, k * P:(k + 1) * P], hg[par][:, k * P:(k + 1) * P], ident[:, :])
                    last.then_inc(tr_done, 1)

                def split_product(bank, par, hi, lo):
                    terms = [(x_[par][:, k, :], w_[par][:, k, :]) for k in range(KD)
                             for x_, w_ in ((ht_hi, hi), (ht_lo, hi), (ht_hi, lo))]
                    for n, (x_, w_) in enumerate(terms):
                        last = T.matmul(bank[:, :], x_, w_, start=(n == 0), stop=(n == len(terms) - 1))
                    return last

                def gate(par, i):
                    pe.wait_ge(ht_ready, i + 1)
                    pe.wait_ge(gate_split, i + 1)
                    w(pe, silu_done, i)
                    split_product(G, par, wg_hi, wg_lo).then_inc(gate_done, 1)

                def up(par, i):
                    pe.wait_ge(up_split, i + 1)
                    w(pe, a_ready, i)
                    split_product(U, par, wu_hi, wu_lo).then_inc(up_done, 1)

                def transpose_a(i):
                    pe.wait_ge(a_ready, i + 1)
                    w(pe, at_ready, i)
                    for k in range(KI):
                        last = T.transpose(AT[:, k * P:(k + 1) * P], a[:, k * P:(k + 1) * P], ident[:, :])
                    last.then_inc(at_done, 1)

                def down(i, e):
                    pe.wait_ge(at_ready, i + 1)
                    w(pe, gated, i)
                    for k in range(KI):
                        last = T.matmul(Y[:, 0:D], at_[:, k, :], w_down[:, ds(e, 1), k, :].rearrange("p e d -> p (e d)"),
                                        start=(k == 0), stop=(k == KI - 1))
                    last.then_inc(down_done, 1)

                pe.wait_ge(w_loaded[2], 16 * E)
                transpose_rows(0, 0, 0)
                gate(0, 0)
                transpose_rows(0, 1, 1)
                up(0, 0)

                def step(i, par, q, next_):
                    gate(par, i)
                    transpose_a(i - 1)
                    if next_ is not None:
                        transpose_rows(*next_)
                    up(par, i)
                    down(i - 1, expert(mybir.EngineType.PE, i - 1))

                steps(pe, step)
                transpose_a(TILES - 1)
                down(TILES - 1, expert(mybir.EngineType.PE, TILES - 1))

            @block.scalar
            def _(act):
                A = nc.scalar.activation

                def silu(i):
                    act.wait_ge(gate_done, i + 1)
                    w(act, a_ready, i)
                    A(sg[:, :], G[:, :], ACT.Silu).then_inc(silu_done, 1)

                def evacuate_a(i):
                    act.wait_ge(at_done, i + 1)
                    w(act, down_done, i)
                    A(at_[:, :, :].rearrange("p k c -> p (k c)"), AT[:, :], ACT.Copy).then_inc(at_ready, 1)

                def gate_hi(e, par, i):
                    w(act, up_done, i - 1)
                    A(flat(wg_hi[par]), weights_of(w_gate, e), ACT.Copy).then_inc(gate_hi_done, 1)

                def up_hi(e, par):
                    A(flat(wu_hi[par]), weights_of(w_up, e), ACT.Copy).then_inc(up_hi_done, 1)

                def rows_hi(par, i):
                    act.wait_ge(tr_done, i + 1)
                    w(act, up_done, i - 1)
                    A(flat(ht_hi[par]), HT[:, 0:KD * P], ACT.Copy).then_inc(ht_hi_done, 1)

                def step(i, par, q, next_):
                    if next_ is not None:
                        e = expert(mybir.EngineType.Activation, next_[2])
                        gate_hi(e, next_[1], next_[2])
                    silu(i)
                    evacuate_a(i - 1)
                    if next_ is not None:
                        up_hi(e, next_[1])
                        rows_hi(next_[1], next_[2])

                A(sg[0:1, 0:1], ident[0:1, 0:1], ACT.Silu)
                for j in range(2):
                    act.wait_ge(w_loaded[j], 16 * E)
                e0, e1 = (expert(mybir.EngineType.Activation, i) for i in range(2))
                gate_hi(e0, 0, 0)
                up_hi(e0, 0)
                gate_hi(e1, 1, 1)
                rows_hi(0, 0)
                up_hi(e1, 1)
                rows_hi(1, 1)
                silu(0)
                steps(act, step)
                evacuate_a(TILES - 1)

            @block.vector
            def _(dve):
                V = nc.vector

                def gate_lo(e, par, i):
                    dve.wait_ge(gate_hi_done, i + 1)
                    V.tensor_tensor(flat(wg_lo[par]), weights_of(w_gate, e), flat(wg_hi[par]).bitcast(f32), ALU.subtract).then_inc(gate_split, 1)

                def up_lo(e, par, i):
                    dve.wait_ge(up_hi_done, i + 1)
                    V.tensor_tensor(flat(wu_lo[par]), weights_of(w_up, e), flat(wu_hi[par]).bitcast(f32), ALU.subtract).then_inc(up_split, 1)

                def rows_lo(par, i):
                    dve.wait_ge(ht_hi_done, i + 1)
                    V.tensor_tensor(flat(ht_lo[par]), HT[:, 0:KD * P], flat(ht_hi[par]).bitcast(f32), ALU.subtract).then_inc(ht_ready, 1)

                def product(i):
                    dve.wait_ge(up_done, i + 1)
                    dve.wait_ge(silu_done, i + 1)
                    w(dve, at_done, i)
                    V.tensor_tensor(a[:, :], sg[:, :], U[:, :], ALU.mult).then_inc(a_ready, 1)

                def output(q, par, i):
                    dve.wait_ge(down_done, i + 1)
                    w(dve, scattered[par], 16 * q)
                    dve.wait_ge(res_gathered[par], 16 * q + 16)
                    V.tensor_tensor(yb[par][:, :], Y[:, 0:D], res[par][:, D:2 * D], ALU.mult).then_inc(gated, 1)
                    dve.wait_ge(gated, i + 1)
                    V.tensor_tensor(yb[par][:, :], yb[par][:, :], res[par][:, 0:D], ALU.add).then_inc(y_ready, 1)

                e0, e1 = (expert(mybir.EngineType.DVE, i) for i in range(2))
                gate_lo(e0, 0, 0)
                up_lo(e0, 0, 0)
                gate_lo(e1, 1, 1)
                rows_lo(0, 0)
                up_lo(e1, 1, 1)
                rows_lo(1, 1)
                product(0)

                def step(i, par, q, next_):
                    if next_ is not None:
                        e = expert(mybir.EngineType.DVE, next_[2])
                        gate_lo(e, next_[1], next_[2])
                    product(i)
                    if next_ is not None:
                        rows_lo(next_[1], next_[2])
                        up_lo(e, next_[1], next_[2])
                    output(q, 1 - par, i - 1)

                steps(dve, step)
                output(TILES // 2, 0, TILES - 1)


_INS = ["L0_attn_x", "L0_attn_norm_scale", "L0_attn_split_scale", "L0_attn_Wq", "L0_attn_Wk", "L0_attn_Wv",
        "L0_attn_Wo", "L0_ffn_router_w", "L0_ffn_gate_w", "L0_ffn_up_w", "L0_ffn_down_w", "L0_c", "L0_wmod"]


def kernel(**inputs):
    import numpy as np
    import concourse.bacc as bacc
    from concourse import mybir
    from concourse.bass_utils import run_bass_kernel_spmd

    nc = bacc.Bacc("TRN2", target_bir_lowering=False, num_devices=1)
    arrays, io = {}, {}
    for name in _INS:
        arr = np.ascontiguousarray(inputs[name])
        arrays[name + "_dram"] = arr
        io[name] = nc.dram_tensor(name + "_dram", arr.shape, mybir.dt.from_np(arr.dtype), kind="ExternalInput").ap()
    shape = inputs["L0_attn_x"].shape
    io["out"] = nc.dram_tensor("out_dram", shape, mybir.dt.float32, kind="ExternalOutput").ap()
    build(nc, io)
    r = run_bass_kernel_spmd(nc, [arrays], core_ids=[0])
    return r.results[0]["out_dram"]
```
